# Optimizing a Trainium2 kernel written in Bass

```python
import numpy as np
import jax
import jax.numpy as jnp

def _softmax(x, axis=-1):
    return jax.nn.softmax(x, axis=axis)

def _gelu(x):
    return jax.nn.gelu(x, approximate=True)

def _silu(x):
    return jax.nn.silu(x)

def _sigmoid(x):
    return jax.nn.sigmoid(x)

def _layernorm(x, axis=-1, eps=1e-05):
    m = jnp.mean(x, axis=axis, keepdims=True)
    v = jnp.var(x, axis=axis, keepdims=True)
    return (x - m) / jnp.sqrt(v + eps)

def _scatter_add(tgt, idx, src, axis=0):
    return tgt.at[idx].add(src)

def _segment_sum(src, seg, n):
    return jax.ops.segment_sum(src, seg, n)
kernel_name = 'mk_gnn_resnorm_d4_gnn_r32_98088c'

def setup_inputs(seed: int=0):
    np.random.seed(seed)
    _w = jnp.asarray

    def _rec_inputs():
        import jax
        import jax.numpy as jnp
        _gk = jax.random.key(seed)
        x = -0.0005121 + 1.001 * jax.random.normal(jax.random.fold_in(_gk, 1), (3125, 32), jnp.float32)
        src = jax.random.randint(jax.random.fold_in(_gk, 2), (100000,), 0, 3125, jnp.int32)
        dst = jax.random.randint(jax.random.fold_in(_gk, 3), (100000,), 0, 3125, jnp.int32)
        _o = jnp.argsort(dst, stable=True)
        src = src[_o]
        dst = dst[_o]
        edge_attr_4 = 0.000398945 + 1.00003 * jax.random.normal(jax.random.fold_in(_gk, 12), (100000, 4), jnp.float32)
        edge_weight = jax.random.uniform(jax.random.fold_in(_gk, 14), (100000,), jnp.float32, 0.0, 1)
        return (x, src, dst, edge_attr_4, edge_weight)
    x, src, dst, edge_attr_4, edge_weight = _rec_inputs()

    def _L0_gnn_setup():
        import jax, jax.numpy as jnp
        import numpy as np
        N_NODES = 3125
        N_EDGES = 50000
        D_FEAT = 32
        key = jax.random.key(seed)
        k1, k2, k3 = jax.random.split(key, 3)
        features = jax.random.normal(k1, (N_NODES, D_FEAT), dtype=jnp.float32)
        src = jax.random.randint(k2, (N_EDGES,), 0, N_NODES, dtype=jnp.int64)
        dst = jax.random.randint(k3, (N_EDGES,), 0, N_NODES, dtype=jnp.int64)
        return {'features': features, 'src': src, 'dst': dst}
    _L0_gnn_all = _L0_gnn_setup()
    _L0_gnn_in = {k: v for k, v in _L0_gnn_all.items() if k in ()}
    del _L0_gnn_all

    def _L1_gnn_setup():
        import jax, jax.numpy as jnp
        import numpy as np
        N_NODES = 3125
        N_EDGES = 50000
        C = 32
        key = jax.random.key(seed)
        k1, k2, k3, k4 = jax.random.split(key, 4)
        signal = jax.random.normal(k1, (N_NODES, C), dtype=jnp.float32)
        weights = jax.random.uniform(k2, (N_EDGES,), dtype=jnp.float32)
        edge_src = jax.random.randint(k3, (N_EDGES,), 0, N_NODES)
        edge_dst = jax.random.randint(k4, (N_EDGES,), 0, N_NODES)
        return {'signal': signal, 'weights': weights, 'edge_src': edge_src, 'edge_dst': edge_dst, 'itr': 10}
    _L1_gnn_all = _L1_gnn_setup()
    _L1_gnn_in = {k: v for k, v in _L1_gnn_all.items() if k in ()}
    del _L1_gnn_all

    def _L2_gnn_setup():
        import jax, jax.numpy as jnp
        import numpy as np
        N = 3125
        E = 50000
        D = 32
        L = 3

        def _gcn_norm(edge_index, edge_weight, n):
            loop = jnp.arange(n)
            src = jnp.concatenate([edge_index[0], loop])
            dst = jnp.concatenate([edge_index[1], loop])
            w = jnp.concatenate([edge_weight, jnp.ones((n,), edge_weight.dtype)])
            deg = jax.ops.segment_sum(w, dst, num_segments=n)
            dinv = jnp.where(deg > 0, jax.lax.rsqrt(deg), jnp.zeros_like(deg))
            return (src, dst, dinv[src] * w * dinv[dst])
        key = jax.random.key(seed)
        ks = jax.random.split(key, 6)
        X = jax.random.normal(ks[0], (N, D), jnp.float32)
        edge_index = jax.random.randint(ks[1], (2, E), 0, N)
        edge_weight = jax.random.uniform(ks[2], (E,), jnp.float32)
        conv_w = jax.random.normal(ks[3], (L, 8, D, D), jnp.float32) * np.float32(1.0 / np.sqrt(D))
        conv_b = jnp.zeros((L, 8, D), jnp.float32)
        wc = jax.random.normal(ks[4], (L, 3, D), jnp.float32) * np.float32(0.1)
        bg = jnp.zeros((L, 4, D), jnp.float32)
        return dict(X=X, edge_index=edge_index, edge_weight=edge_weight, conv_w=conv_w, conv_b=conv_b, wc=wc, bg=bg)
    _L2_gnn_all = _L2_gnn_setup()
    _L2_gnn_in = {k: v for k, v in _L2_gnn_all.items() if k in ('conv_w', 'conv_b', 'wc', 'bg')}
    del _L2_gnn_all

    def _L3_gnn_setup():
        import jax, jax.numpy as jnp
        import numpy as np
        N_NODES = 3125
        N_EDGES = 50000
        IN_DIM = 32
        HID = 64
        OUT_DIM = 32
        EDGE_DIM = 4
        key = jax.random.key(seed)
        ks = jax.random.split(key, 12)
        x = jax.random.normal(ks[0], (N_NODES, IN_DIM), dtype=jnp.float32)
        edge_index = jax.random.randint(ks[1], (2, N_EDGES), 0, N_NODES, dtype=jnp.int32)
        edge_attr = jax.random.normal(ks[2], (N_EDGES, EDGE_DIM), dtype=jnp.float32)

        def lin(k, fan_in, fan_out):
            kw, kb = jax.random.split(k)
            bound = 1.0 / np.sqrt(fan_in)
            W = jax.random.uniform(kw, (fan_in, fan_out), minval=-bound, maxval=bound, dtype=jnp.float32)
            b = jax.random.uniform(kb, (fan_out,), minval=-bound, maxval=bound, dtype=jnp.float32)
            return (W, b)
        W1, b1 = lin(ks[3], 2 * IN_DIM, HID)
        W2, b2 = lin(ks[4], HID, 2 * HID)
        W3, b3 = lin(ks[5], 2 * HID, HID)
        W4, b4 = lin(ks[6], HID, OUT_DIM)
        return {'x': x, 'edge_index': edge_index, 'edge_attr': edge_attr, 'W1': W1, 'b1': b1, 'W2': W2, 'b2': b2, 'W3': W3, 'b3': b3, 'W4': W4, 'b4': b4}
    _L3_gnn_all = _L3_gnn_setup()
    _L3_gnn_in = {k: v for k, v in _L3_gnn_all.items() if k in ('W1', 'b1', 'W2', 'b2', 'W3', 'b3', 'W4', 'b4')}
    del _L3_gnn_all
    return {'x': x, 'src': src, 'dst': dst, 'edge_attr_4': edge_attr_4, 'edge_weight': edge_weight, 'L2_gnn_conv_w': _L2_gnn_in['conv_w'], 'L2_gnn_conv_b': _L2_gnn_in['conv_b'], 'L2_gnn_wc': _L2_gnn_in['wc'], 'L2_gnn_bg': _L2_gnn_in['bg'], 'L3_gnn_W1': _L3_gnn_in['W1'], 'L3_gnn_b1': _L3_gnn_in['b1'], 'L3_gnn_W2': _L3_gnn_in['W2'], 'L3_gnn_b2': _L3_gnn_in['b2'], 'L3_gnn_W3': _L3_gnn_in['W3'], 'L3_gnn_b3': _L3_gnn_in['b3'], 'L3_gnn_W4': _L3_gnn_in['W4'], 'L3_gnn_b4': _L3_gnn_in['b4']}

def reference(x, src, dst, edge_attr_4, edge_weight, L2_gnn_conv_w, L2_gnn_conv_b, L2_gnn_wc, L2_gnn_bg, L3_gnn_W1, L3_gnn_b1, L3_gnn_W2, L3_gnn_b2, L3_gnn_W3, L3_gnn_b3, L3_gnn_W4, L3_gnn_b4):
    import jax
    import jax.numpy as jnp

    def _L0_gnn_ref(features, src, dst):
        import jax, jax.numpy as jnp
        import numpy as np
        N_NODES = 3125
        N_EDGES = 50000
        D_FEAT = 32
        messages = features[src]
        h = jax.ops.segment_sum(messages, dst, num_segments=N_NODES)
        return h

    def _L1_gnn_ref(signal, weights, edge_src, edge_dst, itr):
        import jax, jax.numpy as jnp
        import numpy as np
        N_NODES = 3125
        N_EDGES = 50000
        C = 32
        n = signal.shape[0]
        sqrt_w = jnp.sqrt(weights)[:, None]

        def step(f, _):
            up = jnp.maximum(f[edge_dst] - f[edge_src], 0.0) * sqrt_w
            inf_norm = jax.ops.segment_max(up, edge_src, num_segments=n)
            inf_norm = jnp.maximum(inf_norm, 0.0)
            return (f + inf_norm, None)
        out, _ = jax.lax.scan(step, signal, None, length=itr)
        return out

    def _L2_gnn_ref(X, edge_index, edge_weight, conv_w, conv_b, wc, bg):
        import jax, jax.numpy as jnp
        import numpy as np
        N = 3125
        E = 50000
        D = 32
        L = 3

        def _gcn_norm(edge_index, edge_weight, n):
            loop = jnp.arange(n)
            src = jnp.concatenate([edge_index[0], loop])
            dst = jnp.concatenate([edge_index[1], loop])
            w = jnp.concatenate([edge_weight, jnp.ones((n,), edge_weight.dtype)])
            deg = jax.ops.segment_sum(w, dst, num_segments=n)
            dinv = jnp.where(deg > 0, jax.lax.rsqrt(deg), jnp.zeros_like(deg))
            return (src, dst, dinv[src] * w * dinv[dst])
        n = X.shape[0]
        src, dst, nw = _gcn_norm(edge_index, edge_weight, n)

        def gcn(x, W, b):
            xw = x @ W
            agg = jax.ops.segment_sum(nw[:, None] * xw[src], dst, num_segments=n)
            return agg + b
        out = X
        for l in range(conv_w.shape[0]):
            x = out
            H = jnp.zeros((n, conv_w.shape[-1]), x.dtype)
            C = jnp.zeros_like(H)
            Wl, bl = (conv_w[l], conv_b[l])
            I = jax.nn.sigmoid(gcn(x, Wl[0], bl[0]) + gcn(H, Wl[1], bl[1]) + wc[l, 0] * C + bg[l, 0])
            F = jax.nn.sigmoid(gcn(x, Wl[2], bl[2]) + gcn(H, Wl[3], bl[3]) + wc[l, 1] * C + bg[l, 1])
            T = jnp.tanh(gcn(x, Wl[4], bl[4]) + gcn(H, Wl[5], bl[5]) + bg[l, 2])
            C = F * C + I * T
            O = jax.nn.sigmoid(gcn(x, Wl[6], bl[6]) + gcn(H, Wl[7], bl[7]) + wc[l, 2] * C + bg[l, 3])
            out = O * jnp.tanh(C)
        return out

    def _L3_gnn_ref(x, edge_index, edge_attr, W1, b1, W2, b2, W3, b3, W4, b4):
        import jax, jax.numpy as jnp
        import numpy as np
        N_NODES = 3125
        N_EDGES = 50000
        IN_DIM = 32
        HID = 64
        OUT_DIM = 32
        EDGE_DIM = 4
        j_idx = edge_index[0]
        i_idx = edge_index[1]
        x_j = x[j_idx]
        x_i = x[i_idx]
        msg = jnp.concatenate([x_i, x_j - x_i], axis=-1)
        h = jax.nn.relu(msg @ W1 + b1)
        h = jax.nn.relu(h @ W2 + b2)
        h = jax.nn.relu(h @ W3 + b3)
        m = h @ W4 + b4
        s = jax.ops.segment_sum(m, i_idx, num_segments=N_NODES)
        cnt = jax.ops.segment_sum(jnp.ones((m.shape[0],), m.dtype), i_idx, num_segments=N_NODES)
        return s / jnp.maximum(cnt, 1.0)[:, None]
    edge_index = jnp.stack([src, dst])
    x = _layernorm(x + _L0_gnn_ref(x, src, dst), axis=-1)
    x = _layernorm(x + _L1_gnn_ref(x, edge_weight, src, dst, 10), axis=-1)
    x = _layernorm(x + _L2_gnn_ref(x, edge_index, edge_weight, L2_gnn_conv_w, L2_gnn_conv_b, L2_gnn_wc, L2_gnn_bg), axis=-1)
    x = _layernorm(x + _L3_gnn_ref(x, edge_index, edge_attr_4, L3_gnn_W1, L3_gnn_b1, L3_gnn_W2, L3_gnn_b2, L3_gnn_W3, L3_gnn_b3, L3_gnn_W4, L3_gnn_b4), axis=-1)
    return x

_drawn_inputs = setup_inputs


def setup_inputs(seed=0):
    import zlib

    import numpy as np

    out = dict(_drawn_inputs(seed))
    spreads = {'L2_gnn_conv_b': (0.0, 0.1), 'L2_gnn_bg': (0.0, 0.416)}
    factors = {'edge_weight': 8.0,
     'L2_gnn_conv_w': 5.475,
     'L2_gnn_wc': 8.0,
     'L3_gnn_W1': 2.986,
     'L3_gnn_b1': 8.0,
     'L3_gnn_b2': 5.636,
     'L3_gnn_b3': 2.822}
    for name, (base, spread) in spreads.items():
        noise = np.random.default_rng([zlib.crc32(name.encode()), seed]).standard_normal(out[name].shape)
        drawn = base * np.exp(spread * noise) if base else spread * noise
        out[name] = jnp.asarray(drawn.astype(out[name].dtype))
    for name, factor in factors.items():
        out[name] = (out[name] * factor).astype(out[name].dtype)
    return out
```

```python
from contextlib import ExitStack, contextmanager

import concourse.bass as bass
from concourse import mybir

F32, I32, U32, BF16 = mybir.dt.float32, mybir.dt.int32, mybir.dt.uint32, mybir.dt.bfloat16
I16, U8 = mybir.dt.int16, mybir.dt.uint8
ALU, ACT, AX = mybir.AluOpType, mybir.ActivationFunctionType, mybir.AxisListType

N, E, D = 3125, 100000, 32
P = 128
HI = -(-N // P)
NPAD = HI * P
RUN = -(-(N + E) // P)
DMA_TILES, HOT_TILES = 21, 16
CT = DMA_TILES + HOT_TILES
CHUNKS = -(-(RUN + 1) // CT)
COLS = CHUNKS * CT
HOT = HOT_TILES * P
BANK = 512
HOT_BANKS = HOT // BANK
RING, ACT_RING = 8, 3
ACT_BLOCKS = (8, 16, 24)
DVE_BLOCKS = tuple(b for b in range(HI) if b not in ACT_BLOCKS)
SPLIT = 3 * D
EP, EF = 125, 800
SORT = 1024
LOG_F, LOG_N = 10, 17
ID_BITS = 17
ID_MASK = (1 << ID_BITS) - 1
KEY_BIAS = 64
EPS = 1e-5
HID = 64
assert ACT_BLOCKS[-1] == HI - 1
assert EP * EF == E and HOT_TILES * D == BANK and HOT == HOT_BANKS * BANK


def program(nc, x, src, dst, edge_weight, conv_w, conv_b, wc, bg, W1, b1, W2, b2, W3, b3, W4, b4, out, debug=None):
    ctx = ExitStack()
    keys_dram = nc.dram_tensor("keys_dram", [2, P, SORT], I32, kind="Internal").ap()
    sorted_dram = nc.dram_tensor("sorted_dram", [2, P * SORT], I32, kind="Internal").ap()
    edges_dram = nc.dram_tensor("edges_dram", [E + 1, 4], I32, kind="Internal").ap()
    table_dram = nc.dram_tensor("table_dram", [NPAD, D], F32, kind="Internal").ap()
    scan_dram = nc.dram_tensor("scan_dram", [P * COLS, D], F32, kind="Internal").ap()
    scan_rows = scan_dram.rearrange("(p t) c -> p t c", p=P)
    degree_dram = nc.dram_tensor("degree_dram", [P * COLS, 1], F32, kind="Internal").ap()
    hot_index_dram = nc.dram_tensor("hot_index_dram", [2, CHUNKS * HOT_TILES, P], I16, kind="Internal").ap()
    table_nodes = table_dram.rearrange("(h p) c -> p h c", p=P)

    @contextmanager
    def phase(*names):
        with ExitStack() as own:
            sems = [own.enter_context(nc.semaphore(n)) for n in names]
            with nc.Block() as block:
                yield (block, *sems)
            nums = sorted(s.num for s in sems)
            first = nums[0]
            for num, after in zip(nums, nums[1:] + [None]):
                if after != num + 1:
                    nc.gpsimd.dma_reset(range(first, num + 1))
                    nc.all_engine_barrier(sems_to_clear=range(first, num + 1))
                    first = after

    def chain(engine, sem):
        count = [0]

        def link(instruction):
            count[0] += 1
            instruction.then_inc(sem, 1)
            engine.wait_ge(sem, count[0])
        return link

    with ctx:
        def sb(name, shape, dt=F32, stack=ctx):
            return stack.enter_context(nc.sbuf_tensor(name, shape, dt))

        gather_index = [sb(f"gather_index{o}", [P, COLS], U32) for o in range(2)]
        starts = [sb(f"starts{o}", [P, COLS]) for o in range(2)]
        inside = [sb(f"inside{o}", [P, CHUNKS, D, CT + 1], U8) for o in range(2)]
        end_row = [sb(f"end_row{o}", [P, HI], U32) for o in range(2)]
        fix_row = [sb(f"fix_row{o}", [P, 1], U32) for o in range(2)]
        whole = [sb(f"whole{o}", [D, P]) for o in range(2)]
        root_weight = sb("root_weight", [P, COLS])
        weight = sb("weight", [P, COLS])
        real = sb("real", [P, COLS])
        degree = sb("degree", [P, HI])
        inv_root = sb("inv_root", [P, HI])
        state = sb("state", [P, HI, D])
        rows = sb("rows", [P, HI, D])
        ends = sb("ends", [P, HI, D])
        spare = sb("spare", [P, HI, D])
        parts = sb("parts", [P, HI, 3, D], BF16)
        stat = sb("stat", [P, 4, HI])
        node_f = sb("node_f", [P, HI])
        minus_node = sb("minus_node", [P, HI])
        identity = sb("identity", [P, P])
        sum_parts = sb("sum_parts", [SPLIT, D], BF16)

        def split_rows(link, of):
            V = nc.vector
            link(V.tensor_copy(parts[:, :, 0, :], of))
            link(V.tensor_tensor(spare[:, :, :], of, parts[:, :, 0, :], ALU.subtract))
            link(V.tensor_copy(parts[:, :, 1, :], spare[:, :, :]))
            link(V.tensor_tensor(spare[:, :, :], spare[:, :, :], parts[:, :, 1, :], ALU.subtract))
            link(V.tensor_copy(parts[:, :, 2, :], spare[:, :, :]))

        with ExitStack() as own:
            src_in = sb("src_in", [P, EF], I32, own)
            dst_in = sb("dst_in", [P, EF], I32, own)
            w_in = sb("w_in", [P, EF], F32, own)
            edge_id = sb("edge_id", [P, EF], I32, own)
            node_id = sb("node_id", [P, HI], I32, own)
            keys = [sb(f"keys{o}", [P, SORT], I32, own) for o in range(2)]
            record = sb("record", [P, EF, 4], I32, own)
            blank = sb("blank", [1, 4], I32, own)
            with phase("loaded", "iota_done", "padded", "vec", "keyed", "x_cleared", "stored") as (
                    block, loaded, iota_done, padded, vec, keyed, x_cleared, stored):
                @block.sync
                def _(sp):
                    sp.dma_start(src_in[0:EP, :], src.rearrange("(p f) -> p f", p=EP)).then_inc(loaded, 16)
                    sp.dma_start(dst_in[0:EP, :], dst.rearrange("(p f) -> p f", p=EP)).then_inc(loaded, 16)
                    sp.dma_start(w_in[0:EP, :], edge_weight.rearrange("(p f) -> p f", p=EP)).then_inc(loaded, 16)
                    full = (N // P) * P
                    sp.wait_ge(x_cleared, 1)
                    sp.dma_start(state[:, 0:N // P, :], x[0:full, :].rearrange("(h p) c -> p h c", p=P)).then_inc(stored, 16)
                    sp.dma_start(state[0:N - full, HI - 1, :], x[full:N, :]).then_inc(stored, 16)
                    sp.wait_ge(stored, 32)
                    sp.dma_start(table_nodes, state[:, :, :]).then_inc(stored, 16)
                    sp.wait_ge(keyed, 1)
                    for o in range(2):
                        sp.dma_start(keys_dram[o, :, :], keys[o][:, :]).then_inc(stored, 16)
                    sp.dma_start(edges_dram[1:E + 1, :].rearrange("(p f) c -> p f c", p=EP), record[0:EP, :, :]).then_inc(stored, 16)
                    sp.dma_start(edges_dram[0:1, :], blank[:, :]).then_inc(stored, 16)
                    sp.wait_ge(stored, 16 * 7)

                @block.gpsimd
                def _(pool):
                    pool.iota(edge_id[:, :], [[1, EF]], base=1, channel_multiplier=EF).then_inc(iota_done, 1)
                    pool.iota(node_id[:, :], [[P, HI]], base=0, channel_multiplier=1).then_inc(iota_done, 1)
                    pool.memset(identity[:, :], 0.0).then_inc(padded, 1)
                    pool.wait_ge(padded, 1)
                    pool.affine_select(out=identity[:, :], in_=identity[:, :], compare_op=ALU.not_equal, fill=1.0,
                                       base=0, pattern=[[-1, P]], channel_multiplier=1).then_inc(padded, 1)
                    pool.wait_ge(padded, 2)

                @block.vector
                def _(dve):
                    link = chain(dve, vec)
                    nc.vector.memset(state[:, HI - 1, :], 0.0).then_inc(x_cleared, 1)
                    for o in range(2):
                        nc.vector.memset(keys[o][:, :], float((NPAD + KEY_BIAS) << ID_BITS))
                    nc.vector.memset(record[:, :, 3], 0)
                    link(nc.vector.memset(blank[:, :], 0))
                    dve.wait_ge(iota_done, 2)
                    dve.wait_ge(loaded, 48)
                    ends_of = (src_in, dst_in)
                    for o in range(2):
                        nc.vector.tensor_scalar(keys[o][:, EF:EF + HI], node_id[:, :], KEY_BIAS, None, ALU.add)
                        link(nc.vector.tensor_scalar(keys[o][0:EP, 0:EF], ends_of[o][0:EP, :], KEY_BIAS, None, ALU.add))
                    for o in range(2):
                        link(nc.vector.tensor_scalar(keys[o][:, EF:EF + HI], keys[o][:, EF:EF + HI], ID_BITS, None, ALU.logical_shift_left))
                        link(nc.vector.tensor_scalar(keys[o][0:EP, 0:EF], keys[o][0:EP, 0:EF], ID_BITS, None, ALU.logical_shift_left))
                    for o in range(2):
                        nc.vector.tensor_tensor(keys[o][0:EP, 0:EF], keys[o][0:EP, 0:EF], edge_id[0:EP, :], ALU.bitwise_or)
                    nc.vector.tensor_copy(record[0:EP, :, 0], src_in[0:EP, :])
                    nc.vector.tensor_copy(record[0:EP, :, 1], dst_in[0:EP, :])
                    link(nc.vector.tensor_copy(record[0:EP, :, 2].bitcast(F32), w_in[0:EP, :]))
                    nc.vector.drain().then_inc(keyed, 1)
                    dve.wait_ge(stored, 32)
                    split_rows(link, state[:, :, :])
                    dve.wait_ge(padded, 2)
                    for i in range(3):
                        link(nc.vector.tensor_copy(sum_parts[i * D:(i + 1) * D, :], identity[i * D:(i + 1) * D, i * D:(i + 1) * D]))

        with ExitStack() as own:
            ping = [sb(f"ping{i}", [P, SORT], F32, own) for i in range(2)]
            sign = sb("sign", [P, LOG_N - LOG_F], F32, own)
            bit = sb("bit", [P, LOG_N - LOG_F], I32, own)
            turned = own.enter_context(nc.psum_tensor("turned", [P, SORT], F32))
            with phase("iota_done", "vec") as (block, iota_done, vec):
                @block.gpsimd
                def _(pool):
                    pool.iota(bit[:, :], [[0, LOG_N - LOG_F]], base=0, channel_multiplier=1).then_inc(iota_done, 1)

                @block.vector
                def _(dve):
                    link = chain(dve, vec)
                    dve.wait_ge(iota_done, 1)
                    for m in range(LOG_N - LOG_F):
                        link(nc.vector.tensor_scalar(bit[:, m:m + 1], bit[:, m:m + 1], m, 1, ALU.logical_shift_right, ALU.bitwise_and))
                    link(nc.vector.tensor_scalar(sign[:, :], bit[:, :], -2.0, 1.0, ALU.mult, ALU.add))

            with nc.Fori(0, 2) as order:
                with phase("keys_in", "vec", "turn_ready", "turned_done", "copied", "keys_out") as (
                        block, keys_in, vec, turn_ready, turned_done, copied, keys_out):
                    turns = 2 * (LOG_N - LOG_F)

                    @block.sync
                    def _(sp):
                        sp.dma_start(ping[0][:, :].bitcast(I32), keys_dram[bass.ds(order, 1), :, :].rearrange("o p f -> (o p) f")).then_inc(keys_in, 16)
                        sp.wait_ge(turn_ready, turns + 1)
                        sp.dma_start(sorted_dram[bass.ds(order, 1), :].rearrange("o (p f) -> (o p) f", p=P),
                                     ping[0][:, :].bitcast(I32)).then_inc(keys_out, 16)
                        sp.wait_ge(keys_out, 16)

                    @block.tensor
                    def _(pe):
                        for n in range(turns):
                            pe.wait_ge(turn_ready, n + 1)
                            if n:
                                pe.wait_ge(copied, n)
                            for b in range(SORT // P):
                                last = nc.tensor.transpose(turned[:, b * P:(b + 1) * P], ping[0][:, b * P:(b + 1) * P], identity[:, :])
                            last.then_inc(turned_done, 1)

                    @block.scalar
                    def _(act):
                        for n in range(turns):
                            act.wait_ge(turned_done, n + 1)
                            act.activation(ping[0][:, :], turned[:, :], ACT.Copy).then_inc(copied, 1)

                    @block.vector
                    def _(dve):
                        link = chain(dve, vec)
                        dve.wait_ge(keys_in, 16)
                        at = [0]

                        def stage(m):
                            a = ping[at[0]][:, :].rearrange("p (n s w) -> p n s w", s=2, w=1 << m)
                            z = ping[1 - at[0]][:, :].rearrange("p (n s w) -> p n s w", s=2, w=1 << m)
                            nc.vector.tensor_tensor(z[:, :, 0, :], a[:, :, 0, :], a[:, :, 1, :], ALU.min)
                            link(nc.vector.tensor_tensor(z[:, :, 1, :], a[:, :, 0, :], a[:, :, 1, :], ALU.max))
                            at[0] = 1 - at[0]

                        def flip_columns(m):
                            v = ping[at[0]][:, :].rearrange("p (n s w) -> p n s w", s=2, w=1 << m)[:, :, 1, :]
                            link(nc.vector.tensor_scalar(v, v, -1.0, None, ALU.mult))

                        def flip_partitions(m):
                            link(nc.vector.tensor_scalar(ping[at[0]][:, :], ping[at[0]][:, :], sign[:, m:m + 1], None, ALU.mult))

                        def home():
                            if at[0]:
                                link(nc.vector.tensor_copy(ping[0][:, :], ping[1][:, :]))
                                at[0] = 0

                        turn_count = [0]

                        def turn():
                            home()
                            turn_count[0] += 1
                            nc.vector.drain().then_inc(turn_ready, 1)
                            dve.wait_ge(copied, turn_count[0])

                        for k in range(1, LOG_N + 1):
                            if k < LOG_F:
                                flip_columns(k)
                            elif k == LOG_F:
                                flip_partitions(0)
                            else:
                                turn()
                                if k < LOG_N:
                                    flip_columns(k - LOG_F)
                                for m in range(k - LOG_F - 1, -1, -1):
                                    stage(m)
                                turn()
                            for m in range(min(k, LOG_F) - 1, -1, -1):
                                stage(m)
                            if k < LOG_F:
                                flip_columns(k)
                            elif k < LOG_N:
                                flip_partitions(k - LOG_F)
                        home()
                        nc.vector.drain().then_inc(turn_ready, 1)

        with ExitStack() as own:
            slot_key = [sb(f"slot_key{o}", [P, COLS], I32, own) for o in range(2)]
            slot_node = [sb(f"slot_node{o}", [P, COLS], F32, own) for o in range(2)]
            slot_int = sb("slot_int", [P, COLS], I32, own)
            slot_edge = [sb(f"slot_edge{o}", [P, COLS], U32, own) for o in range(2)]
            got = [sb(f"got{o}", [P, COLS, 4], I32, own) for o in range(2)]
            tmp = sb("tmp", [P, COLS], F32, own)
            tmp2 = sb("tmp2", [P, COLS], F32, own)
            HOTS = CHUNKS * HOT_TILES
            hot_cols = sb("hot_cols", [P, HOTS], F32, own)
            hot_rows = sb("hot_rows", [P, -(-HOTS // P), P], I16, own)
            ends_in = [sb(f"ends_in{o}", [P, EF], I32, own) for o in range(2)]
            low = sb("low", [P, EF], I32, own)
            high = sb("high", [P, EF], I32, own)
            low16 = sb("low16", [P, EF], BF16, own)
            high16 = sb("high16", [P, EF], BF16, own)
            EB = 20
            one_low = sb("one_low", [P, 2, EB, P], BF16, own)
            one_high = sb("one_high", [P, 2, EB, HI], BF16, own)
            ramp = sb("ramp", [P, P], F32, own)
            ramp16 = sb("ramp16", [P, P], BF16, own)
            slot_ramp = sb("slot_ramp", [P, COLS], F32, own)
            part_f = sb("part_f", [P, 1], F32, own)
            upto = sb("upto", [P, P], F32, own)
            ones = sb("ones", [P, P], F32, own)
            count = sb("count", [P, HI], F32, own)
            total = sb("total", [P, HI], F32, own)
            cum = sb("cum", [P, HI + 1], F32, own)
            last_at = sb("last_at", [P, HI], F32, own)
            t0 = sb("t0", [P, HI], F32, own)
            t1 = sb("t1", [P, HI], F32, own)
            run = sb("run", [P, HI], I32, own)
            first = sb("first", [P, 1], F32, own)
            full = sb("full", [P, 1], F32, own)
            f1 = sb("f1", [P, 1], F32, own)
            hist = own.enter_context(nc.psum_tensor("hist", [P, BANK], F32))
            sums = own.enter_context(nc.psum_tensor("sums", [P, BANK], F32))
            full_t = own.enter_context(nc.psum_tensor("full_t", [P, BANK], F32))
            hot_t = own.enter_context(nc.psum_tensor("hot_t", [P, BANK], F32))
            with phase("keys_in", "ends_loaded", "const_done", "vec", "edge_ready", "hot_ready", "hot_used", "count_ready",
                       "sums_done", "got_done0", "got_done1", "root_ready", "root_done", "full_ready", "full_turned",
                       "cols_ready", "cols_turned", "index_ready", "index_out") as (
                    block, keys_in, ends_loaded, const_done, vec, edge_ready, hot_ready, hot_used, count_ready,
                    sums_done, got_done0, got_done1, root_ready, root_done, full_ready, full_turned,
                    cols_ready, cols_turned, index_ready, index_out):
                got_done = (got_done0, got_done1)
                steps = EF // EB
                blocks = [(b, min(P, HOTS - b * P)) for b in range(-(-HOTS // P))]

                @block.sync
                def _(sp):
                    for o in range(2):
                        sp.dma_start(slot_key[o][:, 1:RUN + 1], sorted_dram[o, 0:P * RUN].rearrange("(p t) -> p t", p=P)).then_inc(keys_in, 16)
                    sp.dma_start(ends_in[0][0:EP, :], src.rearrange("(p f) -> p f", p=EP)).then_inc(ends_loaded, 16)
                    sp.dma_start(ends_in[1][0:EP, :], dst.rearrange("(p f) -> p f", p=EP)).then_inc(ends_loaded, 16)
                    for o in range(2):
                        sp.wait_ge(index_ready, o + 1)
                        for b, n in blocks:
                            sp.dma_start(hot_index_dram[o, b * P:b * P + n, :], hot_rows[0:n, b, :]).then_inc(index_out, 16)
                    sp.wait_ge(index_out, 16 * 2 * len(blocks))

                @block.gpsimd
                def _(pool):
                    pool.iota(ramp[:, :], [[1, P]], base=0, channel_multiplier=0,
                              allow_small_or_imprecise_dtypes=True).then_inc(const_done, 1)
                    pool.iota(node_f[:, :], [[P, HI]], base=0, channel_multiplier=1,
                              allow_small_or_imprecise_dtypes=True).then_inc(const_done, 1)
                    pool.iota(slot_ramp[:, :], [[1, COLS]], base=0, channel_multiplier=0,
                              allow_small_or_imprecise_dtypes=True).then_inc(const_done, 1)
                    pool.iota(part_f[:, :], [[0, 1]], base=0, channel_multiplier=1,
                              allow_small_or_imprecise_dtypes=True).then_inc(const_done, 1)
                    pool.memset(ones[:, :], 1.0).then_inc(const_done, 1)
                    pool.wait_ge(const_done, 5)
                    pool.affine_select(out=upto[:, :], in_=ones[:, :], compare_op=ALU.is_ge, fill=0.0,
                                       base=0, pattern=[[1, P]], channel_multiplier=-1).then_inc(const_done, 1)
                    for o in range(2):
                        pool.wait_ge(edge_ready, o + 1)
                        for t in range(RUN + 1):
                            pool.indirect_dma_start(got[o][:, t, :], None, edges_dram,
                                                    bass.IndirectOffsetOnAxis(ap=slot_edge[o][:, t:t + 1], axis=0)).then_inc(got_done[o], 16)
                    for o in range(2):
                        pool.wait_ge(got_done[o], 16 * (RUN + 1))

                @block.tensor
                def _(pe):
                    pe.wait_ge(const_done, 6)
                    for o in range(2):
                        pe.wait_ge(full_ready, o + 1)
                        nc.tensor.transpose(full_t[0:D, o * P:(o + 1) * P], tmp[:, o * D:(o + 1) * D], identity[:, :]).then_inc(full_turned, 1)
                    for o in range(2):
                        for s in range(steps):
                            n = o * steps + s
                            pe.wait_ge(hot_ready, n + 1)
                            if o and not s:
                                pe.wait_ge(count_ready, 1)
                            for f in range(EB):
                                last = nc.tensor.matmul(hist[:, 0:HI], one_low[0:EP, n % 2, f, :], one_high[0:EP, n % 2, f, :],
                                                        start=(s == 0 and f == 0), stop=(s == steps - 1 and f == EB - 1))
                            last.then_inc(hot_used, 1)
                        pe.wait_ge(count_ready, o + 1)
                        nc.tensor.matmul(sums[:, 0:HI], upto[:, :], count[:, :], start=True, stop=True)
                        nc.tensor.matmul(sums[:, HI:2 * HI], ones[:, :], count[:, :], start=True, stop=True).then_inc(sums_done, 1)
                    for o in range(2):
                        pe.wait_ge(cols_ready, o + 1)
                        for b, n in blocks:
                            last = nc.tensor.transpose(hot_t[0:n, b * P:(b + 1) * P], hot_cols[:, b * P:b * P + n], identity[:, :])
                        last.then_inc(cols_turned, 1)

                @block.scalar
                def _(act):
                    act.wait_ge(root_ready, 1)
                    act.activation(tmp2[:, :], tmp2[:, :], ACT.Sqrt).then_inc(root_done, 1)

                @block.vector
                def _(dve):
                    link = chain(dve, vec)
                    V = nc.vector
                    for o in range(2):
                        V.memset(slot_key[o][:, RUN + 1:COLS], 0)
                    dve.wait_ge(keys_in, 32)
                    for o in range(2):
                        link(V.tensor_copy(slot_key[o][:, 0:1].bitcast(F32), slot_key[o][:, 1:2].bitcast(F32)))
                        link(V.tensor_scalar(slot_edge[o][:, :], slot_key[o][:, :].bitcast(U32), ID_MASK, None, ALU.bitwise_and))
                        link(V.memset(slot_edge[o][:, 0:1], 0))
                        V.drain().then_inc(edge_ready, 1)
                    dve.wait_ge(const_done, 6)
                    link(V.tensor_scalar(minus_node[:, :], node_f[:, :], -1.0, None, ALU.mult))
                    for o in range(2):
                        link(V.tensor_scalar(slot_int[:, :], slot_key[o][:, :], ID_BITS, None, ALU.logical_shift_right))
                        link(V.tensor_scalar(tmp[:, :], slot_int[:, :], -float(KEY_BIAS), float(NPAD - 1), ALU.add, ALU.min))
                        link(V.tensor_scalar(slot_node[o][:, :], tmp[:, :], 0.0, None, ALU.max))
                        link(V.tensor_scalar(starts[o][:, :], slot_edge[o][:, :], 0.0, None, ALU.is_equal))
                        link(V.memset(starts[o][:, RUN + 1:COLS], 0.0))
                        link(V.tensor_scalar(tmp[:, :], starts[o][:, :], -4096.0, 4096.0, ALU.mult, ALU.add))
                        link(V.tensor_tensor(tmp[:, :], tmp[:, :], slot_ramp[:, :], ALU.add))
                        link(V.tensor_reduce(first[:, :], tmp[:, 1:RUN + 1], AX.X, ALU.min))
                        link(V.tensor_scalar(full[:, :], first[:, :], 4096.0, None, ALU.is_ge))
                        link(V.tensor_scalar(first[:, :], first[:, :], float(RUN + 1), -1.0, ALU.min, ALU.add))
                        link(V.tensor_scalar(f1[:, :], part_f[:, :], float(COLS), None, ALU.mult))
                        link(V.tensor_tensor(fix_row[o][:, :], f1[:, :], first[:, :], ALU.add))
                        if o:
                            dve.wait_ge(full_turned, o)
                        link(V.tensor_copy(tmp[:, o * D:(o + 1) * D], full[:, 0:1].broadcast_to([P, D])))
                        V.drain().then_inc(full_ready, 1)
                        dve.wait_ge(full_turned, o + 1)
                        link(V.tensor_copy(whole[o][:, :], full_t[0:D, o * P:(o + 1) * P]))
                    for o in range(2):
                        link(V.memset(inside[o][:, :, :, 0:1], 0))
                        link(V.tensor_scalar(tmp[:, :], starts[o][:, :], -1.0, 1.0, ALU.mult, ALU.add))
                        for k in range(CHUNKS):
                            link(V.tensor_copy(inside[o][:, k, :, 1:CT + 1], tmp[:, k * CT:(k + 1) * CT].unsqueeze(1).broadcast_to([P, D, CT])))
                    dve.wait_ge(ends_loaded, 32)
                    link(V.tensor_copy(ramp16[:, :], ramp[:, :]))
                    for o in range(2):
                        link(V.tensor_scalar(low[0:EP, :], ends_in[o][0:EP, :], P - 1, None, ALU.bitwise_and))
                        link(V.tensor_scalar(high[0:EP, :], ends_in[o][0:EP, :], 7, None, ALU.logical_shift_right))
                        V.tensor_copy(low16[0:EP, :], low[0:EP, :])
                        link(V.tensor_copy(high16[0:EP, :], high[0:EP, :]))
                        for s in range(steps):
                            n = o * steps + s
                            if n >= 2:
                                dve.wait_ge(hot_used, n - 1)
                            part = slice(s * EB, (s + 1) * EB)
                            V.tensor_tensor(one_low[0:EP, n % 2, :, :], low16[0:EP, part].unsqueeze(2).broadcast_to([EP, EB, P]),
                                            ramp16[0:EP, :].unsqueeze(1).broadcast_to([EP, EB, P]), ALU.is_equal)
                            link(V.tensor_tensor(one_high[0:EP, n % 2, :, :], high16[0:EP, part].unsqueeze(2).broadcast_to([EP, EB, HI]),
                                                 ramp16[0:EP, 0:HI].unsqueeze(1).broadcast_to([EP, EB, HI]), ALU.is_equal))
                            V.drain().then_inc(hot_ready, 1)
                        dve.wait_ge(hot_used, (o + 1) * steps)
                        link(V.tensor_copy(count[:, :], hist[:, 0:HI]))
                        V.drain().then_inc(count_ready, 1)
                        if o:
                            V.tensor_copy(degree[:, :], count[:, :])
                        dve.wait_ge(sums_done, o + 1)
                        link(V.tensor_copy(total[:, :], sums[:, HI:2 * HI]))
                        link(V.memset(cum[:, 0:1], 0.0))
                        link(V.memset(t0[:, :], 1.0))
                        link(V.tensor_tensor_scan(cum[:, 1:HI + 1], t0[:, :], total[:, :], 0.0, ALU.mult, ALU.add))
                        link(V.tensor_tensor(last_at[:, :], sums[:, 0:HI], cum[:, 0:HI], ALU.add))
                        link(V.tensor_tensor(last_at[:, :], last_at[:, :], node_f[:, :], ALU.add))
                        link(V.tensor_scalar(last_at[:, :], last_at[:, :], float(P * RUN - 1), None, ALU.min))
                        link(V.tensor_scalar(run[:, :], last_at[:, :], 1.0 / RUN, None, ALU.mult))
                        link(V.tensor_scalar(t0[:, :], run[:, :], -float(RUN), None, ALU.mult))
                        link(V.tensor_tensor(t0[:, :], t0[:, :], last_at[:, :], ALU.add))
                        link(V.tensor_scalar(t1[:, :], t0[:, :], 0.0, None, ALU.is_lt))
                        link(V.tensor_scalar(t0[:, :], t0[:, :], float(RUN), None, ALU.is_ge))
                        link(V.tensor_tensor(t0[:, :], t0[:, :], t1[:, :], ALU.subtract))
                        link(V.tensor_tensor(t0[:, :], t0[:, :], run[:, :], ALU.add))
                        link(V.tensor_scalar(t0[:, :], t0[:, :], float(COLS - RUN), 1.0, ALU.mult, ALU.add))
                        link(V.tensor_tensor(end_row[o][:, :], t0[:, :], last_at[:, :], ALU.add))
                    for o in range(2):
                        dve.wait_ge(got_done[o], 16 * (RUN + 1))
                        V.memset(got[o][:, RUN + 1:COLS, :], 0)
                        link(V.tensor_scalar(tmp2[:, :], starts[o][:, :], -1.0, 1.0, ALU.mult, ALU.add))
                        link(V.tensor_copy(tmp[:, :], got[o][:, :, 1 - o]))
                        link(V.tensor_tensor(tmp[:, :], tmp[:, :], tmp2[:, :], ALU.mult))
                        link(V.tensor_tensor(slot_node[o][:, :], slot_node[o][:, :], starts[o][:, :], ALU.mult))
                        link(V.tensor_tensor(tmp[:, :], tmp[:, :], slot_node[o][:, :], ALU.add))
                        V.tensor_copy(gather_index[o][:, :], tmp[:, :])
                        if o:
                            dve.wait_ge(cols_turned, o)
                        link(V.tensor_copy(hot_cols[:, :].rearrange("p (k i) -> p k i", i=HOT_TILES),
                                           tmp[:, :].rearrange("p (k t) -> p k t", t=CT)[:, :, DMA_TILES:CT]))
                        V.drain().then_inc(cols_ready, 1)
                        dve.wait_ge(cols_turned, o + 1)
                        if o:
                            dve.wait_ge(index_out, 16 * len(blocks))
                        for b, n in blocks:
                            link(V.tensor_copy(hot_rows[0:n, b, :], hot_t[0:n, b * P:(b + 1) * P]))
                        V.drain().then_inc(index_ready, 1)
                        w_got = got[o][:, :, 2].bitcast(F32)
                        if o == 0:
                            link(V.tensor_scalar(tmp[:, :], w_got, 0.0, None, ALU.is_gt))
                            link(V.tensor_tensor(tmp[:, :], tmp[:, :], tmp2[:, :], ALU.mult))
                            link(V.tensor_scalar(tmp2[:, :], w_got, 1e-30, None, ALU.max))
                            V.drain().then_inc(root_ready, 1)
                            dve.wait_ge(root_done, 1)
                            link(V.tensor_tensor(root_weight[:, :], tmp2[:, :], tmp[:, :], ALU.mult))
                        else:
                            link(V.tensor_tensor(tmp[:, :], w_got, tmp2[:, :], ALU.mult))
                            link(V.tensor_tensor(weight[:, :], tmp[:, :], starts[o][:, :], ALU.add))
                            link(V.memset(real[:, :], 1.0))
                            for part in (weight, real):
                                V.memset(part[:, 0:1], 0.0)
                                link(V.memset(part[:, RUN + 1:COLS], 0.0))

        gathered = [sb(f"gathered{i}", [P, CT, D]) for i in range(2)]
        staged = [sb(f"staged{i}", [P, CT, D]) for i in range(2)]
        own_row = [sb(f"own_row{i}", [P, D, CT + 1]) for i in range(2)]
        value = sb("value", [P, D, CT + 1])
        result = [sb(f"result{i}", [P, D, CT + 1]) for i in range(2)]
        last_row = sb("last_row", [P, D])
        last_t = sb("last_t", [D, 1 + P])
        fix = sb("fix", [P, D])
        BY_SRC, BY_DST = 0, 1
        LAST = RUN - (CHUNKS - 1) * CT

        def of_chunk(tile, k):
            return tile[:, k * CT:(k + 1) * CT]

        def over_channels(columns):
            return columns.unsqueeze(1).broadcast_to([P, D, CT])

        def layer_norm(dve, link, norm_ready, norm_root, count, to, of):
            V = nc.vector
            mean, var = stat[:, 0, :], stat[:, 1, :]
            link(V.tensor_reduce(mean, of, AX.X, ALU.add))
            link(V.tensor_scalar(mean, mean, 1.0 / D, None, ALU.mult))
            link(V.tensor_tensor(to, of, mean.unsqueeze(2).broadcast_to([P, HI, D]), ALU.subtract))
            link(V.tensor_tensor(spare[:, :, :], to, to, ALU.mult))
            link(V.tensor_reduce(var, spare[:, :, :], AX.X, ALU.add))
            link(V.tensor_scalar(var, var, 1.0 / D, EPS, ALU.mult, ALU.add))
            V.drain().then_inc(norm_ready, 1)
            dve.wait_ge(norm_root, count)
            link(V.reciprocal(stat[:, 3, :], stat[:, 2, :]))
            link(V.tensor_tensor(to, to, stat[:, 3, :].unsqueeze(2).broadcast_to([P, HI, D]), ALU.mult))

        def root(act, norm_ready, norm_root, count):
            act.wait_ge(norm_ready, count)
            act.activation(stat[:, 2, :], stat[:, 1, :], ACT.Sqrt).then_inc(norm_root, 1)

        def gather_chunks(pool, o, chunk_in, used, tiles):
            for k in range(CHUNKS):
                if k >= 2:
                    pool.wait_ge(used, k - 1)
                for t in range(tiles):
                    at = k * CT + t
                    pool.indirect_dma_start(gathered[k % 2][:, t, :], None, table_dram,
                                            bass.IndirectOffsetOnAxis(ap=gather_index[o][:, at:at + 1], axis=0)).then_inc(chunk_in[k % 2], 16)
            for i in range(2):
                pool.wait_ge(chunk_in[i], 16 * tiles * CHUNKS // 2)

        def hot_blocks(dve, k, part, index_rows, hot, hot_index_in, hot_ready, hot_used):
            dve.wait_ge(hot_index_in[k % 2], 16 * (k // 2 + 1))
            for i in part:
                n = k * len(DVE_BLOCKS) + i
                if n >= RING:
                    dve.wait_ge(hot_used, n - RING + 1)
                nc.vector.tensor_scalar(hot[n % RING][:, :], index_rows[k % 2][:, :], node_f[:, DVE_BLOCKS[i]:DVE_BLOCKS[i] + 1],
                                        None, ALU.is_equal).then_inc(hot_ready, 1)

        def act_hot_block(act, n, index_rows, far, act_hot, hot_index_in, far_ready, act_hot_ready, act_hot_used, acc_done):
            k, i = divmod(n, len(ACT_BLOCKS))
            if k >= CHUNKS:
                return
            b = ACT_BLOCKS[i]
            act.wait_ge(hot_index_in[k % 2], 16 * (k // 2 + 1))
            if n >= 2:
                act.wait_ge(act_hot_ready, n - 1)
            act.activation(far[n % 2][:, :], index_rows[k % 2][:, :], ACT.Abs, bias=minus_node[:, b:b + 1]).then_inc(far_ready, 1)
            if n >= ACT_RING:
                k_was, i_was = divmod(n - ACT_RING, len(ACT_BLOCKS))
                if i_was == len(ACT_BLOCKS) - 1:
                    act.wait_ge(acc_done, (k_was + 1) * HOT_BANKS)
                else:
                    act.wait_ge(act_hot_used, k_was * (len(ACT_BLOCKS) - 1) + i_was + 1)
            act.wait_ge(far_ready, n + 1)
            act.activation(act_hot[n % ACT_RING][:, :], far[n % 2][:, :], ACT.Relu, bias=1.0, scale=-1.0).then_inc(act_hot_ready, 1)

        def load_hot_index(sp, o, k, index_rows, hot_index_in, hot_ready, act_hot_ready):
            if k >= 2:
                sp.wait_ge(hot_ready, (k - 1) * len(DVE_BLOCKS))
                sp.wait_ge(act_hot_ready, (k - 1) * len(ACT_BLOCKS))
            of = hot_index_dram[o, k * HOT_TILES:(k + 1) * HOT_TILES, :].rearrange("i p -> (i p)")
            sp.dma_start(index_rows[k % 2][:, :], of.partition_broadcast(P)).then_inc(hot_index_in[k % 2], 16)

        def multiply_hot(pe, hot, act_hot, acc, moved, summed, hot_ready, hot_used, act_hot_ready, act_hot_used, acc_done, acc_moved, sum_done, row_ready):
            def sum_up(k):
                for j in range(HOT_BANKS):
                    pe.wait_ge(acc_moved, k * HOT_BANKS + j + 1)
                    if k and not j:
                        pe.wait_ge(row_ready, k)
                    for i in range(BANK // P):
                        t = j * (BANK // P) + i
                        last = nc.tensor.matmul(summed[:, t * D:(t + 1) * D], moved[k % 2][:, t * P:(t + 1) * P], sum_parts[:, :], start=True, stop=True)
                last.then_inc(sum_done, 1)

            for k in range(CHUNKS):
                for b in range(HI):
                    if b == 6 and k:
                        sum_up(k - 1)
                    if b in ACT_BLOCKS:
                        n = k * len(ACT_BLOCKS) + ACT_BLOCKS.index(b)
                        pe.wait_ge(act_hot_ready, n + 1)
                        columns, columns_used = act_hot[n % ACT_RING], act_hot_used
                    else:
                        n = k * len(DVE_BLOCKS) + DVE_BLOCKS.index(b)
                        pe.wait_ge(hot_ready, n + 1)
                        columns, columns_used = hot[n % RING], hot_used
                    for j in range(HOT_BANKS):
                        m = k * HOT_BANKS + j
                        if not b and m >= len(acc):
                            pe.wait_ge(acc_moved, m - len(acc) + 1)
                        last = nc.tensor.matmul(acc[m % len(acc)][0:SPLIT, :], parts[:, b, :, :].rearrange("p s c -> p (s c)"),
                                                columns[:, j * BANK:(j + 1) * BANK], start=(b == 0), stop=(b == HI - 1))
                        if b == HI - 1:
                            last.then_inc(acc_done, 1)
                    if b < HI - 1:
                        last.then_inc(columns_used, 1)
            sum_up(CHUNKS - 1)

        def move_parts(act, k, acc, moved, acc_done, acc_moved, sum_done):
            for j in range(HOT_BANKS):
                m = k * HOT_BANKS + j
                act.wait_ge(acc_done, m + 1)
                if k >= 2 and not j:
                    act.wait_ge(sum_done, k - 1)
                act.activation(moved[k % 2][:, j * BANK:(j + 1) * BANK], acc[m % len(acc)][0:SPLIT, :], ACT.Copy).then_inc(acc_moved, 1)

        def move_rows(act, k, summed, sum_done, used, row_ready):
            act.wait_ge(sum_done, k + 1)
            if k >= 2:
                act.wait_ge(used, k - 1)
            act.activation(gathered[k % 2][:, DMA_TILES:CT, :].rearrange("p t c -> p (t c)"), summed[:, :], ACT.Copy).then_inc(row_ready, 1)

        def scalar_chunks(act, index_rows, far, act_hot, hot_index_in, far_ready, act_hot_ready, act_hot_used, acc, moved, summed,
                          acc_done, acc_moved, sum_done, used, row_ready, result_ready, stored, staged_ready):
            def hot_block(n):
                act_hot_block(act, n, index_rows, far, act_hot, hot_index_in, far_ready, act_hot_ready, act_hot_used, acc_done)
            count = len(ACT_BLOCKS)
            for n in range(ACT_RING):
                hot_block(n)
            for k in range(CHUNKS + 1):
                if k:
                    move_rows(act, k - 1, summed, sum_done, used, row_ready)
                for n in range(k * count + ACT_RING, (k + 1) * count):
                    hot_block(n)
                if k >= 2:
                    stage_result(act, k - 2, result_ready, stored, staged_ready)
                hot_block((k + 1) * count)
                hot_block((k + 1) * count + 1)
                if k < CHUNKS:
                    move_parts(act, k, acc, moved, acc_done, acc_moved, sum_done)
                hot_block((k + 1) * count + 2)
            stage_result(act, CHUNKS - 1, result_ready, stored, staged_ready)

        def stage_result(act, k, result_ready, stored, staged_ready):
            act.wait_ge(result_ready, k + 1)
            if k >= 2:
                act.wait_ge(stored[k % 2], 16 * (k // 2))
            act.activation(staged[k % 2][:, :, :], result[k % 2][:, :, 1:CT + 1].rearrange("p c t -> p t c"), ACT.Copy).then_inc(staged_ready, 1)

        def store_chunk(sp, k, staged_ready, stored):
            sp.wait_ge(staged_ready, k + 1)
            sp.dma_start(scan_rows[:, k * CT:(k + 1) * CT, :], staged[k % 2][:, :, :]).then_inc(stored[k % 2], 16)

        def turn_last(pe, turned, last_ready, last_turned, joined_ready, w=D):
            pe.wait_ge(last_ready, 1)
            nc.tensor.transpose(turned[0:w, 0:P], last_row[:, 0:w], identity[:, :]).then_inc(last_turned, 1)
            pe.wait_ge(joined_ready, 1)
            nc.tensor.transpose(turned[:, P:P + w], last_t[0:w, 0:P], identity[0:w, 0:w]).then_inc(last_turned, 1)

        def join_runs(dve, link, o, op, turned, last_turned, joined_ready, w=D):
            V = nc.vector
            link(V.memset(last_t[0:w, 0:1], 0.0))
            dve.wait_ge(last_turned, 1)
            link(V.tensor_tensor_scan(last_t[0:w, 1:P + 1], whole[o][0:w, :], turned[0:w, 0:P], 0.0, ALU.mult, op))
            V.drain().then_inc(joined_ready, 1)

        def fix_ends(dve, link, op, turned, last_turned, fix_in, fix_ready, w=D):
            dve.wait_ge(last_turned, 2)
            dve.wait_ge(fix_in, 16)
            link(nc.vector.tensor_tensor(fix[:, 0:w], fix[:, 0:w], turned[:, P:P + w], op))
            nc.vector.drain().then_inc(fix_ready, 1)

        def gather_ends(pool, o, table, stored, count, fix_in, fix_ready, ends_in_, w=D):
            for s in stored:
                pool.wait_ge(s, count)
            row = bass.IndirectOffsetOnAxis(ap=fix_row[o][:, :], axis=0)
            pool.indirect_dma_start(fix[:, 0:w], None, table, row).then_inc(fix_in, 16)
            pool.wait_ge(fix_ready, 1)
            pool.indirect_dma_start(table, row, fix[:, 0:w], None).then_inc(fix_in, 16)
            pool.wait_ge(fix_in, 32)
            for h in range(HI):
                pool.indirect_dma_start(ends[:, h, 0:w], None, table,
                                        bass.IndirectOffsetOnAxis(ap=end_row[o][:, h:h + 1], axis=0)).then_inc(ends_in_, 16)
            pool.wait_ge(ends_in_, 16 * HI)

        def carry(link, k, tile, before):
            if k:
                link(nc.vector.tensor_copy(tile[:, :, 0:1], before[:, :, CT:CT + 1]))
            else:
                link(nc.vector.memset(tile[:, :, 0:1], 0.0))

        def spread_own_rows(link, k, o):
            V = nc.vector
            carry(link, k, value, own_row[(k - 1) % 2])
            link(V.tensor_tensor(value[:, :, 1:CT + 1], gathered[k % 2][:, :, :].rearrange("p t c -> p c t"),
                                 over_channels(of_chunk(starts[o], k)), ALU.mult))
            link(V.tensor_tensor_scan(flat(own_row[k % 2]), inside_of(o, k), flat(value), 0.0, ALU.mult, ALU.add))

        def flat(tile):
            return tile[:, :, :].rearrange("p c t -> p (c t)")

        def inside_of(o, k):
            return inside[o][:, k, :, :].rearrange("p c t -> p (c t)")

        def scan_value(dve, link, k, o, op, staged_ready, result_ready):
            carry(link, k, value, result[(k - 1) % 2])
            if k >= 2:
                dve.wait_ge(staged_ready, k - 1)
            link(nc.vector.tensor_tensor_scan(flat(result[k % 2]), inside_of(o, k), flat(value), 0.0, ALU.mult, op))
            nc.vector.drain().then_inc(result_ready, 1)

        def keep_last(link, last_ready):
            link(nc.vector.tensor_copy(last_row[:, :], result[(CHUNKS - 1) % 2][:, :, 1 + LAST]))
            nc.vector.drain().then_inc(last_ready, 1)

        def wait_rows(dve, k, chunk_in, tiles, row_ready=None):
            dve.wait_ge(chunk_in[k % 2], 16 * tiles * (k // 2 + 1))
            if row_ready is not None:
                dve.wait_ge(row_ready, k + 1)

        COMMON = ("chunk_in0", "chunk_in1", "used", "vec", "result_ready", "staged_ready", "stored0", "stored1",
                  "last_ready", "last_turned", "joined_ready", "fix_in", "fix_ready", "ends_in",
                  "rows_ready", "table_in", "norm_ready", "norm_root")
        HOTS_ = ("hot_index_in0", "hot_index_in1", "hot_ready", "hot_used", "far_ready", "act_hot_ready", "act_hot_used",
                 "acc_done", "acc_moved", "sum_done", "row_ready")

        FIRST_PART, SECOND_PART = range(0, 12), range(12, len(DVE_BLOCKS))

        def sum_chunk(dve, link, k, factor, chunk_in, row_ready, used):
            V = nc.vector
            wait_rows(dve, k, chunk_in, DMA_TILES, row_ready)
            link(V.tensor_tensor(value[:, :, 1:CT + 1], gathered[k % 2][:, :, :].rearrange("p t c -> p c t"),
                                 over_channels(of_chunk(factor, k)), ALU.mult))
            V.drain().then_inc(used, 1)

        with ExitStack() as own:
            weight_sum = sb("weight_sum", [P, COLS], F32, own)
            keep = sb("keep", [P, COLS], F32, own)
            turned = own.enter_context(nc.psum_tensor("turned_d", [P, BANK], F32))
            with phase("vec", "sum_ready", "stored", "last_ready", "last_turned", "joined_ready", "fix_in", "fix_ready",
                       "ends_in", "norm_ready", "norm_root") as (
                    block, vec, sum_ready, stored, last_ready, last_turned, joined_ready, fix_in, fix_ready,
                    ends_in_, norm_ready, norm_root):
                @block.sync
                def _(sp):
                    sp.wait_ge(sum_ready, 1)
                    sp.dma_start(degree_dram.rearrange("(p t) c -> p (t c)", p=P), weight_sum[:, :]).then_inc(stored, 16)

                @block.gpsimd
                def _(pool):
                    gather_ends(pool, BY_DST, degree_dram, (stored,), 16, fix_in, fix_ready, ends_in_, w=1)

                @block.tensor
                def _(pe):
                    turn_last(pe, turned, last_ready, last_turned, joined_ready, w=1)

                @block.scalar
                def _(act):
                    root(act, norm_ready, norm_root, 1)

                @block.vector
                def _(dve):
                    link = chain(dve, vec)
                    V = nc.vector
                    link(V.tensor_scalar(keep[:, :], starts[BY_DST][:, :], -1.0, 1.0, ALU.mult, ALU.add))
                    link(V.tensor_tensor_scan(weight_sum[:, :], keep[:, :], weight[:, :], 0.0, ALU.mult, ALU.add))
                    V.drain().then_inc(sum_ready, 1)
                    link(V.tensor_copy(last_row[:, 0:1], weight_sum[:, RUN:RUN + 1]))
                    V.drain().then_inc(last_ready, 1)
                    join_runs(dve, link, BY_DST, ALU.add, turned, last_turned, joined_ready, w=1)
                    fix_ends(dve, link, ALU.add, turned, last_turned, fix_in, fix_ready, w=1)
                    dve.wait_ge(ends_in_, 16 * HI)
                    link(V.tensor_scalar(stat[:, 1, :], ends[:, :, 0], 1e-30, None, ALU.max))
                    V.drain().then_inc(norm_ready, 1)
                    dve.wait_ge(norm_root, 1)
                    link(V.reciprocal(stat[:, 3, :], stat[:, 2, :]))
                    link(V.tensor_scalar(stat[:, 0, :], ends[:, :, 0], 0.0, None, ALU.is_gt))
                    link(V.tensor_tensor(inv_root[:, :], stat[:, 3, :], stat[:, 0, :], ALU.mult))

        with ExitStack() as hots:
            index_rows = [sb(f"index_rows{i}", [P, HOT], I16, hots) for i in range(2)]
            hot_space = sb("hot_space", [P, RING * HOT], BF16, hots)
            hot = [hot_space[:, i * HOT:(i + 1) * HOT] for i in range(RING)]
            act_hot = [sb(f"act_hot{i}", [P, HOT], BF16, hots) for i in range(ACT_RING)]
            far = [sb(f"far{i}", [P, HOT], BF16, hots) for i in range(2)]
            moved = [sb(f"moved{i}", [SPLIT, HOT], BF16, hots) for i in range(2)]

            with ExitStack() as own:
                acc = [own.enter_context(nc.psum_tensor(f"acc0_{i}", [P, BANK], F32)) for i in range(7)]
                summed = own.enter_context(nc.psum_tensor("summed0", [P, BANK], F32))
                with phase(*COMMON, *HOTS_) as (
                        block, chunk_in0, chunk_in1, used, vec, result_ready, staged_ready, stored0, stored1,
                        last_ready, last_turned, joined_ready, fix_in, fix_ready, ends_in_, rows_ready, table_in, norm_ready, norm_root,
                        hot_index_in0, hot_index_in1, hot_ready, hot_used, far_ready, act_hot_ready, act_hot_used, acc_done, acc_moved, sum_done, row_ready):
                    chunk_in, stored, hot_index_in = (chunk_in0, chunk_in1), (stored0, stored1), (hot_index_in0, hot_index_in1)

                    @block.sync
                    def _(sp):
                        for k in range(CHUNKS + 2):
                            if k < CHUNKS:
                                load_hot_index(sp, BY_DST, k, index_rows, hot_index_in, hot_ready, act_hot_ready)
                            if k >= 2:
                                store_chunk(sp, k - 2, staged_ready, stored)
                        sp.wait_ge(rows_ready, 1)
                        sp.dma_start(table_nodes, state[:, :, :]).then_inc(table_in, 16)
                        sp.wait_ge(table_in, 16)

                    @block.gpsimd
                    def _(pool):
                        gather_chunks(pool, BY_DST, chunk_in, used, DMA_TILES)
                        gather_ends(pool, BY_DST, scan_dram, stored, 16 * CHUNKS // 2, fix_in, fix_ready, ends_in_)

                    @block.tensor
                    def _(pe):
                        multiply_hot(pe, hot, act_hot, acc, moved, summed, hot_ready, hot_used, act_hot_ready, act_hot_used, acc_done, acc_moved, sum_done, row_ready)
                        turn_last(pe, acc[0], last_ready, last_turned, joined_ready)

                    @block.scalar
                    def _(act):
                        scalar_chunks(act, index_rows, far, act_hot, hot_index_in, far_ready, act_hot_ready, act_hot_used, acc, moved, summed,
                                      acc_done, acc_moved, sum_done, used, row_ready, result_ready, stored, staged_ready)
                        root(act, norm_ready, norm_root, 1)

                    @block.vector
                    def _(dve):
                        link = chain(dve, vec)
                        for k in range(CHUNKS + 1):
                            if k < CHUNKS:
                                hot_blocks(dve, k, FIRST_PART, index_rows, hot, hot_index_in, hot_ready, hot_used)
                            if k:
                                sum_chunk(dve, link, k - 1, real, chunk_in, row_ready, used)
                            if k < CHUNKS:
                                hot_blocks(dve, k, SECOND_PART, index_rows, hot, hot_index_in, hot_ready, hot_used)
                            if k:
                                scan_value(dve, link, k - 1, BY_DST, ALU.add, staged_ready, result_ready)
                        keep_last(link, last_ready)
                        join_runs(dve, link, BY_DST, ALU.add, acc[0], last_turned, joined_ready)
                        fix_ends(dve, link, ALU.add, acc[0], last_turned, fix_in, fix_ready)
                        dve.wait_ge(ends_in_, 16 * HI)
                        layer_norm(dve, link, norm_ready, norm_root, 1, state[:, :, :], ends[:, :, :])
                        link(nc.vector.tensor_copy(rows[:, :, :], state[:, :, :]))
                        nc.vector.drain().then_inc(rows_ready, 1)
                        split_rows(link, rows[:, :, :])

            with ExitStack() as own:
                acc = [own.enter_context(nc.psum_tensor(f"acc1_{i}", [P, BANK], F32)) for i in range(7)]
                summed = own.enter_context(nc.psum_tensor("summed1", [P, BANK], F32))
                with nc.Fori(0, 10):
                    with phase(*COMMON, *HOTS_) as (
                            block, chunk_in0, chunk_in1, used, vec, result_ready, staged_ready, stored0, stored1,
                            last_ready, last_turned, joined_ready, fix_in, fix_ready, ends_in_, rows_ready, table_in, norm_ready, norm_root,
                            hot_index_in0, hot_index_in1, hot_ready, hot_used, far_ready, act_hot_ready, act_hot_used, acc_done, acc_moved, sum_done, row_ready):
                        chunk_in, stored, hot_index_in = (chunk_in0, chunk_in1), (stored0, stored1), (hot_index_in0, hot_index_in1)

                        @block.sync
                        def _(sp):
                            for k in range(CHUNKS + 2):
                                if k < CHUNKS:
                                    load_hot_index(sp, BY_SRC, k, index_rows, hot_index_in, hot_ready, act_hot_ready)
                                if k >= 2:
                                    store_chunk(sp, k - 2, staged_ready, stored)
                            sp.wait_ge(rows_ready, 1)
                            sp.dma_start(table_nodes, rows[:, :, :]).then_inc(table_in, 16)
                            sp.wait_ge(table_in, 16)

                        @block.gpsimd
                        def _(pool):
                            gather_chunks(pool, BY_SRC, chunk_in, used, DMA_TILES)
                            gather_ends(pool, BY_SRC, scan_dram, stored, 16 * CHUNKS // 2, fix_in, fix_ready, ends_in_)

                        @block.tensor
                        def _(pe):
                            multiply_hot(pe, hot, act_hot, acc, moved, summed, hot_ready, hot_used, act_hot_ready, act_hot_used, acc_done, acc_moved, sum_done, row_ready)
                            turn_last(pe, acc[0], last_ready, last_turned, joined_ready)

                        @block.scalar
                        def _(act):
                            scalar_chunks(act, index_rows, far, act_hot, hot_index_in, far_ready, act_hot_ready, act_hot_used, acc, moved, summed,
                                          acc_done, acc_moved, sum_done, used, row_ready, result_ready, stored, staged_ready)

                        @block.vector
                        def _(dve):
                            link = chain(dve, vec)
                            V = nc.vector
                            for k in range(CHUNKS + 1):
                                if k < CHUNKS:
                                    hot_blocks(dve, k, FIRST_PART, index_rows, hot, hot_index_in, hot_ready, hot_used)
                                if k:
                                    c = k - 1
                                    wait_rows(dve, c, chunk_in, DMA_TILES, row_ready)
                                    spread_own_rows(link, c, BY_SRC)
                                    link(V.tensor_tensor(value[:, :, 1:CT + 1], gathered[c % 2][:, :, :].rearrange("p t c -> p c t"),
                                                         own_row[c % 2][:, :, 1:CT + 1], ALU.subtract))
                                    V.drain().then_inc(used, 1)
                                if k < CHUNKS:
                                    hot_blocks(dve, k, SECOND_PART, index_rows, hot, hot_index_in, hot_ready, hot_used)
                                if k:
                                    link(V.scalar_tensor_tensor(value[:, :, 1:CT + 1], value[:, :, 1:CT + 1], 0.0,
                                                                over_channels(of_chunk(root_weight, c)), ALU.max, ALU.mult))
                                    scan_value(dve, link, c, BY_SRC, ALU.max, staged_ready, result_ready)
                            keep_last(link, last_ready)
                            join_runs(dve, link, BY_SRC, ALU.max, acc[0], last_turned, joined_ready)
                            fix_ends(dve, link, ALU.max, acc[0], last_turned, fix_in, fix_ready)
                            dve.wait_ge(ends_in_, 16 * HI)
                            link(V.tensor_tensor(rows[:, :, :], rows[:, :, :], ends[:, :, :], ALU.add))
                            V.drain().then_inc(rows_ready, 1)
                            split_rows(link, rows[:, :, :])

            with phase("vec", "norm_ready", "norm_root", "rows_ready", "table_in") as (block, vec, norm_ready, norm_root, rows_ready, table_in):
                @block.scalar
                def _(act):
                    root(act, norm_ready, norm_root, 1)

                @block.sync
                def _(sp):
                    sp.wait_ge(rows_ready, 1)
                    sp.dma_start(table_nodes, rows[:, :, :]).then_inc(table_in, 16)
                    sp.wait_ge(table_in, 16)

                @block.vector
                def _(dve):
                    link = chain(dve, vec)
                    V = nc.vector
                    link(V.tensor_tensor(ends[:, :, :], state[:, :, :], rows[:, :, :], ALU.add))
                    layer_norm(dve, link, norm_ready, norm_root, 1, state[:, :, :], ends[:, :, :])
                    link(V.tensor_tensor(rows[:, :, :], state[:, :, :], inv_root[:, :].unsqueeze(2).broadcast_to([P, HI, D]), ALU.mult))
                    V.drain().then_inc(rows_ready, 1)
                    split_rows(link, rows[:, :, :])

            GATES = (0, 4, 6)
            GW = len(GATES) * D
            with ExitStack() as own:
                gate_w = sb("gate_w", [D + 1, 3, D], F32, own)
                bias_in = sb("bias_in", [D + 1, 3, GW], F32, own)
                peep = sb("peep", [P, D], F32, own)
                flat_t = hot_space[0:D + 1, 0:2 * NPAD].bitcast(F32)
                cell = spare
                gate = hot_space[:, 2 * NPAD:2 * (NPAD + HI * D)].bitcast(F32).rearrange("p (h c) -> p h c", c=D)
                psum = [own.enter_context(nc.psum_tensor(f"bank{i}", [P, BANK], F32)) for i in range(8)]
                acc, summed = psum[0:7], psum[7]
                with nc.Fori(0, 3) as layer:
                    with phase(*COMMON, *HOTS_, "weights_in", "bias_ready", "agg_ready", "agg_turned", "flat_ready", "gates_done", "act_done") as (
                            block, chunk_in0, chunk_in1, used, vec, result_ready, staged_ready, stored0, stored1,
                            last_ready, last_turned, joined_ready, fix_in, fix_ready, ends_in_, rows_ready, table_in, norm_ready, norm_root,
                            hot_index_in0, hot_index_in1, hot_ready, hot_used, far_ready, act_hot_ready, act_hot_used, acc_done, acc_moved, sum_done, row_ready,
                            weights_in, bias_ready, agg_ready, agg_turned, flat_ready, gates_done, act_done):
                        chunk_in, stored, hot_index_in = (chunk_in0, chunk_in1), (stored0, stored1), (hot_index_in0, hot_index_in1)
                        per_bank = 4
                        banks = -(-HI // per_bank)
                        per_gate = 5

                        @block.sync
                        def _(sp):
                            for i, g in enumerate(GATES):
                                sp.dma_start(gate_w[0:D, i, :], conv_w[bass.ds(layer, 1), g, :, :].rearrange("l k n -> (l k) n")).then_inc(weights_in, 16)
                                for r, gg in enumerate((g, g + 1)):
                                    sp.dma_start(bias_in[D:D + 1, r, i * D:(i + 1) * D], conv_b[bass.ds(layer, 1), gg, :]).then_inc(weights_in, 16)
                                sp.dma_start(bias_in[D:D + 1, 2, i * D:(i + 1) * D], bg[bass.ds(layer, 1), (0, 2, 3)[i], :]).then_inc(weights_in, 16)
                            sp.dma_start(peep[:, :], wc[bass.ds(layer, 1), 2, :].broadcast_to([P, D])).then_inc(weights_in, 16)
                            for k in range(CHUNKS + 2):
                                if k < CHUNKS:
                                    load_hot_index(sp, BY_DST, k, index_rows, hot_index_in, hot_ready, act_hot_ready)
                                if k >= 2:
                                    store_chunk(sp, k - 2, staged_ready, stored)
                            sp.wait_ge(rows_ready, 1)
                            sp.dma_start(table_nodes, gate[:, :, :]).then_inc(table_in, 16)
                            sp.wait_ge(table_in, 16)
                            sp.wait_ge(weights_in, 16 * 13)

                        @block.gpsimd
                        def _(pool):
                            gather_chunks(pool, BY_DST, chunk_in, used, DMA_TILES)
                            gather_ends(pool, BY_DST, scan_dram, stored, 16 * CHUNKS // 2, fix_in, fix_ready, ends_in_)

                        @block.tensor
                        def _(pe):
                            multiply_hot(pe, hot, act_hot, acc, moved, summed, hot_ready, hot_used, act_hot_ready, act_hot_used, acc_done, acc_moved, sum_done, row_ready)
                            turn_last(pe, acc[0], last_ready, last_turned, joined_ready)
                            pe.wait_ge(agg_ready, 1)
                            for h in range(HI):
                                last = nc.tensor.transpose(psum[h // per_bank][0:D, (h % per_bank) * P:(h % per_bank + 1) * P], ends[:, h, :], identity[:, :])
                            last.then_inc(agg_turned, 1)
                            pe.wait_ge(bias_ready, 1)
                            pe.wait_ge(flat_ready, banks)
                            for h in range(HI):
                                last = nc.tensor.matmul(psum[h // per_gate][:, (h % per_gate) * GW:(h % per_gate + 1) * GW],
                                                        flat_t[:, h * P:(h + 1) * P], gate_w[:, :, :].rearrange("k g n -> k (g n)"), start=True, stop=True)
                            last.then_inc(gates_done, 1)

                        @block.scalar
                        def _(act):
                            scalar_chunks(act, index_rows, far, act_hot, hot_index_in, far_ready, act_hot_ready, act_hot_used, acc, moved, summed,
                                          acc_done, acc_moved, sum_done, used, row_ready, result_ready, stored, staged_ready)
                            act.wait_ge(agg_turned, 1)
                            for b in range(banks):
                                n = min(per_bank, HI - b * per_bank) * P
                                act.activation(flat_t[0:D, b * per_bank * P:b * per_bank * P + n], psum[b][0:D, 0:n], ACT.Copy).then_inc(flat_ready, 1)
                            act.wait_ge(gates_done, 1)

                            def of_gate(i, b):
                                return psum[b][:, 0:per_gate * GW].rearrange("p (h n) -> p h n", n=GW)[:, :, i * D:(i + 1) * D]
                            for b in range(HI // per_gate):
                                cols = slice(b * per_gate, (b + 1) * per_gate)
                                act.activation(ends[:, cols, :], of_gate(0, b), ACT.Sigmoid).then_inc(act_done, 1)
                                act.activation(gate[:, cols, :], of_gate(1, b), ACT.Tanh).then_inc(act_done, 1)
                            act.wait_ge(norm_ready, 1)
                            act.activation(gate[:, :, :], gate[:, :, :], ACT.Sigmoid).then_inc(act_done, 1)
                            act.activation(cell[:, :, :], cell[:, :, :], ACT.Tanh).then_inc(act_done, 1)

                        @block.vector
                        def _(dve):
                            link = chain(dve, vec)
                            V = nc.vector
                            dve.wait_ge(weights_in, 16 * 13)
                            bias = gate_w[D:D + 1, :, :].rearrange("k g n -> k (g n)")
                            link(V.tensor_tensor(bias, bias_in[D:D + 1, 0, :], bias_in[D:D + 1, 1, :], ALU.add))
                            link(V.tensor_tensor(bias, bias, bias_in[D:D + 1, 2, :], ALU.add))
                            V.drain().then_inc(bias_ready, 1)
                            for k in range(CHUNKS + 1):
                                if k < CHUNKS:
                                    hot_blocks(dve, k, FIRST_PART, index_rows, hot, hot_index_in, hot_ready, hot_used)
                                if k:
                                    sum_chunk(dve, link, k - 1, weight, chunk_in, row_ready, used)
                                if k < CHUNKS:
                                    hot_blocks(dve, k, SECOND_PART, index_rows, hot, hot_index_in, hot_ready, hot_used)
                                if k:
                                    scan_value(dve, link, k - 1, BY_DST, ALU.add, staged_ready, result_ready)
                            keep_last(link, last_ready)
                            join_runs(dve, link, BY_DST, ALU.add, acc[0], last_turned, joined_ready)
                            fix_ends(dve, link, ALU.add, acc[0], last_turned, fix_in, fix_ready)
                            dve.wait_ge(ends_in_, 16 * HI)
                            link(V.tensor_tensor(ends[:, :, :], ends[:, :, :], inv_root[:, :].unsqueeze(2).broadcast_to([P, HI, D]), ALU.mult))
                            link(V.memset(flat_t[D:D + 1, :], 1.0))
                            V.drain().then_inc(agg_ready, 1)
                            gates = 2 * (HI // per_gate)
                            dve.wait_ge(act_done, gates)
                            link(V.tensor_tensor(cell[:, :, :], ends[:, :, :], gate[:, :, :], ALU.mult))
                            link(V.tensor_tensor(gate[:, :, :], cell[:, :, :], peep[:, :].unsqueeze(1).broadcast_to([P, HI, D]), ALU.mult))
                            for b in range(HI // per_gate):
                                cols = slice(b * per_gate, (b + 1) * per_gate)
                                link(V.tensor_tensor(gate[:, cols, :], gate[:, cols, :],
                                                     psum[b][:, 0:per_gate * GW].rearrange("p (h n) -> p h n", n=GW)[:, :, 2 * D:3 * D], ALU.add))
                            V.drain().then_inc(norm_ready, 1)
                            dve.wait_ge(act_done, gates + 2)
                            link(V.tensor_tensor(rows[:, :, :], gate[:, :, :], cell[:, :, :], ALU.mult))
                            link(V.tensor_tensor(gate[:, :, :], rows[:, :, :], inv_root[:, :].unsqueeze(2).broadcast_to([P, HI, D]), ALU.mult))
                            V.drain().then_inc(rows_ready, 1)
                            split_rows(link, gate[:, :, :])

        with phase("vec", "norm_ready", "norm_root", "rows_ready", "table_in") as (block, vec, norm_ready, norm_root, rows_ready, table_in):
            @block.scalar
            def _(act):
                root(act, norm_ready, norm_root, 1)

            @block.sync
            def _(sp):
                sp.wait_ge(rows_ready, 1)
                sp.dma_start(table_nodes, state[:, :, :]).then_inc(table_in, 16)
                sp.wait_ge(table_in, 16)

            @block.vector
            def _(dve):
                link = chain(dve, vec)
                link(nc.vector.tensor_tensor(ends[:, :, :], state[:, :, :], rows[:, :, :], ALU.add))
                layer_norm(dve, link, norm_ready, norm_root, 1, state[:, :, :], ends[:, :, :])
                nc.vector.drain().then_inc(rows_ready, 1)

        PAIRS = -(-CT // 2)
        STEP = BANK // P
        STEPS = [(i, min(STEP, PAIRS - i)) for i in range(0, PAIRS, STEP)]
        NS = len(STEPS)
        with ExitStack() as own:
            w1 = sb("w1", [P, 2 * HID], F32, own)
            w2 = sb("w2", [P, 2 * HID], F32, own)
            w3 = sb("w3", [P, HID], F32, own)
            w4 = sb("w4", [P, 2 * D], F32, own)
            bias1 = sb("bias1", [P, 1], F32, own)
            bias2 = sb("bias2", [P, 1], F32, own)
            bias3 = sb("bias3", [P, 1], F32, own)
            bias4 = sb("bias4", [P, D], F32, own)
            message = [sb(f"message{i}", [P, 2 * PAIRS, 2 * D], F32, own) for i in range(2)]
            turned_in = [sb(f"turned_in{i}", [P, BANK], F32, own) for i in range(2)]
            act1 = [sb(f"act1_{i}", [P, BANK], F32, own) for i in range(2)]
            act2 = [sb(f"act2_{i}", [P, 2, BANK], F32, own) for i in range(2)]
            act3 = [sb(f"act3_{i}", [P, BANK], F32, own) for i in range(2)]
            ps0 = own.enter_context(nc.psum_tensor("ps0", [P, BANK], F32))
            ps1 = own.enter_context(nc.psum_tensor("ps1", [P, BANK], F32))
            ps2 = [own.enter_context(nc.psum_tensor(f"ps2_{i}", [P, BANK], F32)) for i in range(2)]
            ps3 = own.enter_context(nc.psum_tensor("ps3", [P, BANK], F32))
            ps4 = [own.enter_context(nc.psum_tensor(f"ps4_{i}", [P, BANK // D, D], F32)) for i in range(2)]
            with phase(*COMMON, "blank", "weights_in", "message_ready", "turns", "turned_moved", "mm1", "mm2", "mm3", "mm4",
                       "relu1", "relu2", "relu3", "masked") as (
                    block, chunk_in0, chunk_in1, used, vec, result_ready, staged_ready, stored0, stored1,
                    last_ready, last_turned, joined_ready, fix_in, fix_ready, ends_in_, rows_ready, table_in, norm_ready, norm_root,
                    blank, weights_in, message_ready, turns, turned_moved, mm1, mm2, mm3, mm4, relu1, relu2, relu3, masked):
                chunk_in, stored = (chunk_in0, chunk_in1), (stored0, stored1)
                LOADS = 2 * 5 + 2
                TOTAL = CHUNKS * NS

                def width(n):
                    return STEPS[n % NS][1] * P


                @block.sync
                def _(sp):
                    col = lambda v: v.rearrange("(n o) -> n o", o=1)
                    sp.wait_ge(blank, 1)
                    for a, half in enumerate((slice(0, HID), slice(HID, 2 * HID))):
                        sp.dma_start(w1[half, half], W1).then_inc(weights_in, 16)
                        sp.dma_start(w2[half, :], W2).then_inc(weights_in, 16)
                        sp.dma_start(w4[half, a * D:(a + 1) * D], W4).then_inc(weights_in, 16)
                        sp.dma_start(bias1[half, :], col(b1)).then_inc(weights_in, 16)
                        sp.dma_start(bias3[half, :], col(b3)).then_inc(weights_in, 16)
                    sp.dma_start(w3[:, :], W3).then_inc(weights_in, 16)
                    sp.dma_start(bias2[:, :], col(b2)).then_inc(weights_in, 16)
                    sp.dma_start(bias4[:, :], b4.partition_broadcast(P)).then_inc(table_in, 16)
                    for k in range(CHUNKS):
                        store_chunk(sp, k, staged_ready, stored)
                    sp.wait_ge(rows_ready, 1)
                    full = (N // P) * P
                    sp.dma_start(out[0:full, :].rearrange("(h p) c -> p h c", p=P), rows[:, 0:N // P, :]).then_inc(table_in, 16)
                    sp.dma_start(out[full:N, :], rows[0:N - full, HI - 1, :]).then_inc(table_in, 16)
                    sp.wait_ge(table_in, 48)

                @block.gpsimd
                def _(pool):
                    gather_chunks(pool, BY_DST, chunk_in, used, CT)
                    gather_ends(pool, BY_DST, scan_dram, stored, 16 * CHUNKS // 2, fix_in, fix_ready, ends_in_)

                @block.tensor
                def _(pe):
                    pe.wait_ge(weights_in, 16 * LOADS)

                    def turn(n):
                        k, (at, pairs) = n // NS, STEPS[n % NS]
                        pe.wait_ge(message_ready, k + 1)
                        if n:
                            pe.wait_ge(turned_moved, n)
                        for i in range(pairs):
                            last = nc.tensor.transpose(ps0[:, i * P:(i + 1) * P],
                                                       message[k % 2][:, 2 * (at + i):2 * (at + i) + 2, :].rearrange("p t c -> p (t c)"), identity[:, :])
                        last.then_inc(turns, 1)

                    halves = [slice(a * HID, (a + 1) * HID) for a in range(2)]
                    for i in range(TOTAL + 4):
                        if i < TOTAL:
                            turn(i)
                        n = i - 1
                        if 0 <= n < TOTAL:
                            w = width(n)
                            pe.wait_ge(turned_moved, n + 1)
                            if n:
                                pe.wait_ge(relu1, n)
                            nc.tensor.matmul(ps1[:, 0:w], w1[:, :], turned_in[n % 2][:, 0:w], start=True, stop=True).then_inc(mm1, 1)
                        n = i - 2
                        if 0 <= n < TOTAL:
                            w = width(n)
                            pe.wait_ge(relu1, n + 1)
                            for a, half in enumerate(halves):
                                if n:
                                    pe.wait_ge(relu2, 2 * (n - 1) + a + 1)
                                nc.tensor.matmul(ps2[a][:, 0:w], w2[half, :], act1[n % 2][half, 0:w], start=True, stop=True).then_inc(mm2, 1)
                        n = i - 3
                        if 0 <= n < TOTAL:
                            w = width(n)
                            if n:
                                pe.wait_ge(relu3, n)
                            for a, half in enumerate(halves):
                                pe.wait_ge(relu2, 2 * n + a + 1)
                                last = nc.tensor.matmul(ps3[half, 0:w], w3[:, :], act2[n % 2][:, a, 0:w], start=True, stop=True)
                            last.then_inc(mm3, 1)
                        n = i - 4
                        if n >= 0:
                            pe.wait_ge(relu3, n + 1)
                            if n >= 2:
                                pe.wait_ge(masked, n - 1)
                            for j in range(STEPS[n % NS][1]):
                                last = nc.tensor.matmul(ps4[n % 2][:, 2 * j:2 * j + 2, :].rearrange("p t c -> p (t c)"),
                                                        act3[n % 2][:, j * P:(j + 1) * P], w4[:, :], start=True, stop=True)
                            last.then_inc(mm4, 1)
                    turn_last(pe, ps0, last_ready, last_turned, joined_ready)

                @block.scalar
                def _(act):
                    act.wait_ge(weights_in, 16 * LOADS)
                    for i in range(TOTAL + 3):
                        n = i
                        if n < TOTAL:
                            act.wait_ge(turns, n + 1)
                            if n >= 2:
                                act.wait_ge(mm1, n - 1)
                            act.activation(turned_in[n % 2][:, 0:width(n)], ps0[:, 0:width(n)], ACT.Copy).then_inc(turned_moved, 1)
                        n = i - 1
                        if 0 <= n < TOTAL:
                            act.wait_ge(mm1, n + 1)
                            if n >= 2:
                                act.wait_ge(mm2, 2 * (n - 1))
                            act.activation(act1[n % 2][:, 0:width(n)], ps1[:, 0:width(n)], ACT.Relu, bias=bias1[:, :]).then_inc(relu1, 1)
                        n = i - 2
                        if 0 <= n < TOTAL:
                            for a in range(2):
                                act.wait_ge(mm2, 2 * n + a + 1)
                                if n >= 2:
                                    act.wait_ge(mm3, n - 1)
                                act.activation(act2[n % 2][:, a, 0:width(n)], ps2[a][:, 0:width(n)], ACT.Relu, bias=bias2[:, :]).then_inc(relu2, 1)
                        n = i - 3
                        if n >= 0:
                            act.wait_ge(mm3, n + 1)
                            if n >= 2:
                                act.wait_ge(mm4, n - 1)
                            act.activation(act3[n % 2][:, 0:width(n)], ps3[:, 0:width(n)], ACT.Relu, bias=bias3[:, :]).then_inc(relu3, 1)
                        if i % NS == NS - 1 and i >= NS:
                            stage_result(act, i // NS - 1, result_ready, stored, staged_ready)
                    stage_result(act, CHUNKS - 1, result_ready, stored, staged_ready)
                    root(act, norm_ready, norm_root, 1)

                @block.vector
                def _(dve):
                    link = chain(dve, vec)
                    V = nc.vector
                    V.memset(w1[:, :], 0.0)
                    link(V.memset(w4[:, :], 0.0))
                    V.drain().then_inc(blank, 1)
                    for i in range(2):
                        if CT % 2:
                            V.memset(message[i][:, CT:2 * PAIRS, :], 0.0)
                    for k in range(CHUNKS + 1):
                        if k < CHUNKS:
                            wait_rows(dve, k, chunk_in, CT)
                            spread_own_rows(link, k, BY_DST)
                            if k >= 2:
                                dve.wait_ge(turns, (k - 1) * NS)
                            own = own_row[k % 2][:, :, 1:CT + 1].rearrange("p c t -> p t c")
                            V.tensor_copy(message[k % 2][:, 0:CT, 0:D], own)
                            link(V.tensor_tensor(message[k % 2][:, 0:CT, D:2 * D], gathered[k % 2][:, :, :], own, ALU.subtract))
                            V.drain().then_inc(message_ready, 1)
                            V.drain().then_inc(used, 1)
                        if k:
                            c = k - 1
                            for s, (at, pairs) in enumerate(STEPS):
                                n = c * NS + s
                                cols = min(2 * pairs, CT - 2 * at)
                                lo = c * CT + 2 * at
                                dve.wait_ge(mm4, n + 1)
                                link(V.scalar_tensor_tensor(value[:, :, 1 + 2 * at:1 + 2 * at + cols],
                                                            starts[BY_DST][:, lo:lo + cols].unsqueeze(1).broadcast_to([P, D, cols]), 0.0,
                                                            ps4[n % 2][:, 0:cols, :].rearrange("p t c -> p c t"), ALU.is_equal, ALU.mult))
                                V.drain().then_inc(masked, 1)
                            scan_value(dve, link, c, BY_DST, ALU.add, staged_ready, result_ready)
                    keep_last(link, last_ready)
                    join_runs(dve, link, BY_DST, ALU.add, ps0, last_turned, joined_ready)
                    fix_ends(dve, link, ALU.add, ps0, last_turned, fix_in, fix_ready)
                    dve.wait_ge(ends_in_, 16 * HI)
                    dve.wait_ge(table_in, 16)
                    link(V.tensor_tensor(spare[:, :, :], degree[:, :].unsqueeze(2).broadcast_to([P, HI, D]),
                                         bias4[:, :].unsqueeze(1).broadcast_to([P, HI, D]), ALU.mult))
                    link(V.tensor_tensor(ends[:, :, :], ends[:, :, :], spare[:, :, :], ALU.add))
                    link(V.tensor_scalar(stat[:, 0, :], degree[:, :], 1.0, None, ALU.max))
                    link(V.reciprocal(stat[:, 1, :], stat[:, 0, :]))
                    link(V.tensor_tensor(ends[:, :, :], ends[:, :, :], stat[:, 1, :].unsqueeze(2).broadcast_to([P, HI, D]), ALU.mult))
                    link(V.tensor_tensor(ends[:, :, :], ends[:, :, :], state[:, :, :], ALU.add))
                    layer_norm(dve, link, norm_ready, norm_root, 1, rows[:, :, :], ends[:, :, :])
                    V.drain().then_inc(rows_ready, 1)


_INS = ["x", "src", "dst", "edge_weight", "L2_gnn_conv_w", "L2_gnn_conv_b", "L2_gnn_wc", "L2_gnn_bg",
        "L3_gnn_W1", "L3_gnn_b1", "L3_gnn_W2", "L3_gnn_b2", "L3_gnn_W3", "L3_gnn_b3", "L3_gnn_W4", "L3_gnn_b4"]


def kernel(**inputs):
    import numpy as _np
    import concourse.bacc as _bacc
    from concourse.bass_utils import run_bass_kernel_spmd as _run

    nc = _bacc.Bacc("TRN2", target_bir_lowering=False, num_devices=1)
    arrays, args = {}, []
    for name in _INS:
        a = _np.ascontiguousarray(inputs[name])
        arrays[f"in_{name}"] = a
        args.append(nc.dram_tensor(f"in_{name}", a.shape, mybir.dt.from_np(a.dtype), kind="ExternalInput").ap())
    args.append(nc.dram_tensor("out_rows", (N, D), F32, kind="ExternalOutput").ap())
    program(nc, *args)
    r = _run(nc, [arrays], core_ids=[0])
    return r.results[0]["out_rows"]
```

```python
from contextlib import ExitStack, contextmanager

import concourse.bass as bass
from concourse import mybir

F32, I32, U32, BF16 = mybir.dt.float32, mybir.dt.int32, mybir.dt.uint32, mybir.dt.bfloat16
I16, U8 = mybir.dt.int16, mybir.dt.uint8
ALU, ACT, AX = mybir.AluOpType, mybir.ActivationFunctionType, mybir.AxisListType

N, E, D = 3125, 100000, 32
P = 128
HI = -(-N // P)
NPAD = HI * P
RUN = -(-(N + E) // P)
DMA_TILES, HOT_TILES = 21, 16
CT = DMA_TILES + HOT_TILES
SETS = (DMA_TILES, DMA_TILES, DMA_TILES - HOT_TILES)
CHUNKS = -(-(RUN + 1) // CT)
COLS = CHUNKS * CT
HOT = HOT_TILES * P
BANK = 512
HOT_BANKS = HOT // BANK
RING, ACT_RING = 8, 3
ACT_BLOCKS = (8, 16, 24)
DVE_BLOCKS = tuple(b for b in range(HI) if b not in ACT_BLOCKS)
SPLIT = 3 * D
EP, EF = 125, 800
SORT = 1024
LOG_F, LOG_N = 10, 17
ID_BITS = 17
ID_MASK = (1 << ID_BITS) - 1
KEY_BIAS = 64
EPS = 1e-5
HID = 64
assert ACT_BLOCKS[-1] == HI - 1
assert EP * EF == E and HOT_TILES * D == BANK and HOT == HOT_BANKS * BANK


def program(nc, x, src, dst, edge_weight, conv_w, conv_b, wc, bg, W1, b1, W2, b2, W3, b3, W4, b4, out, debug=None):
    ctx = ExitStack()
    keys_dram = nc.dram_tensor("keys_dram", [2, P, SORT], I32, kind="Internal").ap()
    sorted_dram = nc.dram_tensor("sorted_dram", [2, P * SORT], I32, kind="Internal").ap()
    edges_dram = [nc.dram_tensor(f"edges_dram{o}", [E + 1, 2], I32, kind="Internal").ap() for o in range(2)]
    table_dram = nc.dram_tensor("table_dram", [NPAD, D], F32, kind="Internal").ap()
    scan_dram = nc.dram_tensor("scan_dram", [P * COLS, D], F32, kind="Internal").ap()
    scan_rows = scan_dram.rearrange("(p t) c -> p t c", p=P)
    degree_dram = nc.dram_tensor("degree_dram", [P * COLS, 1], F32, kind="Internal").ap()
    hot_index_dram = nc.dram_tensor("hot_index_dram", [len(SETS), CHUNKS * HOT_TILES, P], I16, kind="Internal").ap()
    table_nodes = table_dram.rearrange("(h p) c -> p h c", p=P)

    @contextmanager
    def phase(*names):
        with ExitStack() as own:
            sems = [own.enter_context(nc.semaphore(n)) for n in names]
            with nc.Block() as block:
                yield (block, *sems)
            nums = sorted(s.num for s in sems)
            first = nums[0]
            for num, after in zip(nums, nums[1:] + [None]):
                if after != num + 1:
                    nc.gpsimd.dma_reset(range(first, num + 1))
                    nc.all_engine_barrier(sems_to_clear=range(first, num + 1))
                    first = after

    def chain(engine, sem):
        count = [0]

        def link(instruction):
            count[0] += 1
            instruction.then_inc(sem, 1)
            engine.wait_ge(sem, count[0])
        return link

    with ctx:
        def sb(name, shape, dt=F32, stack=ctx):
            return stack.enter_context(nc.sbuf_tensor(name, shape, dt))

        gather_index = [sb(f"gather_index{o}", [P, COLS], U32) for o in range(2)]
        starts = [sb(f"starts{o}", [P, COLS]) for o in range(2)]
        inside = [sb(f"inside{o}", [P, CHUNKS, D, CT + 1], U8) for o in range(2)]
        end_row = [sb(f"end_row{o}", [P, HI], U32) for o in range(2)]
        fix_row = [sb(f"fix_row{o}", [P, 1], U32) for o in range(2)]
        whole = [sb(f"whole{o}", [D, P]) for o in range(2)]
        root_weight = sb("root_weight", [P, COLS])
        weight = sb("weight", [P, COLS])
        real = sb("real", [P, COLS])
        degree = sb("degree", [P, HI])
        inv_root = sb("inv_root", [P, HI])
        state = sb("state", [P, HI, D])
        rows = sb("rows", [P, HI, D])
        ends = sb("ends", [P, HI, D])
        spare = sb("spare", [P, HI, D])
        parts = sb("parts", [P, HI, 3, D], BF16)
        stat = sb("stat", [P, 4, HI])
        node_f = sb("node_f", [P, HI])
        minus_node = sb("minus_node", [P, HI])
        identity = sb("identity", [P, P])
        sum_parts = sb("sum_parts", [SPLIT, D], BF16)

        def split_rows(link, of):
            V = nc.vector
            link(V.tensor_copy(parts[:, :, 0, :], of))
            link(V.tensor_tensor(spare[:, :, :], of, parts[:, :, 0, :], ALU.subtract))
            link(V.tensor_copy(parts[:, :, 1, :], spare[:, :, :]))
            link(V.tensor_tensor(spare[:, :, :], spare[:, :, :], parts[:, :, 1, :], ALU.subtract))
            link(V.tensor_copy(parts[:, :, 2, :], spare[:, :, :]))

        with ExitStack() as own:
            src_in = sb("src_in", [P, EF], I32, own)
            dst_in = sb("dst_in", [P, EF], I32, own)
            w_in = sb("w_in", [P, EF], F32, own)
            edge_id = sb("edge_id", [P, EF], I32, own)
            node_id = sb("node_id", [P, HI], I32, own)
            keys = [sb(f"keys{o}", [P, SORT], I32, own) for o in range(2)]
            record = [sb(f"record{o}", [P, EF, 2], I32, own) for o in range(2)]
            blank = sb("blank", [1, 2], I32, own)
            with phase("loaded", "iota_done", "padded", "vec", "keyed", "x_cleared", "stored") as (
                    block, loaded, iota_done, padded, vec, keyed, x_cleared, stored):
                @block.sync
                def _(sp):
                    sp.dma_start(src_in[0:EP, :], src.rearrange("(p f) -> p f", p=EP)).then_inc(loaded, 16)
                    sp.dma_start(dst_in[0:EP, :], dst.rearrange("(p f) -> p f", p=EP)).then_inc(loaded, 16)
                    sp.dma_start(w_in[0:EP, :], edge_weight.rearrange("(p f) -> p f", p=EP)).then_inc(loaded, 16)
                    full = (N // P) * P
                    sp.wait_ge(x_cleared, 1)
                    sp.dma_start(state[:, 0:N // P, :], x[0:full, :].rearrange("(h p) c -> p h c", p=P)).then_inc(stored, 16)
                    sp.dma_start(state[0:N - full, HI - 1, :], x[full:N, :]).then_inc(stored, 16)
                    sp.wait_ge(stored, 32)
                    sp.dma_start(table_nodes, state[:, :, :]).then_inc(stored, 16)
                    sp.wait_ge(keyed, 1)
                    for o in range(2):
                        sp.dma_start(keys_dram[o, :, :], keys[o][:, :]).then_inc(stored, 16)
                        sp.dma_start(edges_dram[o][1:E + 1, :].rearrange("(p f) c -> p f c", p=EP), record[o][0:EP, :, :]).then_inc(stored, 16)
                        sp.dma_start(edges_dram[o][0:1, :], blank[:, :]).then_inc(stored, 16)
                    sp.wait_ge(stored, 16 * 9)

                @block.gpsimd
                def _(pool):
                    pool.iota(edge_id[:, :], [[1, EF]], base=1, channel_multiplier=EF).then_inc(iota_done, 1)
                    pool.iota(node_id[:, :], [[P, HI]], base=0, channel_multiplier=1).then_inc(iota_done, 1)
                    pool.memset(identity[:, :], 0.0).then_inc(padded, 1)
                    pool.wait_ge(padded, 1)
                    pool.affine_select(out=identity[:, :], in_=identity[:, :], compare_op=ALU.not_equal, fill=1.0,
                                       base=0, pattern=[[-1, P]], channel_multiplier=1).then_inc(padded, 1)
                    pool.wait_ge(padded, 2)

                @block.vector
                def _(dve):
                    link = chain(dve, vec)
                    nc.vector.memset(state[:, HI - 1, :], 0.0).then_inc(x_cleared, 1)
                    for o in range(2):
                        nc.vector.memset(keys[o][:, :], float((NPAD + KEY_BIAS) << ID_BITS))
                    link(nc.vector.memset(blank[:, :], 0))
                    dve.wait_ge(iota_done, 2)
                    dve.wait_ge(loaded, 48)
                    ends_of = (src_in, dst_in)
                    for o in range(2):
                        nc.vector.tensor_scalar(keys[o][:, EF:EF + HI], node_id[:, :], KEY_BIAS, None, ALU.add)
                        link(nc.vector.tensor_scalar(keys[o][0:EP, 0:EF], ends_of[o][0:EP, :], KEY_BIAS, None, ALU.add))
                    for o in range(2):
                        link(nc.vector.tensor_scalar(keys[o][:, EF:EF + HI], keys[o][:, EF:EF + HI], ID_BITS, None, ALU.logical_shift_left))
                        link(nc.vector.tensor_scalar(keys[o][0:EP, 0:EF], keys[o][0:EP, 0:EF], ID_BITS, None, ALU.logical_shift_left))
                    for o in range(2):
                        nc.vector.tensor_tensor(keys[o][0:EP, 0:EF], keys[o][0:EP, 0:EF], edge_id[0:EP, :], ALU.bitwise_or)
                    for o in range(2):
                        nc.vector.tensor_copy(record[o][0:EP, :, 0], ends_of[1 - o][0:EP, :])
                        link(nc.vector.tensor_copy(record[o][0:EP, :, 1].bitcast(F32), w_in[0:EP, :]))
                    nc.vector.drain().then_inc(keyed, 1)
                    dve.wait_ge(stored, 32)
                    split_rows(link, state[:, :, :])
                    dve.wait_ge(padded, 2)
                    for i in range(3):
                        link(nc.vector.tensor_copy(sum_parts[i * D:(i + 1) * D, :], identity[i * D:(i + 1) * D, i * D:(i + 1) * D]))

        own_node = (root_weight, weight)
        HOTS = CHUNKS * HOT_TILES
        HOT_PARTS = [(b, min(P, HOTS - b * P)) for b in range(-(-HOTS // P))]

        def gather_records(pool, o, at, to, got, got_done):
            for t in range(at, to):
                pool.indirect_dma_start(got[:, t, :], None, edges_dram[o],
                                        bass.IndirectOffsetOnAxis(ap=gather_index[o][:, t:t + 1], axis=0)).then_inc(got_done, 16)

        def read_records(dve, link, o, sets, got, tmp, tmp2, hot_cols, hot_rows, hot_t, cols_ready, cols_turned, index_ready):
            V = nc.vector
            link(V.memset(got[:, RUN + 1:COLS, :], 0))
            link(V.tensor_scalar(tmp2[:, :], starts[o][:, :], -1.0, 1.0, ALU.mult, ALU.add))
            link(V.tensor_copy(tmp[:, :], got[:, :, 0]))
            link(V.tensor_tensor(tmp[:, :], tmp[:, :], tmp2[:, :], ALU.mult))
            link(V.tensor_tensor(tmp[:, :], tmp[:, :], own_node[o][:, :], ALU.add))
            link(V.tensor_copy(gather_index[o][:, :], tmp[:, :]))
            for i, s in enumerate(sets):
                link(V.tensor_copy(hot_cols[:, i, :].rearrange("p (k i) -> p k i", i=HOT_TILES),
                                   tmp[:, :].rearrange("p (k t) -> p k t", t=CT)[:, :, SETS[s]:SETS[s] + HOT_TILES]))
            V.drain().then_inc(cols_ready, 1)
            dve.wait_ge(cols_turned, 1)
            for i, s in enumerate(sets):
                for b, n in HOT_PARTS:
                    link(V.tensor_copy(hot_rows[0:n, i, b, :], hot_t[i][0:n, b * P:(b + 1) * P]))
            V.drain().then_inc(index_ready, 1)

        def turn_hot_index(pe, count, hot_cols, hot_t, cols_ready, cols_turned):
            pe.wait_ge(cols_ready, 1)
            for i in range(count):
                for b, n in HOT_PARTS:
                    last = nc.tensor.transpose(hot_t[i][0:n, b * P:(b + 1) * P], hot_cols[:, i, b * P:b * P + n], identity[:, :])
            last.then_inc(cols_turned, 1)

        def store_hot_index(sp, sets, hot_rows, index_ready, index_out):
            sp.wait_ge(index_ready, 1)
            for i, s in enumerate(sets):
                for b, n in HOT_PARTS:
                    sp.dma_start(hot_index_dram[s, b * P:b * P + n, :], hot_rows[0:n, i, b, :]).then_inc(index_out, 16)
            sp.wait_ge(index_out, 16 * len(sets) * len(HOT_PARTS))

        with ExitStack() as own:
            ping = [sb(f"ping{i}", [P, SORT], F32, own) for i in range(2)]
            sign = sb("sign", [P, LOG_N - LOG_F], F32, own)
            bit = sb("bit", [P, LOG_N - LOG_F], I32, own)
            turned = own.enter_context(nc.psum_tensor("turned", [P, SORT], F32))
            with phase("iota_done", "vec") as (block, iota_done, vec):
                @block.gpsimd
                def _(pool):
                    pool.iota(bit[:, :], [[0, LOG_N - LOG_F]], base=0, channel_multiplier=1).then_inc(iota_done, 1)

                @block.vector
                def _(dve):
                    link = chain(dve, vec)
                    dve.wait_ge(iota_done, 1)
                    for m in range(LOG_N - LOG_F):
                        link(nc.vector.tensor_scalar(bit[:, m:m + 1], bit[:, m:m + 1], m, 1, ALU.logical_shift_right, ALU.bitwise_and))
                    link(nc.vector.tensor_scalar(sign[:, :], bit[:, :], -2.0, 1.0, ALU.mult, ALU.add))

            turns = 2 * (LOG_N - LOG_F)

            def sort_sync(sp, o, sort_in, turn_ready, keys_out):
                sp.dma_start(ping[0][:, :].bitcast(I32), keys_dram[o, :, :]).then_inc(sort_in, 16)
                sp.wait_ge(turn_ready, turns + 1)
                sp.dma_start(sorted_dram[o, :].rearrange("(p f) -> p f", p=P),
                             ping[0][:, :].bitcast(I32)).then_inc(keys_out, 16)
                sp.wait_ge(keys_out, 16)

            def sort_tensor(pe, turn_ready, turned_done, copied):
                for n in range(turns):
                    pe.wait_ge(turn_ready, n + 1)
                    if n:
                        pe.wait_ge(copied, n)
                    for b in range(SORT // P):
                        last = nc.tensor.transpose(turned[:, b * P:(b + 1) * P], ping[0][:, b * P:(b + 1) * P], identity[:, :])
                    last.then_inc(turned_done, 1)

            def sort_scalar(act, turned_done, copied):
                for n in range(turns):
                    act.wait_ge(turned_done, n + 1)
                    act.activation(ping[0][:, :], turned[:, :], ACT.Copy).then_inc(copied, 1)

            def sort_vector(dve, link, sort_in, turn_ready, copied):
                dve.wait_ge(sort_in, 16)
                at = [0]

                def stage(m):
                    a = ping[at[0]][:, :].rearrange("p (n s w) -> p n s w", s=2, w=1 << m)
                    z = ping[1 - at[0]][:, :].rearrange("p (n s w) -> p n s w", s=2, w=1 << m)
                    nc.vector.tensor_tensor(z[:, :, 0, :], a[:, :, 0, :], a[:, :, 1, :], ALU.min)
                    link(nc.vector.tensor_tensor(z[:, :, 1, :], a[:, :, 0, :], a[:, :, 1, :], ALU.max))
                    at[0] = 1 - at[0]

                def flip_columns(m):
                    v = ping[at[0]][:, :].rearrange("p (n s w) -> p n s w", s=2, w=1 << m)[:, :, 1, :]
                    link(nc.vector.tensor_scalar(v, v, -1.0, None, ALU.mult))

                def flip_partitions(m):
                    link(nc.vector.tensor_scalar(ping[at[0]][:, :], ping[at[0]][:, :], sign[:, m:m + 1], None, ALU.mult))

                def home():
                    if at[0]:
                        link(nc.vector.tensor_copy(ping[0][:, :], ping[1][:, :]))
                        at[0] = 0

                turn_count = [0]

                def turn():
                    home()
                    turn_count[0] += 1
                    nc.vector.drain().then_inc(turn_ready, 1)
                    dve.wait_ge(copied, turn_count[0])

                for k in range(1, LOG_N + 1):
                    if k < LOG_F:
                        flip_columns(k)
                    elif k == LOG_F:
                        flip_partitions(0)
                    else:
                        turn()
                        if k < LOG_N:
                            flip_columns(k - LOG_F)
                        for m in range(k - LOG_F - 1, -1, -1):
                            stage(m)
                        turn()
                    for m in range(min(k, LOG_F) - 1, -1, -1):
                        stage(m)
                    if k < LOG_F:
                        flip_columns(k)
                    elif k < LOG_N:
                        flip_partitions(k - LOG_F)
                home()
                nc.vector.drain().then_inc(turn_ready, 1)

            with phase("sort_in", "vec", "turn_ready", "turned_done", "copied", "keys_out") as (
                    block, sort_in, vec, turn_ready, turned_done, copied, keys_out):
                @block.sync
                def _(sp):
                    sort_sync(sp, 1, sort_in, turn_ready, keys_out)

                @block.tensor
                def _(pe):
                    sort_tensor(pe, turn_ready, turned_done, copied)

                @block.scalar
                def _(act):
                    sort_scalar(act, turned_done, copied)

                @block.vector
                def _(dve):
                    sort_vector(dve, chain(dve, vec), sort_in, turn_ready, copied)

            slot_key = [sb(f"slot_key{o}", [P, COLS], I32, own) for o in range(2)]
            slot_int = sb("slot_int", [P, COLS], I32, own)
            got = sb("got", [P, COLS, 2], I32, own)
            tmp = sb("tmp", [P, COLS], F32, own)
            tmp2 = sb("tmp2", [P, COLS], F32, own)
            hot_cols = sb("hot_cols", [P, 2, HOTS], F32, own)
            hot_rows = sb("hot_rows", [P, 2, len(HOT_PARTS), P], I16, own)
            ends_in = [sb(f"ends_in{o}", [P, EF], I32, own) for o in range(2)]
            low = sb("low", [P, EF], I32, own)
            high = sb("high", [P, EF], I32, own)
            low16 = sb("low16", [P, EF], BF16, own)
            high16 = sb("high16", [P, EF], BF16, own)
            EB = 20
            one_low = sb("one_low", [P, 2, EB, P], BF16, own)
            one_high = sb("one_high", [P, 2, EB, HI], BF16, own)
            ramp = sb("ramp", [P, P], F32, own)
            ramp16 = sb("ramp16", [P, P], BF16, own)
            slot_ramp = sb("slot_ramp", [P, COLS], F32, own)
            part_f = sb("part_f", [P, 1], F32, own)
            upto = sb("upto", [P, P], F32, own)
            ones = sb("ones", [P, P], F32, own)
            count = sb("count", [P, HI], F32, own)
            total = sb("total", [P, HI], F32, own)
            cum = sb("cum", [P, HI + 1], F32, own)
            last_at = sb("last_at", [P, HI], F32, own)
            t0 = sb("t0", [P, HI], F32, own)
            t1 = sb("t1", [P, HI], F32, own)
            run = sb("run", [P, HI], I32, own)
            first = sb("first", [P, 1], F32, own)
            full = sb("full", [P, 1], F32, own)
            f1 = sb("f1", [P, 1], F32, own)
            hist = own.enter_context(nc.psum_tensor("hist", [P, BANK], F32))
            sums = own.enter_context(nc.psum_tensor("sums", [P, BANK], F32))
            full_t = own.enter_context(nc.psum_tensor("full_t", [P, BANK], F32))
            hot_t = [own.enter_context(nc.psum_tensor(f"hot_t{i}", [P, BANK], F32)) for i in range(2)]
            with phase("sort_in", "turn_ready", "turned_done", "copied", "keys_out", "keys_in0", "keys_in1", "ends_loaded", "const_done", "vec",
                       "edge_ready", "hot_ready", "hot_used", "count_ready", "sums_done", "got_done", "full_ready", "full_turned",
                       "cols_ready", "cols_turned", "index_ready", "index_out") as (
                    block, sort_in, turn_ready, turned_done, copied, keys_out, keys_in0, keys_in1, ends_loaded, const_done, vec,
                    edge_ready, hot_ready, hot_used, count_ready, sums_done, got_done, full_ready, full_turned,
                    cols_ready, cols_turned, index_ready, index_out):
                steps = EF // EB

                @block.sync
                def _(sp):
                    def load_keys(o, keys_in):
                        sp.dma_start(slot_key[o][:, 1:RUN + 1], sorted_dram[o, 0:P * RUN].rearrange("(p t) -> p t", p=P)).then_inc(keys_in, 16)
                    load_keys(1, keys_in1)
                    sp.dma_start(ends_in[0][0:EP, :], src.rearrange("(p f) -> p f", p=EP)).then_inc(ends_loaded, 16)
                    sp.dma_start(ends_in[1][0:EP, :], dst.rearrange("(p f) -> p f", p=EP)).then_inc(ends_loaded, 16)
                    sort_sync(sp, 0, sort_in, turn_ready, keys_out)
                    load_keys(0, keys_in0)
                    store_hot_index(sp, (1, 2), hot_rows, index_ready, index_out)

                @block.gpsimd
                def _(pool):
                    pool.iota(ramp[:, :], [[1, P]], base=0, channel_multiplier=0,
                              allow_small_or_imprecise_dtypes=True).then_inc(const_done, 1)
                    pool.iota(node_f[:, :], [[P, HI]], base=0, channel_multiplier=1,
                              allow_small_or_imprecise_dtypes=True).then_inc(const_done, 1)
                    pool.iota(slot_ramp[:, :], [[1, COLS]], base=0, channel_multiplier=0,
                              allow_small_or_imprecise_dtypes=True).then_inc(const_done, 1)
                    pool.iota(part_f[:, :], [[0, 1]], base=0, channel_multiplier=1,
                              allow_small_or_imprecise_dtypes=True).then_inc(const_done, 1)
                    pool.memset(ones[:, :], 1.0).then_inc(const_done, 1)
                    pool.wait_ge(const_done, 5)
                    pool.affine_select(out=upto[:, :], in_=ones[:, :], compare_op=ALU.is_ge, fill=0.0,
                                       base=0, pattern=[[1, P]], channel_multiplier=-1).then_inc(const_done, 1)
                    pool.wait_ge(edge_ready, 1)
                    gather_records(pool, 1, 0, RUN + 1, got, got_done)
                    pool.wait_ge(got_done, 16 * (RUN + 1))

                @block.tensor
                def _(pe):
                    pe.wait_ge(const_done, 6)
                    for o in (1, 0):
                        pe.wait_ge(full_ready, 2 - o)
                        nc.tensor.transpose(full_t[0:D, o * P:(o + 1) * P], tmp[:, o * D:(o + 1) * D], identity[:, :]).then_inc(full_turned, 1)
                        if o:
                            sort_tensor(pe, turn_ready, turned_done, copied)
                    for o in range(2):
                        for s in range(steps):
                            n = o * steps + s
                            pe.wait_ge(hot_ready, n + 1)
                            if o and not s:
                                pe.wait_ge(count_ready, 1)
                            for f in range(EB):
                                last = nc.tensor.matmul(hist[:, 0:HI], one_low[0:EP, n % 2, f, :], one_high[0:EP, n % 2, f, :],
                                                        start=(s == 0 and f == 0), stop=(s == steps - 1 and f == EB - 1))
                            last.then_inc(hot_used, 1)
                        pe.wait_ge(count_ready, o + 1)
                        nc.tensor.matmul(sums[:, 0:HI], upto[:, :], count[:, :], start=True, stop=True)
                        nc.tensor.matmul(sums[:, HI:2 * HI], ones[:, :], count[:, :], start=True, stop=True).then_inc(sums_done, 1)
                    turn_hot_index(pe, 2, hot_cols, hot_t, cols_ready, cols_turned)

                @block.scalar
                def _(act):
                    sort_scalar(act, turned_done, copied)

                @block.vector
                def _(dve):
                    link = chain(dve, vec)
                    V = nc.vector
                    for o in range(2):
                        V.memset(slot_key[o][:, RUN + 1:COLS], 0)

                    def slots(o):
                        link(V.tensor_copy(slot_key[o][:, 0:1].bitcast(F32), slot_key[o][:, 1:2].bitcast(F32)))
                        link(V.tensor_scalar(gather_index[o][:, :], slot_key[o][:, :].bitcast(U32), ID_MASK, None, ALU.bitwise_and))
                        link(V.memset(gather_index[o][:, 0:1], 0))
                        V.drain().then_inc(edge_ready, 1)
                        if o:
                            dve.wait_ge(const_done, 6)
                        link(V.tensor_scalar(slot_int[:, :], slot_key[o][:, :], ID_BITS, None, ALU.logical_shift_right))
                        link(V.tensor_scalar(tmp[:, :], slot_int[:, :], -float(KEY_BIAS), float(NPAD - 1), ALU.add, ALU.min))
                        link(V.tensor_scalar(own_node[o][:, :], tmp[:, :], 0.0, None, ALU.max))
                        link(V.tensor_scalar(starts[o][:, :], gather_index[o][:, :], 0.0, None, ALU.is_equal))
                        link(V.memset(starts[o][:, RUN + 1:COLS], 0.0))
                        link(V.tensor_tensor(own_node[o][:, :], own_node[o][:, :], starts[o][:, :], ALU.mult))
                        link(V.tensor_scalar(tmp[:, :], starts[o][:, :], -4096.0, 4096.0, ALU.mult, ALU.add))
                        link(V.tensor_tensor(tmp[:, :], tmp[:, :], slot_ramp[:, :], ALU.add))
                        link(V.tensor_reduce(first[:, :], tmp[:, 1:RUN + 1], AX.X, ALU.min))
                        link(V.tensor_scalar(full[:, :], first[:, :], 4096.0, None, ALU.is_ge))
                        link(V.tensor_scalar(first[:, :], first[:, :], float(RUN + 1), -1.0, ALU.min, ALU.add))
                        link(V.tensor_scalar(f1[:, :], part_f[:, :], float(COLS), None, ALU.mult))
                        link(V.tensor_tensor(fix_row[o][:, :], f1[:, :], first[:, :], ALU.add))
                        link(V.tensor_copy(tmp[:, o * D:(o + 1) * D], full[:, 0:1].broadcast_to([P, D])))
                        V.drain().then_inc(full_ready, 1)
                        dve.wait_ge(full_turned, 2 - o)
                        link(V.tensor_copy(whole[o][:, :], full_t[0:D, o * P:(o + 1) * P]))

                    dve.wait_ge(keys_in1, 16)
                    slots(1)
                    link(V.tensor_scalar(minus_node[:, :], node_f[:, :], -1.0, None, ALU.mult))
                    sort_vector(dve, link, sort_in, turn_ready, copied)
                    dve.wait_ge(keys_in0, 16)
                    slots(0)
                    for o in range(2):
                        link(V.memset(inside[o][:, :, :, 0:1], 0))
                        link(V.tensor_scalar(tmp[:, :], starts[o][:, :], -1.0, 1.0, ALU.mult, ALU.add))
                        for k in range(CHUNKS):
                            link(V.tensor_copy(inside[o][:, k, :, 1:CT + 1], tmp[:, k * CT:(k + 1) * CT].unsqueeze(1).broadcast_to([P, D, CT])))
                    dve.wait_ge(ends_loaded, 32)
                    link(V.tensor_copy(ramp16[:, :], ramp[:, :]))
                    for o in range(2):
                        link(V.tensor_scalar(low[0:EP, :], ends_in[o][0:EP, :], P - 1, None, ALU.bitwise_and))
                        link(V.tensor_scalar(high[0:EP, :], ends_in[o][0:EP, :], 7, None, ALU.logical_shift_right))
                        V.tensor_copy(low16[0:EP, :], low[0:EP, :])
                        link(V.tensor_copy(high16[0:EP, :], high[0:EP, :]))
                        for s in range(steps):
                            n = o * steps + s
                            if n >= 2:
                                dve.wait_ge(hot_used, n - 1)
                            part = slice(s * EB, (s + 1) * EB)
                            V.tensor_tensor(one_low[0:EP, n % 2, :, :], low16[0:EP, part].unsqueeze(2).broadcast_to([EP, EB, P]),
                                            ramp16[0:EP, :].unsqueeze(1).broadcast_to([EP, EB, P]), ALU.is_equal)
                            link(V.tensor_tensor(one_high[0:EP, n % 2, :, :], high16[0:EP, part].unsqueeze(2).broadcast_to([EP, EB, HI]),
                                                 ramp16[0:EP, 0:HI].unsqueeze(1).broadcast_to([EP, EB, HI]), ALU.is_equal))
                            V.drain().then_inc(hot_ready, 1)
                        dve.wait_ge(hot_used, (o + 1) * steps)
                        link(V.tensor_copy(count[:, :], hist[:, 0:HI]))
                        V.drain().then_inc(count_ready, 1)
                        if o:
                            V.tensor_copy(degree[:, :], count[:, :])
                        dve.wait_ge(sums_done, o + 1)
                        link(V.tensor_copy(total[:, :], sums[:, HI:2 * HI]))
                        link(V.memset(cum[:, 0:1], 0.0))
                        link(V.memset(t0[:, :], 1.0))
                        link(V.tensor_tensor_scan(cum[:, 1:HI + 1], t0[:, :], total[:, :], 0.0, ALU.mult, ALU.add))
                        link(V.tensor_tensor(last_at[:, :], sums[:, 0:HI], cum[:, 0:HI], ALU.add))
                        link(V.tensor_tensor(last_at[:, :], last_at[:, :], node_f[:, :], ALU.add))
                        link(V.tensor_scalar(last_at[:, :], last_at[:, :], float(P * RUN - 1), None, ALU.min))
                        link(V.tensor_scalar(run[:, :], last_at[:, :], 1.0 / RUN, None, ALU.mult))
                        link(V.tensor_scalar(t0[:, :], run[:, :], -float(RUN), None, ALU.mult))
                        link(V.tensor_tensor(t0[:, :], t0[:, :], last_at[:, :], ALU.add))
                        link(V.tensor_scalar(t1[:, :], t0[:, :], 0.0, None, ALU.is_lt))
                        link(V.tensor_scalar(t0[:, :], t0[:, :], float(RUN), None, ALU.is_ge))
                        link(V.tensor_tensor(t0[:, :], t0[:, :], t1[:, :], ALU.subtract))
                        link(V.tensor_tensor(t0[:, :], t0[:, :], run[:, :], ALU.add))
                        link(V.tensor_scalar(t0[:, :], t0[:, :], float(COLS - RUN), 1.0, ALU.mult, ALU.add))
                        link(V.tensor_tensor(end_row[o][:, :], t0[:, :], last_at[:, :], ALU.add))
                    dve.wait_ge(got_done, 16 * (RUN + 1))
                    read_records(dve, link, 1, (1, 2), got, tmp, tmp2, hot_cols, hot_rows, hot_t, cols_ready, cols_turned, index_ready)
                    link(V.tensor_tensor(tmp[:, :], got[:, :, 1].bitcast(F32), tmp2[:, :], ALU.mult))
                    link(V.tensor_tensor(weight[:, :], tmp[:, :], starts[1][:, :], ALU.add))
                    link(V.memset(real[:, :], 1.0))
                    for part in (weight, real):
                        V.memset(part[:, 0:1], 0.0)
                        link(V.memset(part[:, RUN + 1:COLS], 0.0))

        gathered = [sb(f"gathered{i}", [P, CT, D]) for i in range(2)]
        staged = [sb(f"staged{i}", [P, CT, D]) for i in range(2)]
        own_row_space = sb("own_row_space", [P, 2 * D * (CT + 1)])
        own_row = [own_row_space[:, i * D * (CT + 1):(i + 1) * D * (CT + 1)].rearrange("p (c t) -> p c t", c=D) for i in range(2)]
        value = sb("value", [P, D, CT + 1])
        result = [sb(f"result{i}", [P, D, CT + 1]) for i in range(2)]
        last_row = sb("last_row", [P, D])
        last_t = sb("last_t", [D, 1 + P])
        fix = sb("fix", [P, D])
        BY_SRC, BY_DST = 0, 1
        LAST = RUN - (CHUNKS - 1) * CT

        def of_chunk(tile, k):
            return tile[:, k * CT:(k + 1) * CT]

        def over_channels(columns):
            return columns.unsqueeze(1).broadcast_to([P, D, CT])

        def layer_norm(dve, link, norm_ready, norm_root, count, to, of):
            V = nc.vector
            mean, var = stat[:, 0, :], stat[:, 1, :]
            link(V.tensor_reduce(mean, of, AX.X, ALU.add))
            link(V.tensor_scalar(mean, mean, 1.0 / D, None, ALU.mult))
            link(V.tensor_tensor(to, of, mean.unsqueeze(2).broadcast_to([P, HI, D]), ALU.subtract))
            link(V.tensor_tensor(spare[:, :, :], to, to, ALU.mult))
            link(V.tensor_reduce(var, spare[:, :, :], AX.X, ALU.add))
            link(V.tensor_scalar(var, var, 1.0 / D, EPS, ALU.mult, ALU.add))
            V.drain().then_inc(norm_ready, 1)
            dve.wait_ge(norm_root, count)
            link(V.reciprocal(stat[:, 3, :], stat[:, 2, :]))
            link(V.tensor_tensor(to, to, stat[:, 3, :].unsqueeze(2).broadcast_to([P, HI, D]), ALU.mult))

        def root(act, norm_ready, norm_root, count):
            act.wait_ge(norm_ready, count)
            act.activation(stat[:, 2, :], stat[:, 1, :], ACT.Sqrt).then_inc(norm_root, 1)

        def gather_chunk(pool, o, k, chunk_in, used, tiles):
            if k >= 2:
                pool.wait_ge(used, k - 1)
            for t in range(tiles):
                at = k * CT + t
                pool.indirect_dma_start(gathered[k % 2][:, t, :], None, table_dram,
                                        bass.IndirectOffsetOnAxis(ap=gather_index[o][:, at:at + 1], axis=0)).then_inc(chunk_in[k % 2], 16)

        def gather_chunks(pool, o, chunk_in, used, tiles):
            for k in range(CHUNKS):
                gather_chunk(pool, o, k, chunk_in, used, tiles)
            for i in range(2):
                pool.wait_ge(chunk_in[i], 16 * tiles * CHUNKS // 2)

        def hot_blocks(dve, k, part, index_rows, hot, hot_index_in, hot_ready, hot_used):
            dve.wait_ge(hot_index_in[k % 2], 16 * (k // 2 + 1))
            for i in part:
                n = k * len(DVE_BLOCKS) + i
                if n >= RING:
                    dve.wait_ge(hot_used, n - RING + 1)
                nc.vector.tensor_scalar(hot[n % RING][:, :], index_rows[k % 2][:, :], node_f[:, DVE_BLOCKS[i]:DVE_BLOCKS[i] + 1],
                                        None, ALU.is_equal).then_inc(hot_ready, 1)

        def act_hot_block(act, shares, n, index_rows, far, act_hot, hot_index_in, far_ready, act_hot_ready, act_hot_used, acc_done):
            k, i = divmod(n, len(ACT_BLOCKS))
            if k >= shares:
                return
            b = ACT_BLOCKS[i]
            act.wait_ge(hot_index_in[k % 2], 16 * (k // 2 + 1))
            if n >= 2:
                act.wait_ge(act_hot_ready, n - 1)
            act.activation(far[n % 2][:, :], index_rows[k % 2][:, :], ACT.Abs, bias=minus_node[:, b:b + 1]).then_inc(far_ready, 1)
            if n >= ACT_RING:
                k_was, i_was = divmod(n - ACT_RING, len(ACT_BLOCKS))
                if i_was == len(ACT_BLOCKS) - 1:
                    act.wait_ge(acc_done, (k_was + 1) * HOT_BANKS)
                else:
                    act.wait_ge(act_hot_used, k_was * (len(ACT_BLOCKS) - 1) + i_was + 1)
            act.wait_ge(far_ready, n + 1)
            act.activation(act_hot[n % ACT_RING][:, :], far[n % 2][:, :], ACT.Relu, bias=1.0, scale=-1.0).then_inc(act_hot_ready, 1)

        def load_hot_index(sp, sets, k, index_rows, hot_index_in, hot_ready, act_hot_ready):
            if k >= 2:
                sp.wait_ge(hot_ready, (k - 1) * len(DVE_BLOCKS))
                sp.wait_ge(act_hot_ready, (k - 1) * len(ACT_BLOCKS))
            c, u = divmod(k, len(sets))
            of = hot_index_dram[sets[u], c * HOT_TILES:(c + 1) * HOT_TILES, :].rearrange("i p -> (i p)")
            sp.dma_start(index_rows[k % 2][:, :], of.partition_broadcast(P)).then_inc(hot_index_in[k % 2], 16)

        def multiply_hot(pe, sets, hot, act_hot, acc, moved, summed, hot_ready, hot_used, act_hot_ready, act_hot_used, acc_done, acc_moved, sum_done, row_ready):
            def sum_up(k):
                for j in range(HOT_BANKS):
                    pe.wait_ge(acc_moved, k * HOT_BANKS + j + 1)
                    if k and not j:
                        pe.wait_ge(row_ready, k)
                    for i in range(BANK // P):
                        t = j * (BANK // P) + i
                        last = nc.tensor.matmul(summed[:, t * D:(t + 1) * D], moved[k % 2][:, t * P:(t + 1) * P], sum_parts[:, :], start=True, stop=True)
                last.then_inc(sum_done, 1)

            for k in range(len(sets) * CHUNKS):
                for b in range(HI):
                    if b == 6 and k:
                        sum_up(k - 1)
                    if b in ACT_BLOCKS:
                        n = k * len(ACT_BLOCKS) + ACT_BLOCKS.index(b)
                        pe.wait_ge(act_hot_ready, n + 1)
                        columns, columns_used = act_hot[n % ACT_RING], act_hot_used
                    else:
                        n = k * len(DVE_BLOCKS) + DVE_BLOCKS.index(b)
                        pe.wait_ge(hot_ready, n + 1)
                        columns, columns_used = hot[n % RING], hot_used
                    for j in range(HOT_BANKS):
                        m = k * HOT_BANKS + j
                        if not b and m >= len(acc):
                            pe.wait_ge(acc_moved, m - len(acc) + 1)
                        last = nc.tensor.matmul(acc[m % len(acc)][0:SPLIT, :], parts[:, b, :, :].rearrange("p s c -> p (s c)"),
                                                columns[:, j * BANK:(j + 1) * BANK], start=(b == 0), stop=(b == HI - 1))
                        if b == HI - 1:
                            last.then_inc(acc_done, 1)
                    if b < HI - 1:
                        last.then_inc(columns_used, 1)
            sum_up(len(sets) * CHUNKS - 1)

        def move_parts(act, k, acc, moved, acc_done, acc_moved, sum_done):
            for j in range(HOT_BANKS):
                m = k * HOT_BANKS + j
                act.wait_ge(acc_done, m + 1)
                if k >= 2 and not j:
                    act.wait_ge(sum_done, k - 1)
                act.activation(moved[k % 2][:, j * BANK:(j + 1) * BANK], acc[m % len(acc)][0:SPLIT, :], ACT.Copy).then_inc(acc_moved, 1)

        def move_rows(act, sets, k, summed, sum_done, used, row_ready):
            act.wait_ge(sum_done, k + 1)
            c, u = divmod(k, len(sets))
            if c >= 2:
                act.wait_ge(used, c - 1)
            act.activation(gathered[c % 2][:, SETS[sets[u]]:SETS[sets[u]] + HOT_TILES, :].rearrange("p t c -> p (t c)"), summed[:, :],
                           ACT.Copy).then_inc(row_ready, 1)

        def scalar_chunks(act, sets, index_rows, far, act_hot, hot_index_in, far_ready, act_hot_ready, act_hot_used, acc, moved, summed,
                          acc_done, acc_moved, sum_done, used, row_ready, result_ready, stored, staged_ready):
            def hot_block(n):
                act_hot_block(act, len(sets) * CHUNKS, n, index_rows, far, act_hot, hot_index_in, far_ready, act_hot_ready, act_hot_used, acc_done)
            count = len(ACT_BLOCKS)
            for n in range(ACT_RING):
                hot_block(n)
            for k in range(len(sets) * CHUNKS + 1):
                if k:
                    move_rows(act, sets, k - 1, summed, sum_done, used, row_ready)
                for n in range(k * count + ACT_RING, (k + 1) * count):
                    hot_block(n)
                c = (k - 1) // len(sets) - 1
                if c >= 0 and (k - 1) % len(sets) == 0:
                    stage_result(act, c, result_ready, stored, staged_ready)
                hot_block((k + 1) * count)
                hot_block((k + 1) * count + 1)
                if k < len(sets) * CHUNKS:
                    move_parts(act, k, acc, moved, acc_done, acc_moved, sum_done)
                hot_block((k + 1) * count + 2)
            stage_result(act, CHUNKS - 1, result_ready, stored, staged_ready)

        def stage_result(act, k, result_ready, stored, staged_ready):
            act.wait_ge(result_ready, k + 1)
            if k >= 2:
                act.wait_ge(stored[k % 2], 16 * (k // 2))
            act.activation(staged[k % 2][:, :, :], result[k % 2][:, :, 1:CT + 1].rearrange("p c t -> p t c"), ACT.Copy).then_inc(staged_ready, 1)

        def store_chunk(sp, k, staged_ready, stored):
            sp.wait_ge(staged_ready, k + 1)
            sp.dma_start(scan_rows[:, k * CT:(k + 1) * CT, :], staged[k % 2][:, :, :]).then_inc(stored[k % 2], 16)

        def turn_last(pe, turned, last_ready, last_turned, joined_ready, w=D):
            pe.wait_ge(last_ready, 1)
            nc.tensor.transpose(turned[0:w, 0:P], last_row[:, 0:w], identity[:, :]).then_inc(last_turned, 1)
            pe.wait_ge(joined_ready, 1)
            nc.tensor.transpose(turned[:, P:P + w], last_t[0:w, 0:P], identity[0:w, 0:w]).then_inc(last_turned, 1)

        def join_runs(dve, link, o, op, turned, last_turned, joined_ready, w=D):
            V = nc.vector
            link(V.memset(last_t[0:w, 0:1], 0.0))
            dve.wait_ge(last_turned, 1)
            link(V.tensor_tensor_scan(last_t[0:w, 1:P + 1], whole[o][0:w, :], turned[0:w, 0:P], 0.0, ALU.mult, op))
            V.drain().then_inc(joined_ready, 1)

        def fix_ends(dve, link, op, turned, last_turned, fix_in, fix_ready, w=D):
            dve.wait_ge(last_turned, 2)
            dve.wait_ge(fix_in, 16)
            link(nc.vector.tensor_tensor(fix[:, 0:w], fix[:, 0:w], turned[:, P:P + w], op))
            nc.vector.drain().then_inc(fix_ready, 1)

        def gather_ends(pool, o, table, stored, count, fix_in, fix_ready, ends_in_, w=D):
            for s in stored:
                pool.wait_ge(s, count)
            row = bass.IndirectOffsetOnAxis(ap=fix_row[o][:, :], axis=0)
            pool.indirect_dma_start(fix[:, 0:w], None, table, row).then_inc(fix_in, 16)
            pool.wait_ge(fix_ready, 1)
            pool.indirect_dma_start(table, row, fix[:, 0:w], None).then_inc(fix_in, 16)
            pool.wait_ge(fix_in, 32)
            for h in range(HI):
                pool.indirect_dma_start(ends[:, h, 0:w], None, table,
                                        bass.IndirectOffsetOnAxis(ap=end_row[o][:, h:h + 1], axis=0)).then_inc(ends_in_, 16)
            pool.wait_ge(ends_in_, 16 * HI)

        def carry(link, k, tile, before):
            if k:
                link(nc.vector.tensor_copy(tile[:, :, 0:1], before[:, :, CT:CT + 1]))
            else:
                link(nc.vector.memset(tile[:, :, 0:1], 0.0))

        def spread_own_rows(link, k, o):
            V = nc.vector
            carry(link, k, value, own_row[(k - 1) % 2])
            link(V.tensor_tensor(value[:, :, 1:CT + 1], gathered[k % 2][:, :, :].rearrange("p t c -> p c t"),
                                 over_channels(of_chunk(starts[o], k)), ALU.mult))
            link(V.tensor_tensor_scan(flat(own_row[k % 2]), inside_of(o, k), flat(value), 0.0, ALU.mult, ALU.add))

        def flat(tile):
            return tile[:, :, :].rearrange("p c t -> p (c t)")

        def inside_of(o, k):
            return inside[o][:, k, :, :].rearrange("p c t -> p (c t)")

        def scan_value(dve, link, k, o, op, staged_ready, result_ready):
            carry(link, k, value, result[(k - 1) % 2])
            if k >= 2:
                dve.wait_ge(staged_ready, k - 1)
            link(nc.vector.tensor_tensor_scan(flat(result[k % 2]), inside_of(o, k), flat(value), 0.0, ALU.mult, op))
            nc.vector.drain().then_inc(result_ready, 1)

        def keep_last(link, last_ready):
            link(nc.vector.tensor_copy(last_row[:, :], result[(CHUNKS - 1) % 2][:, :, 1 + LAST]))
            nc.vector.drain().then_inc(last_ready, 1)

        def wait_rows(dve, k, chunk_in, tiles, row_ready=None, shares=1):
            dve.wait_ge(chunk_in[k % 2], 16 * tiles * (k // 2 + 1))
            if row_ready is not None:
                dve.wait_ge(row_ready, (k + 1) * shares)

        COMMON = ("chunk_in0", "chunk_in1", "used", "vec", "result_ready", "staged_ready", "stored0", "stored1",
                  "last_ready", "last_turned", "joined_ready", "fix_in", "fix_ready", "ends_in",
                  "rows_ready", "table_in", "norm_ready", "norm_root")
        HOTS_ = ("hot_index_in0", "hot_index_in1", "hot_ready", "hot_used", "far_ready", "act_hot_ready", "act_hot_used",
                 "acc_done", "acc_moved", "sum_done", "row_ready")

        FIRST_PART, SECOND_PART = range(0, 12), range(12, len(DVE_BLOCKS))

        def sum_chunk(dve, link, k, factor, chunk_in, row_ready, used, tiles=DMA_TILES, shares=1):
            V = nc.vector
            wait_rows(dve, k, chunk_in, tiles, row_ready, shares)
            link(V.tensor_tensor(value[:, :, 1:CT + 1], gathered[k % 2][:, :, :].rearrange("p t c -> p c t"),
                                 over_channels(of_chunk(factor, k)), ALU.mult))
            V.drain().then_inc(used, 1)

        with ExitStack() as own:
            weight_sum = sb("weight_sum", [P, COLS], F32, own)
            keep = sb("keep", [P, COLS], F32, own)
            turned = own.enter_context(nc.psum_tensor("turned_d", [P, BANK], F32))
            with phase("vec", "sum_ready", "stored", "last_ready", "last_turned", "joined_ready", "fix_in", "fix_ready",
                       "ends_in", "norm_ready", "norm_root") as (
                    block, vec, sum_ready, stored, last_ready, last_turned, joined_ready, fix_in, fix_ready,
                    ends_in_, norm_ready, norm_root):
                @block.sync
                def _(sp):
                    sp.wait_ge(sum_ready, 1)
                    sp.dma_start(degree_dram.rearrange("(p t) c -> p (t c)", p=P), weight_sum[:, :]).then_inc(stored, 16)

                @block.gpsimd
                def _(pool):
                    gather_ends(pool, BY_DST, degree_dram, (stored,), 16, fix_in, fix_ready, ends_in_, w=1)

                @block.tensor
                def _(pe):
                    turn_last(pe, turned, last_ready, last_turned, joined_ready, w=1)

                @block.scalar
                def _(act):
                    root(act, norm_ready, norm_root, 1)

                @block.vector
                def _(dve):
                    link = chain(dve, vec)
                    V = nc.vector
                    link(V.tensor_scalar(keep[:, :], starts[BY_DST][:, :], -1.0, 1.0, ALU.mult, ALU.add))
                    link(V.tensor_tensor_scan(weight_sum[:, :], keep[:, :], weight[:, :], 0.0, ALU.mult, ALU.add))
                    V.drain().then_inc(sum_ready, 1)
                    link(V.tensor_copy(last_row[:, 0:1], weight_sum[:, RUN:RUN + 1]))
                    V.drain().then_inc(last_ready, 1)
                    join_runs(dve, link, BY_DST, ALU.add, turned, last_turned, joined_ready, w=1)
                    fix_ends(dve, link, ALU.add, turned, last_turned, fix_in, fix_ready, w=1)
                    dve.wait_ge(ends_in_, 16 * HI)
                    link(V.tensor_scalar(stat[:, 1, :], ends[:, :, 0], 1e-30, None, ALU.max))
                    V.drain().then_inc(norm_ready, 1)
                    dve.wait_ge(norm_root, 1)
                    link(V.reciprocal(stat[:, 3, :], stat[:, 2, :]))
                    link(V.tensor_scalar(stat[:, 0, :], ends[:, :, 0], 0.0, None, ALU.is_gt))
                    link(V.tensor_tensor(inv_root[:, :], stat[:, 3, :], stat[:, 0, :], ALU.mult))

        with ExitStack() as hots:
            index_rows = [sb(f"index_rows{i}", [P, HOT], I16, hots) for i in range(2)]
            hot_space = sb("hot_space", [P, RING * HOT], BF16, hots)
            hot = [hot_space[:, i * HOT:(i + 1) * HOT] for i in range(RING)]
            act_hot = [sb(f"act_hot{i}", [P, HOT], BF16, hots) for i in range(ACT_RING)]
            got_src = own_row_space[:, 0:2 * COLS].bitcast(I32).rearrange("p (t w) -> p t w", w=2)
            far = [sb(f"far{i}", [P, HOT], BF16, hots) for i in range(2)]
            moved = [sb(f"moved{i}", [SPLIT, HOT], BF16, hots) for i in range(2)]

            with ExitStack() as own:
                acc = [own.enter_context(nc.psum_tensor(f"acc0_{i}", [P, BANK], F32)) for i in range(7)]
                summed = own.enter_context(nc.psum_tensor("summed0", [P, BANK], F32))
                with phase(*COMMON, *HOTS_, "got_done") as (
                        block, chunk_in0, chunk_in1, used, vec, result_ready, staged_ready, stored0, stored1,
                        last_ready, last_turned, joined_ready, fix_in, fix_ready, ends_in_, rows_ready, table_in, norm_ready, norm_root,
                        hot_index_in0, hot_index_in1, hot_ready, hot_used, far_ready, act_hot_ready, act_hot_used, acc_done, acc_moved, sum_done, row_ready, got_done):
                    chunk_in, stored, hot_index_in = (chunk_in0, chunk_in1), (stored0, stored1), (hot_index_in0, hot_index_in1)

                    SHARES = (2, 1)

                    @block.sync
                    def _(sp):
                        for m in range(len(SHARES) * (CHUNKS + 2)):
                            if m < len(SHARES) * CHUNKS:
                                load_hot_index(sp, SHARES, m, index_rows, hot_index_in, hot_ready, act_hot_ready)
                            if m % len(SHARES) == 0 and m >= 2 * len(SHARES):
                                store_chunk(sp, m // len(SHARES) - 2, staged_ready, stored)
                        sp.wait_ge(rows_ready, 1)
                        sp.dma_start(table_nodes, state[:, :, :]).then_inc(table_in, 16)
                        sp.wait_ge(table_in, 16)

                    @block.gpsimd
                    def _(pool):
                        for k in range(CHUNKS):
                            gather_chunk(pool, BY_DST, k, chunk_in, used, SETS[2])
                            gather_records(pool, BY_SRC, k * CT, min((k + 1) * CT, RUN + 1), got_src, got_done)
                        for i in range(2):
                            pool.wait_ge(chunk_in[i], 16 * SETS[2] * CHUNKS // 2)
                        pool.wait_ge(got_done, 16 * (RUN + 1))
                        gather_ends(pool, BY_DST, scan_dram, stored, 16 * CHUNKS // 2, fix_in, fix_ready, ends_in_)

                    @block.tensor
                    def _(pe):
                        multiply_hot(pe, SHARES, hot, act_hot, acc, moved, summed, hot_ready, hot_used, act_hot_ready, act_hot_used, acc_done, acc_moved, sum_done, row_ready)
                        turn_last(pe, acc[0], last_ready, last_turned, joined_ready)

                    @block.scalar
                    def _(act):
                        scalar_chunks(act, SHARES, index_rows, far, act_hot, hot_index_in, far_ready, act_hot_ready, act_hot_used, acc, moved, summed,
                                      acc_done, acc_moved, sum_done, used, row_ready, result_ready, stored, staged_ready)
                        root(act, norm_ready, norm_root, 1)

                    @block.vector
                    def _(dve):
                        link = chain(dve, vec)
                        for m in range(len(SHARES) * CHUNKS + 1):
                            whole_chunk = m and m % len(SHARES) == 0
                            c = m // len(SHARES) - 1
                            if m < len(SHARES) * CHUNKS:
                                hot_blocks(dve, m, FIRST_PART, index_rows, hot, hot_index_in, hot_ready, hot_used)
                            if whole_chunk:
                                sum_chunk(dve, link, c, real, chunk_in, row_ready, used, SETS[2], len(SHARES))
                            if m < len(SHARES) * CHUNKS:
                                hot_blocks(dve, m, SECOND_PART, index_rows, hot, hot_index_in, hot_ready, hot_used)
                            if whole_chunk:
                                scan_value(dve, link, c, BY_DST, ALU.add, staged_ready, result_ready)
                        keep_last(link, last_ready)
                        join_runs(dve, link, BY_DST, ALU.add, acc[0], last_turned, joined_ready)
                        fix_ends(dve, link, ALU.add, acc[0], last_turned, fix_in, fix_ready)
                        dve.wait_ge(ends_in_, 16 * HI)
                        layer_norm(dve, link, norm_ready, norm_root, 1, state[:, :, :], ends[:, :, :])
                        link(nc.vector.tensor_copy(rows[:, :, :], state[:, :, :]))
                        nc.vector.drain().then_inc(rows_ready, 1)
                        split_rows(link, rows[:, :, :])

            with ExitStack() as own:
                hot_t = own.enter_context(nc.psum_tensor("hot_t_src", [P, BANK], F32))
                with phase("vec", "cols_ready", "cols_turned", "index_ready", "index_out", "root_ready", "root_done") as (
                        block, vec, cols_ready, cols_turned, index_ready, index_out, root_ready, root_done):
                    tmp, tmp2, hot_cols = [hot_space[:, i * 2 * COLS:(i + 1) * 2 * COLS].bitcast(F32) for i in range(3)]
                    hot_cols = hot_cols[:, 0:HOTS].rearrange("p (i n) -> p i n", i=1)
                    hot_rows = act_hot[0][:, 0:len(HOT_PARTS) * P].bitcast(I16).rearrange("p (i b n) -> p i b n", i=1, n=P)

                    @block.sync
                    def _(sp):
                        store_hot_index(sp, (0,), hot_rows, index_ready, index_out)

                    @block.tensor
                    def _(pe):
                        turn_hot_index(pe, 1, hot_cols, (hot_t,), cols_ready, cols_turned)

                    @block.scalar
                    def _(act):
                        act.wait_ge(root_ready, 1)
                        act.activation(tmp2, tmp2, ACT.Sqrt).then_inc(root_done, 1)

                    @block.vector
                    def _(dve):
                        link = chain(dve, vec)
                        V = nc.vector
                        read_records(dve, link, BY_SRC, (0,), got_src, tmp, tmp2, hot_cols, hot_rows, (hot_t,), cols_ready, cols_turned, index_ready)
                        w_got = got_src[:, :, 1].bitcast(F32)
                        link(V.tensor_scalar(tmp, w_got, 0.0, None, ALU.is_gt))
                        link(V.tensor_tensor(tmp, tmp, tmp2, ALU.mult))
                        link(V.tensor_scalar(tmp2, w_got, 1e-30, None, ALU.max))
                        V.drain().then_inc(root_ready, 1)
                        dve.wait_ge(root_done, 1)
                        link(V.tensor_tensor(root_weight[:, :], tmp2, tmp, ALU.mult))

            with ExitStack() as own:
                acc = [own.enter_context(nc.psum_tensor(f"acc1_{i}", [P, BANK], F32)) for i in range(7)]
                summed = own.enter_context(nc.psum_tensor("summed1", [P, BANK], F32))
                with nc.Fori(0, 10):
                    with phase(*COMMON, *HOTS_) as (
                            block, chunk_in0, chunk_in1, used, vec, result_ready, staged_ready, stored0, stored1,
                            last_ready, last_turned, joined_ready, fix_in, fix_ready, ends_in_, rows_ready, table_in, norm_ready, norm_root,
                            hot_index_in0, hot_index_in1, hot_ready, hot_used, far_ready, act_hot_ready, act_hot_used, acc_done, acc_moved, sum_done, row_ready):
                        chunk_in, stored, hot_index_in = (chunk_in0, chunk_in1), (stored0, stored1), (hot_index_in0, hot_index_in1)

                        @block.sync
                        def _(sp):
                            for k in range(CHUNKS + 2):
                                if k < CHUNKS:
                                    load_hot_index(sp, (0,), k, index_rows, hot_index_in, hot_ready, act_hot_ready)
                                if k >= 2:
                                    store_chunk(sp, k - 2, staged_ready, stored)
                            sp.wait_ge(rows_ready, 1)
                            sp.dma_start(table_nodes, rows[:, :, :]).then_inc(table_in, 16)
                            sp.wait_ge(table_in, 16)

                        @block.gpsimd
                        def _(pool):
                            gather_chunks(pool, BY_SRC, chunk_in, used, DMA_TILES)
                            gather_ends(pool, BY_SRC, scan_dram, stored, 16 * CHUNKS // 2, fix_in, fix_ready, ends_in_)

                        @block.tensor
                        def _(pe):
                            multiply_hot(pe, (0,), hot, act_hot, acc, moved, summed, hot_ready, hot_used, act_hot_ready, act_hot_used, acc_done, acc_moved, sum_done, row_ready)
                            turn_last(pe, acc[0], last_ready, last_turned, joined_ready)

                        @block.scalar
                        def _(act):
                            scalar_chunks(act, (0,), index_rows, far, act_hot, hot_index_in, far_ready, act_hot_ready, act_hot_used, acc, moved, summed,
                                          acc_done, acc_moved, sum_done, used, row_ready, result_ready, stored, staged_ready)

                        @block.vector
                        def _(dve):
                            link = chain(dve, vec)
                            V = nc.vector
                            for k in range(CHUNKS + 1):
                                if k < CHUNKS:
                                    hot_blocks(dve, k, FIRST_PART, index_rows, hot, hot_index_in, hot_ready, hot_used)
                                if k:
                                    c = k - 1
                                    wait_rows(dve, c, chunk_in, DMA_TILES, row_ready)
                                    spread_own_rows(link, c, BY_SRC)
                                    link(V.tensor_tensor(value[:, :, 1:CT + 1], gathered[c % 2][:, :, :].rearrange("p t c -> p c t"),
                                                         own_row[c % 2][:, :, 1:CT + 1], ALU.subtract))
                                    V.drain().then_inc(used, 1)
                                if k < CHUNKS:
                                    hot_blocks(dve, k, SECOND_PART, index_rows, hot, hot_index_in, hot_ready, hot_used)
                                if k:
                                    link(V.scalar_tensor_tensor(value[:, :, 1:CT + 1], value[:, :, 1:CT + 1], 0.0,
                                                                over_channels(of_chunk(root_weight, c)), ALU.max, ALU.mult))
                                    scan_value(dve, link, c, BY_SRC, ALU.max, staged_ready, result_ready)
                            keep_last(link, last_ready)
                            join_runs(dve, link, BY_SRC, ALU.max, acc[0], last_turned, joined_ready)
                            fix_ends(dve, link, ALU.max, acc[0], last_turned, fix_in, fix_ready)
                            dve.wait_ge(ends_in_, 16 * HI)
                            link(V.tensor_tensor(rows[:, :, :], rows[:, :, :], ends[:, :, :], ALU.add))
                            V.drain().then_inc(rows_ready, 1)
                            split_rows(link, rows[:, :, :])

            with phase("vec", "norm_ready", "norm_root", "rows_ready", "table_in") as (block, vec, norm_ready, norm_root, rows_ready, table_in):
                @block.scalar
                def _(act):
                    root(act, norm_ready, norm_root, 1)

                @block.sync
                def _(sp):
                    sp.wait_ge(rows_ready, 1)
                    sp.dma_start(table_nodes, rows[:, :, :]).then_inc(table_in, 16)
                    sp.wait_ge(table_in, 16)

                @block.vector
                def _(dve):
                    link = chain(dve, vec)
                    V = nc.vector
                    link(V.tensor_tensor(ends[:, :, :], state[:, :, :], rows[:, :, :], ALU.add))
                    layer_norm(dve, link, norm_ready, norm_root, 1, state[:, :, :], ends[:, :, :])
                    link(V.tensor_tensor(rows[:, :, :], state[:, :, :], inv_root[:, :].unsqueeze(2).broadcast_to([P, HI, D]), ALU.mult))
                    V.drain().then_inc(rows_ready, 1)
                    split_rows(link, rows[:, :, :])

            GATES = (0, 4, 6)
            GW = len(GATES) * D
            with ExitStack() as own:
                gate_w = sb("gate_w", [D + 1, 3, D], F32, own)
                bias_in = sb("bias_in", [D + 1, 3, GW], F32, own)
                peep = sb("peep", [P, D], F32, own)
                flat_t = hot_space[0:D + 1, 0:2 * NPAD].bitcast(F32)
                cell = spare
                gate = hot_space[:, 2 * NPAD:2 * (NPAD + HI * D)].bitcast(F32).rearrange("p (h c) -> p h c", c=D)
                psum = [own.enter_context(nc.psum_tensor(f"bank{i}", [P, BANK], F32)) for i in range(8)]
                acc, summed = psum[0:7], psum[7]
                with nc.Fori(0, 3) as layer:
                    with phase(*COMMON, *HOTS_, "weights_in", "bias_ready", "agg_ready", "agg_turned", "flat_ready", "gates_done", "act_done") as (
                            block, chunk_in0, chunk_in1, used, vec, result_ready, staged_ready, stored0, stored1,
                            last_ready, last_turned, joined_ready, fix_in, fix_ready, ends_in_, rows_ready, table_in, norm_ready, norm_root,
                            hot_index_in0, hot_index_in1, hot_ready, hot_used, far_ready, act_hot_ready, act_hot_used, acc_done, acc_moved, sum_done, row_ready,
                            weights_in, bias_ready, agg_ready, agg_turned, flat_ready, gates_done, act_done):
                        chunk_in, stored, hot_index_in = (chunk_in0, chunk_in1), (stored0, stored1), (hot_index_in0, hot_index_in1)
                        per_bank = 4
                        banks = -(-HI // per_bank)
                        per_gate = 5

                        @block.sync
                        def _(sp):
                            for i, g in enumerate(GATES):
                                sp.dma_start(gate_w[0:D, i, :], conv_w[bass.ds(layer, 1), g, :, :].rearrange("l k n -> (l k) n")).then_inc(weights_in, 16)
                                for r, gg in enumerate((g, g + 1)):
                                    sp.dma_start(bias_in[D:D + 1, r, i * D:(i + 1) * D], conv_b[bass.ds(layer, 1), gg, :]).then_inc(weights_in, 16)
                                sp.dma_start(bias_in[D:D + 1, 2, i * D:(i + 1) * D], bg[bass.ds(layer, 1), (0, 2, 3)[i], :]).then_inc(weights_in, 16)
                            sp.dma_start(peep[:, :], wc[bass.ds(layer, 1), 2, :].broadcast_to([P, D])).then_inc(weights_in, 16)
                            for k in range(CHUNKS + 2):
                                if k < CHUNKS:
                                    load_hot_index(sp, (1,), k, index_rows, hot_index_in, hot_ready, act_hot_ready)
                                if k >= 2:
                                    store_chunk(sp, k - 2, staged_ready, stored)
                            sp.wait_ge(rows_ready, 1)
                            sp.dma_start(table_nodes, gate[:, :, :]).then_inc(table_in, 16)
                            sp.wait_ge(table_in, 16)
                            sp.wait_ge(weights_in, 16 * 13)

                        @block.gpsimd
                        def _(pool):
                            gather_chunks(pool, BY_DST, chunk_in, used, DMA_TILES)
                            gather_ends(pool, BY_DST, scan_dram, stored, 16 * CHUNKS // 2, fix_in, fix_ready, ends_in_)

                        @block.tensor
                        def _(pe):
                            multiply_hot(pe, (1,), hot, act_hot, acc, moved, summed, hot_ready, hot_used, act_hot_ready, act_hot_used, acc_done, acc_moved, sum_done, row_ready)
                            turn_last(pe, acc[0], last_ready, last_turned, joined_ready)
                            pe.wait_ge(agg_ready, 1)
                            for h in range(HI):
                                last = nc.tensor.transpose(psum[h // per_bank][0:D, (h % per_bank) * P:(h % per_bank + 1) * P], ends[:, h, :], identity[:, :])
                            last.then_inc(agg_turned, 1)
                            pe.wait_ge(bias_ready, 1)
                            pe.wait_ge(flat_ready, banks)
                            for h in range(HI):
                                last = nc.tensor.matmul(psum[h // per_gate][:, (h % per_gate) * GW:(h % per_gate + 1) * GW],
                                                        flat_t[:, h * P:(h + 1) * P], gate_w[:, :, :].rearrange("k g n -> k (g n)"), start=True, stop=True)
                            last.then_inc(gates_done, 1)

                        @block.scalar
                        def _(act):
                            scalar_chunks(act, (1,), index_rows, far, act_hot, hot_index_in, far_ready, act_hot_ready, act_hot_used, acc, moved, summed,
                                          acc_done, acc_moved, sum_done, used, row_ready, result_ready, stored, staged_ready)
                            act.wait_ge(agg_turned, 1)
                            for b in range(banks):
                                n = min(per_bank, HI - b * per_bank) * P
                                act.activation(flat_t[0:D, b * per_bank * P:b * per_bank * P + n], psum[b][0:D, 0:n], ACT.Copy).then_inc(flat_ready, 1)
                            act.wait_ge(gates_done, 1)

                            def of_gate(i, b):
                                return psum[b][:, 0:per_gate * GW].rearrange("p (h n) -> p h n", n=GW)[:, :, i * D:(i + 1) * D]
                            for b in range(HI // per_gate):
                                cols = slice(b * per_gate, (b + 1) * per_gate)
                                act.activation(ends[:, cols, :], of_gate(0, b), ACT.Sigmoid).then_inc(act_done, 1)
                                act.activation(gate[:, cols, :], of_gate(1, b), ACT.Tanh).then_inc(act_done, 1)
                            act.wait_ge(norm_ready, 1)
                            act.activation(gate[:, :, :], gate[:, :, :], ACT.Sigmoid).then_inc(act_done, 1)
                            act.activation(cell[:, :, :], cell[:, :, :], ACT.Tanh).then_inc(act_done, 1)

                        @block.vector
                        def _(dve):
                            link = chain(dve, vec)
                            V = nc.vector
                            dve.wait_ge(weights_in, 16 * 13)
                            bias = gate_w[D:D + 1, :, :].rearrange("k g n -> k (g n)")
                            link(V.tensor_tensor(bias, bias_in[D:D + 1, 0, :], bias_in[D:D + 1, 1, :], ALU.add))
                            link(V.tensor_tensor(bias, bias, bias_in[D:D + 1, 2, :], ALU.add))
                            V.drain().then_inc(bias_ready, 1)
                            for k in range(CHUNKS + 1):
                                if k < CHUNKS:
                                    hot_blocks(dve, k, FIRST_PART, index_rows, hot, hot_index_in, hot_ready, hot_used)
                                if k:
                                    sum_chunk(dve, link, k - 1, weight, chunk_in, row_ready, used)
                                if k < CHUNKS:
                                    hot_blocks(dve, k, SECOND_PART, index_rows, hot, hot_index_in, hot_ready, hot_used)
                                if k:
                                    scan_value(dve, link, k - 1, BY_DST, ALU.add, staged_ready, result_ready)
                            keep_last(link, last_ready)
                            join_runs(dve, link, BY_DST, ALU.add, acc[0], last_turned, joined_ready)
                            fix_ends(dve, link, ALU.add, acc[0], last_turned, fix_in, fix_ready)
                            dve.wait_ge(ends_in_, 16 * HI)
                            link(V.tensor_tensor(ends[:, :, :], ends[:, :, :], inv_root[:, :].unsqueeze(2).broadcast_to([P, HI, D]), ALU.mult))
                            link(V.memset(flat_t[D:D + 1, :], 1.0))
                            V.drain().then_inc(agg_ready, 1)
                            gates = 2 * (HI // per_gate)
                            dve.wait_ge(act_done, gates)
                            link(V.tensor_tensor(cell[:, :, :], ends[:, :, :], gate[:, :, :], ALU.mult))
                            link(V.tensor_tensor(gate[:, :, :], cell[:, :, :], peep[:, :].unsqueeze(1).broadcast_to([P, HI, D]), ALU.mult))
                            for b in range(HI // per_gate):
                                cols = slice(b * per_gate, (b + 1) * per_gate)
                                link(V.tensor_tensor(gate[:, cols, :], gate[:, cols, :],
                                                     psum[b][:, 0:per_gate * GW].rearrange("p (h n) -> p h n", n=GW)[:, :, 2 * D:3 * D], ALU.add))
                            V.drain().then_inc(norm_ready, 1)
                            dve.wait_ge(act_done, gates + 2)
                            link(V.tensor_tensor(rows[:, :, :], gate[:, :, :], cell[:, :, :], ALU.mult))
                            link(V.tensor_tensor(gate[:, :, :], rows[:, :, :], inv_root[:, :].unsqueeze(2).broadcast_to([P, HI, D]), ALU.mult))
                            V.drain().then_inc(rows_ready, 1)
                            split_rows(link, gate[:, :, :])

        with phase("vec", "norm_ready", "norm_root", "rows_ready", "table_in") as (block, vec, norm_ready, norm_root, rows_ready, table_in):
            @block.scalar
            def _(act):
                root(act, norm_ready, norm_root, 1)

            @block.sync
            def _(sp):
                sp.wait_ge(rows_ready, 1)
                sp.dma_start(table_nodes, state[:, :, :]).then_inc(table_in, 16)
                sp.wait_ge(table_in, 16)

            @block.vector
            def _(dve):
                link = chain(dve, vec)
                link(nc.vector.tensor_tensor(ends[:, :, :], state[:, :, :], rows[:, :, :], ALU.add))
                layer_norm(dve, link, norm_ready, norm_root, 1, state[:, :, :], ends[:, :, :])
                nc.vector.drain().then_inc(rows_ready, 1)

        PAIRS = -(-CT // 2)
        STEP = BANK // P
        STEPS = [(i, min(STEP, PAIRS - i)) for i in range(0, PAIRS, STEP)]
        NS = len(STEPS)
        with ExitStack() as own:
            w1 = sb("w1", [P, 2 * HID], F32, own)
            w2 = sb("w2", [P, 2 * HID], F32, own)
            w3 = sb("w3", [P, HID], F32, own)
            w4 = sb("w4", [P, 2 * D], F32, own)
            bias1 = sb("bias1", [P, 1], F32, own)
            bias2 = sb("bias2", [P, 1], F32, own)
            bias3 = sb("bias3", [P, 1], F32, own)
            bias4 = sb("bias4", [P, D], F32, own)
            message = [sb(f"message{i}", [P, 2 * PAIRS, 2 * D], F32, own) for i in range(2)]
            turned_in = [sb(f"turned_in{i}", [P, BANK], F32, own) for i in range(2)]
            act1 = [sb(f"act1_{i}", [P, BANK], F32, own) for i in range(2)]
            act2 = [sb(f"act2_{i}", [P, 2, BANK], F32, own) for i in range(2)]
            act3 = [sb(f"act3_{i}", [P, BANK], F32, own) for i in range(2)]
            ps0 = own.enter_context(nc.psum_tensor("ps0", [P, BANK], F32))
            ps1 = own.enter_context(nc.psum_tensor("ps1", [P, BANK], F32))
            ps2 = [own.enter_context(nc.psum_tensor(f"ps2_{i}", [P, BANK], F32)) for i in range(2)]
            ps3 = own.enter_context(nc.psum_tensor("ps3", [P, BANK], F32))
            ps4 = [own.enter_context(nc.psum_tensor(f"ps4_{i}", [P, BANK // D, D], F32)) for i in range(2)]
            with phase(*COMMON, "blank", "weights_in", "message_ready", "turns", "turned_moved", "mm1", "mm2", "mm3", "mm4",
                       "relu1", "relu2", "relu3", "masked") as (
                    block, chunk_in0, chunk_in1, used, vec, result_ready, staged_ready, stored0, stored1,
                    last_ready, last_turned, joined_ready, fix_in, fix_ready, ends_in_, rows_ready, table_in, norm_ready, norm_root,
                    blank, weights_in, message_ready, turns, turned_moved, mm1, mm2, mm3, mm4, relu1, relu2, relu3, masked):
                chunk_in, stored = (chunk_in0, chunk_in1), (stored0, stored1)
                LOADS = 2 * 5 + 2
                TOTAL = CHUNKS * NS

                def width(n):
                    return STEPS[n % NS][1] * P


                @block.sync
                def _(sp):
                    col = lambda v: v.rearrange("(n o) -> n o", o=1)
                    sp.wait_ge(blank, 1)
                    for a, half in enumerate((slice(0, HID), slice(HID, 2 * HID))):
                        sp.dma_start(w1[half, half], W1).then_inc(weights_in, 16)
                        sp.dma_start(w2[half, :], W2).then_inc(weights_in, 16)
                        sp.dma_start(w4[half, a * D:(a + 1) * D], W4).then_inc(weights_in, 16)
                        sp.dma_start(bias1[half, :], col(b1)).then_inc(weights_in, 16)
                        sp.dma_start(bias3[half, :], col(b3)).then_inc(weights_in, 16)
                    sp.dma_start(w3[:, :], W3).then_inc(weights_in, 16)
                    sp.dma_start(bias2[:, :], col(b2)).then_inc(weights_in, 16)
                    sp.dma_start(bias4[:, :], b4.partition_broadcast(P)).then_inc(table_in, 16)
                    for k in range(CHUNKS):
                        store_chunk(sp, k, staged_ready, stored)
                    sp.wait_ge(rows_ready, 1)
                    full = (N // P) * P
                    sp.dma_start(out[0:full, :].rearrange("(h p) c -> p h c", p=P), rows[:, 0:N // P, :]).then_inc(table_in, 16)
                    sp.dma_start(out[full:N, :], rows[0:N - full, HI - 1, :]).then_inc(table_in, 16)
                    sp.wait_ge(table_in, 48)

                @block.gpsimd
                def _(pool):
                    gather_chunks(pool, BY_DST, chunk_in, used, CT)
                    gather_ends(pool, BY_DST, scan_dram, stored, 16 * CHUNKS // 2, fix_in, fix_ready, ends_in_)

                @block.tensor
                def _(pe):
                    pe.wait_ge(weights_in, 16 * LOADS)

                    def turn(n):
                        k, (at, pairs) = n // NS, STEPS[n % NS]
                        pe.wait_ge(message_ready, k + 1)
                        if n:
                            pe.wait_ge(turned_moved, n)
                        for i in range(pairs):
                            last = nc.tensor.transpose(ps0[:, i * P:(i + 1) * P],
                                                       message[k % 2][:, 2 * (at + i):2 * (at + i) + 2, :].rearrange("p t c -> p (t c)"), identity[:, :])
                        last.then_inc(turns, 1)

                    halves = [slice(a * HID, (a + 1) * HID) for a in range(2)]
                    for i in range(TOTAL + 4):
                        if i < TOTAL:
                            turn(i)
                        n = i - 1
                        if 0 <= n < TOTAL:
                            w = width(n)
                            pe.wait_ge(turned_moved, n + 1)
                            if n:
                                pe.wait_ge(relu1, n)
                            nc.tensor.matmul(ps1[:, 0:w], w1[:, :], turned_in[n % 2][:, 0:w], start=True, stop=True).then_inc(mm1, 1)
                        n = i - 2
                        if 0 <= n < TOTAL:
                            w = width(n)
                            pe.wait_ge(relu1, n + 1)
                            for a, half in enumerate(halves):
                                if n:
                                    pe.wait_ge(relu2, 2 * (n - 1) + a + 1)
                                nc.tensor.matmul(ps2[a][:, 0:w], w2[half, :], act1[n % 2][half, 0:w], start=True, stop=True).then_inc(mm2, 1)
                        n = i - 3
                        if 0 <= n < TOTAL:
                            w = width(n)
                            if n:
                                pe.wait_ge(relu3, n)
                            for a, half in enumerate(halves):
                                pe.wait_ge(relu2, 2 * n + a + 1)
                                last = nc.tensor.matmul(ps3[half, 0:w], w3[:, :], act2[n % 2][:, a, 0:w], start=True, stop=True)
                            last.then_inc(mm3, 1)
                        n = i - 4
                        if n >= 0:
                            pe.wait_ge(relu3, n + 1)
                            if n >= 2:
                                pe.wait_ge(masked, n - 1)
                            for j in range(STEPS[n % NS][1]):
                                last = nc.tensor.matmul(ps4[n % 2][:, 2 * j:2 * j + 2, :].rearrange("p t c -> p (t c)"),
                                                        act3[n % 2][:, j * P:(j + 1) * P], w4[:, :], start=True, stop=True)
                            last.then_inc(mm4, 1)
                    turn_last(pe, ps0, last_ready, last_turned, joined_ready)

                @block.scalar
                def _(act):
                    act.wait_ge(weights_in, 16 * LOADS)
                    for i in range(TOTAL + 3):
                        n = i
                        if n < TOTAL:
                            act.wait_ge(turns, n + 1)
                            if n >= 2:
                                act.wait_ge(mm1, n - 1)
                            act.activation(turned_in[n % 2][:, 0:width(n)], ps0[:, 0:width(n)], ACT.Copy).then_inc(turned_moved, 1)
                        n = i - 1
                        if 0 <= n < TOTAL:
                            act.wait_ge(mm1, n + 1)
                            if n >= 2:
                                act.wait_ge(mm2, 2 * (n - 1))
                            act.activation(act1[n % 2][:, 0:width(n)], ps1[:, 0:width(n)], ACT.Relu, bias=bias1[:, :]).then_inc(relu1, 1)
                        n = i - 2
                        if 0 <= n < TOTAL:
                            for a in range(2):
                                act.wait_ge(mm2, 2 * n + a + 1)
                                if n >= 2:
                                    act.wait_ge(mm3, n - 1)
                                act.activation(act2[n % 2][:, a, 0:width(n)], ps2[a][:, 0:width(n)], ACT.Relu, bias=bias2[:, :]).then_inc(relu2, 1)
                        n = i - 3
                        if n >= 0:
                            act.wait_ge(mm3, n + 1)
                            if n >= 2:
                                act.wait_ge(mm4, n - 1)
                            act.activation(act3[n % 2][:, 0:width(n)], ps3[:, 0:width(n)], ACT.Relu, bias=bias3[:, :]).then_inc(relu3, 1)
                        if i % NS == NS - 1 and i >= NS:
                            stage_result(act, i // NS - 1, result_ready, stored, staged_ready)
                    stage_result(act, CHUNKS - 1, result_ready, stored, staged_ready)
                    root(act, norm_ready, norm_root, 1)

                @block.vector
                def _(dve):
                    link = chain(dve, vec)
                    V = nc.vector
                    V.memset(w1[:, :], 0.0)
                    link(V.memset(w4[:, :], 0.0))
                    V.drain().then_inc(blank, 1)
                    for i in range(2):
                        if CT % 2:
                            V.memset(message[i][:, CT:2 * PAIRS, :], 0.0)
                    for k in range(CHUNKS + 1):
                        if k < CHUNKS:
                            wait_rows(dve, k, chunk_in, CT)
                            spread_own_rows(link, k, BY_DST)
                            if k >= 2:
                                dve.wait_ge(turns, (k - 1) * NS)
                            own = own_row[k % 2][:, :, 1:CT + 1].rearrange("p c t -> p t c")
                            V.tensor_copy(message[k % 2][:, 0:CT, 0:D], own)
                            link(V.tensor_tensor(message[k % 2][:, 0:CT, D:2 * D], gathered[k % 2][:, :, :], own, ALU.subtract))
                            V.drain().then_inc(message_ready, 1)
                            V.drain().then_inc(used, 1)
                        if k:
                            c = k - 1
                            for s, (at, pairs) in enumerate(STEPS):
                                n = c * NS + s
                                cols = min(2 * pairs, CT - 2 * at)
                                lo = c * CT + 2 * at
                                dve.wait_ge(mm4, n + 1)
                                link(V.scalar_tensor_tensor(value[:, :, 1 + 2 * at:1 + 2 * at + cols],
                                                            starts[BY_DST][:, lo:lo + cols].unsqueeze(1).broadcast_to([P, D, cols]), 0.0,
                                                            ps4[n % 2][:, 0:cols, :].rearrange("p t c -> p c t"), ALU.is_equal, ALU.mult))
                                V.drain().then_inc(masked, 1)
                            scan_value(dve, link, c, BY_DST, ALU.add, staged_ready, result_ready)
                    keep_last(link, last_ready)
                    join_runs(dve, link, BY_DST, ALU.add, ps0, last_turned, joined_ready)
                    fix_ends(dve, link, ALU.add, ps0, last_turned, fix_in, fix_ready)
                    dve.wait_ge(ends_in_, 16 * HI)
                    dve.wait_ge(table_in, 16)
                    link(V.tensor_tensor(spare[:, :, :], degree[:, :].unsqueeze(2).broadcast_to([P, HI, D]),
                                         bias4[:, :].unsqueeze(1).broadcast_to([P, HI, D]), ALU.mult))
                    link(V.tensor_tensor(ends[:, :, :], ends[:, :, :], spare[:, :, :], ALU.add))
                    link(V.tensor_scalar(stat[:, 0, :], degree[:, :], 1.0, None, ALU.max))
                    link(V.reciprocal(stat[:, 1, :], stat[:, 0, :]))
                    link(V.tensor_tensor(ends[:, :, :], ends[:, :, :], stat[:, 1, :].unsqueeze(2).broadcast_to([P, HI, D]), ALU.mult))
                    link(V.tensor_tensor(ends[:, :, :], ends[:, :, :], state[:, :, :], ALU.add))
                    layer_norm(dve, link, norm_ready, norm_root, 1, rows[:, :, :], ends[:, :, :])
                    V.drain().then_inc(rows_ready, 1)


_INS = ["x", "src", "dst", "edge_weight", "L2_gnn_conv_w", "L2_gnn_conv_b", "L2_gnn_wc", "L2_gnn_bg",
        "L3_gnn_W1", "L3_gnn_b1", "L3_gnn_W2", "L3_gnn_b2", "L3_gnn_W3", "L3_gnn_b3", "L3_gnn_W4", "L3_gnn_b4"]


def kernel(**inputs):
    import numpy as _np
    import concourse.bacc as _bacc
    from concourse.bass_utils import run_bass_kernel_spmd as _run

    nc = _bacc.Bacc("TRN2", target_bir_lowering=False, num_devices=1)
    arrays, args = {}, []
    for name in _INS:
        a = _np.ascontiguousarray(inputs[name])
        arrays[f"in_{name}"] = a
        args.append(nc.dram_tensor(f"in_{name}", a.shape, mybir.dt.from_np(a.dtype), kind="ExternalInput").ap())
    args.append(nc.dram_tensor("out_rows", (N, D), F32, kind="ExternalOutput").ap())
    program(nc, *args)
    r = _run(nc, [arrays], core_ids=[0])
    return r.results[0]["out_rows"]
```

```python
from contextlib import ExitStack, contextmanager

import concourse.bass as bass
from concourse import mybir

F32, I32, U32, BF16 = mybir.dt.float32, mybir.dt.int32, mybir.dt.uint32, mybir.dt.bfloat16
I16, U8 = mybir.dt.int16, mybir.dt.uint8
ALU, ACT, AX = mybir.AluOpType, mybir.ActivationFunctionType, mybir.AxisListType

N, E, D = 3125, 100000, 32
P = 128
HI = -(-N // P)
NPAD = HI * P
RUN = -(-(N + E) // P)
DMA_TILES, HOT_TILES = 21, 16
CT = DMA_TILES + HOT_TILES
SETS = (DMA_TILES, DMA_TILES, DMA_TILES - HOT_TILES)
CHUNKS = -(-(RUN + 1) // CT)
COLS = CHUNKS * CT
HOT = HOT_TILES * P
BANK = 512
HOT_BANKS = HOT // BANK
RING, ACT_RING = 8, 3
ACT_BLOCKS = (8, 16, 24)
DVE_BLOCKS = tuple(b for b in range(HI) if b not in ACT_BLOCKS)
SPLIT = 3 * D
EP, EF = 125, 800
SORT = 1024
LOG_F, LOG_N = 10, 17
ID_BITS = 17
ID_MASK = (1 << ID_BITS) - 1
KEY_BIAS = 64
EPS = 1e-5
HID = 64
assert ACT_BLOCKS[-1] == HI - 1 and CHUNKS % 2 == 0
assert EP * EF == E and HOT_TILES * D == BANK and HOT == HOT_BANKS * BANK


LAST_TILES = RUN + 1 - (CHUNKS - 1) * CT
LAST_BANKS = 2
LAST_HOT_END = DMA_TILES + LAST_BANKS * BANK // P


def banks_of(sets, k):
    return LAST_BANKS if k == len(sets) * CHUNKS - 1 else HOT_BANKS


ONE_SHARE, TWO_SHARES, MLP_SHARE = (SETS[1], CT), (SETS[2], CT), (SETS[1], SETS[1] + BANK // P)


def dma_columns(k, share):
    first, end = share
    if k < CHUNKS - 1:
        return [t for t in range(CT) if not first <= t < end]
    return [t for t in range(LAST_TILES) if not first <= t < min(end, LAST_HOT_END)]


def program(nc, x, src, dst, edge_weight, conv_w, conv_b, wc, bg, W1, b1, W2, b2, W3, b3, W4, b4, out):
    ctx = ExitStack()
    keys_dram = nc.dram_tensor("keys_dram", [2, P, SORT], I32, kind="Internal").ap()
    sorted_dram = nc.dram_tensor("sorted_dram", [2, P * SORT], I32, kind="Internal").ap()
    edges_dram = [nc.dram_tensor(f"edges_dram{o}", [E + 1, 2], I32, kind="Internal").ap() for o in range(2)]
    table_dram = nc.dram_tensor("table_dram", [NPAD, D], F32, kind="Internal").ap()
    scan_dram = nc.dram_tensor("scan_dram", [P * COLS, D], F32, kind="Internal").ap()
    scan_rows = scan_dram.rearrange("(p t) c -> p t c", p=P)
    hot_index_dram = nc.dram_tensor("hot_index_dram", [len(SETS), CHUNKS * HOT_TILES, P], I16, kind="Internal").ap()
    table_nodes = table_dram.rearrange("(h p) c -> p h c", p=P)

    @contextmanager
    def phase(*names):
        with ExitStack() as own:
            sems = [own.enter_context(nc.semaphore(n)) for n in names]
            with nc.Block() as block:
                yield (block, *sems)
            nums = sorted(s.num for s in sems)
            first = nums[0]
            for num, after in zip(nums, nums[1:] + [None]):
                if after != num + 1:
                    nc.gpsimd.dma_reset(range(first, num + 1))
                    nc.all_engine_barrier(sems_to_clear=range(first, num + 1))
                    first = after

    def chain(engine, sem):
        count = [0]

        def link(instruction):
            count[0] += 1
            instruction.then_inc(sem, 1)
            engine.wait_ge(sem, count[0])
        return link

    with ctx:
        def sb(name, shape, dt=F32, stack=ctx):
            return stack.enter_context(nc.sbuf_tensor(name, shape, dt))

        gather_index = [sb(f"gather_index{o}", [P, COLS], U32) for o in range(2)]
        starts = [sb(f"starts{o}", [P, COLS]) for o in range(2)]
        inside_space = [sb(f"inside{o}", [P, CHUNKS * D * (CT + 1)], U8) for o in range(2)]
        inside = [space[:, :].rearrange("p (k c t) -> p k c t", k=CHUNKS, c=D) for space in inside_space]
        end_row = [sb(f"end_row{o}", [P, HI], U32) for o in range(2)]
        fix_row = [sb(f"fix_row{o}", [P, 1], U32) for o in range(2)]
        whole = [sb(f"whole{o}", [D, P]) for o in range(2)]
        root_weight = sb("root_weight", [P, COLS])
        weight = sb("weight", [P, COLS])
        real = sb("real", [P, COLS])
        degree = sb("degree", [P, HI])
        inv_root = sb("inv_root", [P, HI])
        state = sb("state", [P, HI, D])
        rows = sb("rows", [P, HI, D])
        ends = sb("ends", [P, HI, D])
        spare = sb("spare", [P, HI, D])
        parts = sb("parts", [P, HI, 3, D], BF16)
        stat = sb("stat", [P, 4, HI])
        node_f = sb("node_f", [P, HI])
        minus_node = sb("minus_node", [P, HI])
        identity = sb("identity", [P, P])
        sum_parts = sb("sum_parts", [SPLIT, D], BF16)

        def split_rows(link, of, cols=slice(0, HI)):
            left, of = spare[:, cols, :], of[:, cols, :]
            V = nc.vector
            link(V.tensor_copy(parts[:, cols, 0, :], of))
            link(V.tensor_tensor(left, of, parts[:, cols, 0, :], ALU.subtract))
            link(V.tensor_copy(parts[:, cols, 1, :], left))
            link(V.tensor_tensor(left, left, parts[:, cols, 1, :], ALU.subtract))
            link(V.tensor_copy(parts[:, cols, 2, :], left))

        with ExitStack() as own:
            src_in = sb("src_in", [P, EF], I32, own)
            dst_in = sb("dst_in", [P, EF], I32, own)
            w_in = sb("w_in", [P, EF], F32, own)
            edge_id = sb("edge_id", [P, EF], I32, own)
            node_id = sb("node_id", [P, HI], I32, own)
            keys = [sb(f"keys{o}", [P, SORT], I32, own) for o in range(2)]
            record = [sb(f"record{o}", [P, EF, 2], I32, own) for o in range(2)]
            blank = sb("blank", [1, 2], I32, own)
            with phase("loaded", "iota_done", "padded", "vec", "keyed", "x_cleared", "stored") as (
                    block, loaded, iota_done, padded, vec, keyed, x_cleared, stored):
                @block.sync
                def _(sp):
                    sp.dma_start(src_in[0:EP, :], src.rearrange("(p f) -> p f", p=EP)).then_inc(loaded, 16)
                    sp.dma_start(dst_in[0:EP, :], dst.rearrange("(p f) -> p f", p=EP)).then_inc(loaded, 16)
                    sp.dma_start(w_in[0:EP, :], edge_weight.rearrange("(p f) -> p f", p=EP)).then_inc(loaded, 16)
                    full = (N // P) * P
                    sp.wait_ge(x_cleared, 1)
                    sp.dma_start(state[:, 0:N // P, :], x[0:full, :].rearrange("(h p) c -> p h c", p=P)).then_inc(stored, 16)
                    sp.dma_start(state[0:N - full, HI - 1, :], x[full:N, :]).then_inc(stored, 16)
                    sp.wait_ge(stored, 32)
                    sp.dma_start(table_nodes, state[:, :, :]).then_inc(stored, 16)
                    sp.wait_ge(keyed, 1)
                    for o in range(2):
                        sp.dma_start(keys_dram[o, :, :], keys[o][:, :]).then_inc(stored, 16)
                        sp.dma_start(edges_dram[o][1:E + 1, :].rearrange("(p f) c -> p f c", p=EP), record[o][0:EP, :, :]).then_inc(stored, 16)
                        sp.dma_start(edges_dram[o][0:1, :], blank[:, :]).then_inc(stored, 16)
                    sp.wait_ge(stored, 16 * 9)

                @block.gpsimd
                def _(pool):
                    pool.iota(edge_id[:, :], [[1, EF]], base=1, channel_multiplier=EF).then_inc(iota_done, 1)
                    pool.iota(node_id[:, :], [[P, HI]], base=0, channel_multiplier=1).then_inc(iota_done, 1)
                    pool.memset(identity[:, :], 0.0).then_inc(padded, 1)
                    pool.wait_ge(padded, 1)
                    pool.affine_select(out=identity[:, :], in_=identity[:, :], compare_op=ALU.not_equal, fill=1.0,
                                       base=0, pattern=[[-1, P]], channel_multiplier=1).then_inc(padded, 1)
                    pool.wait_ge(padded, 2)

                @block.vector
                def _(dve):
                    link = chain(dve, vec)
                    nc.vector.memset(state[:, HI - 1, :], 0.0).then_inc(x_cleared, 1)
                    for o in range(2):
                        nc.vector.memset(keys[o][:, :], float((NPAD + KEY_BIAS) << ID_BITS))
                    link(nc.vector.memset(blank[:, :], 0))
                    dve.wait_ge(iota_done, 2)
                    dve.wait_ge(loaded, 48)
                    ends_of = (src_in, dst_in)
                    for o in range(2):
                        nc.vector.tensor_scalar(keys[o][:, EF:EF + HI], node_id[:, :], KEY_BIAS, None, ALU.add)
                        link(nc.vector.tensor_scalar(keys[o][0:EP, 0:EF], ends_of[o][0:EP, :], KEY_BIAS, None, ALU.add))
                    for o in range(2):
                        link(nc.vector.tensor_scalar(keys[o][:, EF:EF + HI], keys[o][:, EF:EF + HI], ID_BITS, None, ALU.logical_shift_left))
                        link(nc.vector.tensor_scalar(keys[o][0:EP, 0:EF], keys[o][0:EP, 0:EF], ID_BITS, None, ALU.logical_shift_left))
                    for o in range(2):
                        nc.vector.tensor_tensor(keys[o][0:EP, 0:EF], keys[o][0:EP, 0:EF], edge_id[0:EP, :], ALU.bitwise_or)
                    for o in range(2):
                        nc.vector.tensor_copy(record[o][0:EP, :, 0], ends_of[1 - o][0:EP, :])
                        link(nc.vector.tensor_copy(record[o][0:EP, :, 1].bitcast(F32), w_in[0:EP, :]))
                    nc.vector.drain().then_inc(keyed, 1)
                    dve.wait_ge(stored, 32)
                    split_rows(link, state[:, :, :])
                    dve.wait_ge(padded, 2)
                    for i in range(3):
                        link(nc.vector.tensor_copy(sum_parts[i * D:(i + 1) * D, :], identity[i * D:(i + 1) * D, i * D:(i + 1) * D]))

        own_node = (root_weight, weight)
        HOTS = CHUNKS * HOT_TILES
        HOT_PARTS = [(b, min(P, HOTS - b * P)) for b in range(-(-HOTS // P))]

        def gather_records(pool, o, at, to, got, got_done):
            for t in range(at, to):
                pool.indirect_dma_start(got[:, t, :], None, edges_dram[o],
                                        bass.IndirectOffsetOnAxis(ap=gather_index[o][:, t:t + 1], axis=0)).then_inc(got_done, 16)

        def read_records(dve, link, o, sets, got, tmp, tmp2, hot_cols, hot_rows, hot_t, cols_ready, cols_turned, index_ready):
            V = nc.vector
            link(V.memset(got[:, RUN + 1:COLS, :], 0))
            link(V.tensor_scalar(tmp2[:, :], starts[o][:, :], -1.0, 1.0, ALU.mult, ALU.add))
            link(V.tensor_copy(tmp[:, :], got[:, :, 0]))
            link(V.tensor_tensor(tmp[:, :], tmp[:, :], tmp2[:, :], ALU.mult))
            link(V.tensor_tensor(tmp[:, :], tmp[:, :], own_node[o][:, :], ALU.add))
            link(V.tensor_copy(gather_index[o][:, :], tmp[:, :]))
            for i, s in enumerate(sets):
                link(V.tensor_copy(hot_cols[:, i, :].rearrange("p (k i) -> p k i", i=HOT_TILES),
                                   tmp[:, :].rearrange("p (k t) -> p k t", t=CT)[:, :, SETS[s]:SETS[s] + HOT_TILES]))
            V.drain().then_inc(cols_ready, 1)
            dve.wait_ge(cols_turned, 1)
            for i, s in enumerate(sets):
                for b, n in HOT_PARTS:
                    link(V.tensor_copy(hot_rows[0:n, i, b, :], hot_t[i][0:n, b * P:(b + 1) * P]))
            V.drain().then_inc(index_ready, 1)

        def turn_hot_index(pe, count, hot_cols, hot_t, cols_ready, cols_turned):
            pe.wait_ge(cols_ready, 1)
            for i in range(count):
                for b, n in HOT_PARTS:
                    last = nc.tensor.transpose(hot_t[i][0:n, b * P:(b + 1) * P], hot_cols[:, i, b * P:b * P + n], identity[:, :])
            last.then_inc(cols_turned, 1)

        def store_hot_index(sp, sets, hot_rows, index_ready, index_out):
            sp.wait_ge(index_ready, 1)
            for i, s in enumerate(sets):
                for b, n in HOT_PARTS:
                    sp.dma_start(hot_index_dram[s, b * P:b * P + n, :], hot_rows[0:n, i, b, :]).then_inc(index_out, 16)
            sp.wait_ge(index_out, 16 * len(sets) * len(HOT_PARTS))

        with ExitStack() as own:
            ping = [sb(f"ping{i}", [P, SORT], F32, own) for i in range(2)]
            sign = sb("sign", [P, LOG_N - LOG_F], F32, own)
            bit = sb("bit", [P, LOG_N - LOG_F], I32, own)
            turned = own.enter_context(nc.psum_tensor("turned", [P, SORT], F32))
            with phase("iota_done", "vec") as (block, iota_done, vec):
                @block.gpsimd
                def _(pool):
                    pool.iota(bit[:, :], [[0, LOG_N - LOG_F]], base=0, channel_multiplier=1).then_inc(iota_done, 1)

                @block.vector
                def _(dve):
                    link = chain(dve, vec)
                    dve.wait_ge(iota_done, 1)
                    for m in range(LOG_N - LOG_F):
                        link(nc.vector.tensor_scalar(bit[:, m:m + 1], bit[:, m:m + 1], m, 1, ALU.logical_shift_right, ALU.bitwise_and))
                    link(nc.vector.tensor_scalar(sign[:, :], bit[:, :], -2.0, 1.0, ALU.mult, ALU.add))

            turns = 2 * (LOG_N - LOG_F)

            def sort_sync(sp, o, sort_in, turn_ready, keys_out):
                sp.dma_start(ping[0][:, :].bitcast(I32), keys_dram[o, :, :]).then_inc(sort_in, 16)
                sp.wait_ge(turn_ready, turns + 1)
                sp.dma_start(sorted_dram[o, :].rearrange("(p f) -> p f", p=P),
                             ping[0][:, :].bitcast(I32)).then_inc(keys_out, 16)
                sp.wait_ge(keys_out, 16)

            def sort_tensor(pe, turn_ready, turned_done, copied):
                for n in range(turns):
                    pe.wait_ge(turn_ready, n + 1)
                    if n:
                        pe.wait_ge(copied, n)
                    for b in range(SORT // P):
                        last = nc.tensor.transpose(turned[:, b * P:(b + 1) * P], ping[0][:, b * P:(b + 1) * P], identity[:, :])
                    last.then_inc(turned_done, 1)

            def sort_scalar(act, turned_done, copied):
                for n in range(turns):
                    act.wait_ge(turned_done, n + 1)
                    act.activation(ping[0][:, :], turned[:, :], ACT.Copy).then_inc(copied, 1)

            def sort_vector(dve, link, sort_in, turn_ready, copied):
                dve.wait_ge(sort_in, 16)
                at = [0]

                def stage(m):
                    a = ping[at[0]][:, :].rearrange("p (n s w) -> p n s w", s=2, w=1 << m)
                    z = ping[1 - at[0]][:, :].rearrange("p (n s w) -> p n s w", s=2, w=1 << m)
                    nc.vector.tensor_tensor(z[:, :, 0, :], a[:, :, 0, :], a[:, :, 1, :], ALU.min)
                    link(nc.vector.tensor_tensor(z[:, :, 1, :], a[:, :, 0, :], a[:, :, 1, :], ALU.max))
                    at[0] = 1 - at[0]

                def flip_columns(m):
                    v = ping[at[0]][:, :].rearrange("p (n s w) -> p n s w", s=2, w=1 << m)[:, :, 1, :]
                    link(nc.vector.tensor_scalar(v, v, -1.0, None, ALU.mult))

                def flip_partitions(m):
                    link(nc.vector.tensor_scalar(ping[at[0]][:, :], ping[at[0]][:, :], sign[:, m:m + 1], None, ALU.mult))

                def home():
                    if at[0]:
                        link(nc.vector.tensor_copy(ping[0][:, :], ping[1][:, :]))
                        at[0] = 0

                turn_count = [0]

                def turn():
                    home()
                    turn_count[0] += 1
                    nc.vector.drain().then_inc(turn_ready, 1)
                    dve.wait_ge(copied, turn_count[0])

                for k in range(1, LOG_N + 1):
                    if k < LOG_F:
                        flip_columns(k)
                    elif k == LOG_F:
                        flip_partitions(0)
                    else:
                        turn()
                        if k < LOG_N:
                            flip_columns(k - LOG_F)
                        for m in range(k - LOG_F - 1, -1, -1):
                            stage(m)
                        turn()
                    for m in range(min(k, LOG_F) - 1, -1, -1):
                        stage(m)
                    if k < LOG_F:
                        flip_columns(k)
                    elif k < LOG_N:
                        flip_partitions(k - LOG_F)
                home()
                nc.vector.drain().then_inc(turn_ready, 1)

            with phase("sort_in", "vec", "turn_ready", "turned_done", "copied", "keys_out") as (
                    block, sort_in, vec, turn_ready, turned_done, copied, keys_out):
                @block.sync
                def _(sp):
                    sort_sync(sp, 1, sort_in, turn_ready, keys_out)

                @block.tensor
                def _(pe):
                    sort_tensor(pe, turn_ready, turned_done, copied)

                @block.scalar
                def _(act):
                    sort_scalar(act, turned_done, copied)

                @block.vector
                def _(dve):
                    sort_vector(dve, chain(dve, vec), sort_in, turn_ready, copied)

            slot_key = [sb(f"slot_key{o}", [P, COLS], I32, own) for o in range(2)]
            slot_int = sb("slot_int", [P, COLS], I32, own)
            got = sb("got", [P, COLS, 2], I32, own)
            tmp = sb("tmp", [P, COLS], F32, own)
            tmp2 = sb("tmp2", [P, COLS], F32, own)
            hot_cols = sb("hot_cols", [P, 2, HOTS], F32, own)
            hot_rows = sb("hot_rows", [P, 2, len(HOT_PARTS), P], I16, own)
            ends_in = [sb(f"ends_in{o}", [P, EF], I32, own) for o in range(2)]
            low = sb("low", [P, EF], I32, own)
            high = sb("high", [P, EF], I32, own)
            low16 = sb("low16", [P, EF], BF16, own)
            high16 = sb("high16", [P, EF], BF16, own)
            EB = 20
            one_low = sb("one_low", [P, 2, EB, P], BF16, own)
            one_high = sb("one_high", [P, 2, EB, 4, HI], BF16, own)
            w_in = sb("w_in_order", [P, EF], F32, own)
            w_parts = sb("w_parts", [P, 3, EF], BF16, own)
            ramp = sb("ramp", [P, P], F32, own)
            ramp16 = sb("ramp16", [P, P], BF16, own)
            slot_ramp = sb("slot_ramp", [P, COLS], F32, own)
            part_f = sb("part_f", [P, 1], F32, own)
            upto = sb("upto", [P, P], F32, own)
            ones = sb("ones", [P, P], F32, own)
            count = sb("count", [P, HI], F32, own)
            total = sb("total", [P, HI], F32, own)
            cum = sb("cum", [P, HI + 1], F32, own)
            last_at = sb("last_at", [P, HI], F32, own)
            t0 = sb("t0", [P, HI], F32, own)
            t1 = sb("t1", [P, HI], F32, own)
            run = sb("run", [P, HI], I32, own)
            first = sb("first", [P, 1], F32, own)
            full = sb("full", [P, 1], F32, own)
            f1 = sb("f1", [P, 1], F32, own)
            hist = own.enter_context(nc.psum_tensor("hist", [P, BANK], F32))
            sums = own.enter_context(nc.psum_tensor("sums", [P, BANK], F32))
            full_t = own.enter_context(nc.psum_tensor("full_t", [P, BANK], F32))
            hot_t = [own.enter_context(nc.psum_tensor(f"hot_t{i}", [P, BANK], F32)) for i in range(2)]
            with phase("sort_in", "turn_ready", "turned_done", "copied", "keys_out", "keys_in0", "keys_in1", "ends_loaded", "const_done", "vec",
                       "edge_ready", "hot_ready", "hot_used", "count_ready", "sums_done", "got_done", "full_ready", "full_turned",
                       "cols_ready", "cols_turned", "index_ready", "index_out", "root_ready", "root_done") as (
                    block, sort_in, turn_ready, turned_done, copied, keys_out, keys_in0, keys_in1, ends_loaded, const_done, vec,
                    edge_ready, hot_ready, hot_used, count_ready, sums_done, got_done, full_ready, full_turned,
                    cols_ready, cols_turned, index_ready, index_out, root_ready, root_done):
                steps = EF // EB

                @block.sync
                def _(sp):
                    def load_keys(o, keys_in):
                        sp.dma_start(slot_key[o][:, 1:RUN + 1], sorted_dram[o, 0:P * RUN].rearrange("(p t) -> p t", p=P)).then_inc(keys_in, 16)
                    load_keys(1, keys_in1)
                    sp.dma_start(ends_in[0][0:EP, :], src.rearrange("(p f) -> p f", p=EP)).then_inc(ends_loaded, 16)
                    sp.dma_start(ends_in[1][0:EP, :], dst.rearrange("(p f) -> p f", p=EP)).then_inc(ends_loaded, 16)
                    sp.dma_start(w_in[0:EP, :], edge_weight.rearrange("(p f) -> p f", p=EP)).then_inc(ends_loaded, 16)
                    sort_sync(sp, 0, sort_in, turn_ready, keys_out)
                    load_keys(0, keys_in0)
                    store_hot_index(sp, (1, 2), hot_rows, index_ready, index_out)

                @block.gpsimd
                def _(pool):
                    pool.iota(ramp[:, :], [[1, P]], base=0, channel_multiplier=0,
                              allow_small_or_imprecise_dtypes=True).then_inc(const_done, 1)
                    pool.iota(node_f[:, :], [[P, HI]], base=0, channel_multiplier=1,
                              allow_small_or_imprecise_dtypes=True).then_inc(const_done, 1)
                    pool.iota(slot_ramp[:, :], [[1, COLS]], base=0, channel_multiplier=0,
                              allow_small_or_imprecise_dtypes=True).then_inc(const_done, 1)
                    pool.iota(part_f[:, :], [[0, 1]], base=0, channel_multiplier=1,
                              allow_small_or_imprecise_dtypes=True).then_inc(const_done, 1)
                    pool.memset(ones[:, :], 1.0).then_inc(const_done, 1)
                    pool.wait_ge(const_done, 5)
                    pool.affine_select(out=upto[:, :], in_=ones[:, :], compare_op=ALU.is_ge, fill=0.0,
                                       base=0, pattern=[[1, P]], channel_multiplier=-1).then_inc(const_done, 1)
                    pool.wait_ge(edge_ready, 1)
                    gather_records(pool, 1, 0, RUN + 1, got, got_done)
                    pool.wait_ge(got_done, 16 * (RUN + 1))

                @block.tensor
                def _(pe):
                    pe.wait_ge(const_done, 6)
                    for o in (1, 0):
                        pe.wait_ge(full_ready, 2 - o)
                        nc.tensor.transpose(full_t[0:D, o * P:(o + 1) * P], tmp[:, o * D:(o + 1) * D], identity[:, :]).then_inc(full_turned, 1)
                        if o:
                            sort_tensor(pe, turn_ready, turned_done, copied)
                    for o in range(2):
                        for s in range(steps):
                            n = o * steps + s
                            pe.wait_ge(hot_ready, n + 1)
                            if o and not s:
                                pe.wait_ge(count_ready, 1)
                            for f in range(EB):
                                last = nc.tensor.matmul(hist[:, 0:(1 + 3 * o) * HI], one_low[0:EP, n % 2, f, :],
                                                        one_high[0:EP, n % 2, f, 0:1 + 3 * o, :].rearrange("p a h -> p (a h)"),
                                                        start=(s == 0 and f == 0), stop=(s == steps - 1 and f == EB - 1))
                            last.then_inc(hot_used, 1)
                        pe.wait_ge(count_ready, o + 1)
                        nc.tensor.matmul(sums[:, 0:HI], upto[:, :], count[:, :], start=True, stop=True)
                        nc.tensor.matmul(sums[:, HI:2 * HI], ones[:, :], count[:, :], start=True, stop=True).then_inc(sums_done, 1)
                    turn_hot_index(pe, 2, hot_cols, hot_t, cols_ready, cols_turned)

                @block.scalar
                def _(act):
                    sort_scalar(act, turned_done, copied)
                    act.wait_ge(root_ready, 1)
                    act.activation(stat[:, 2, :], stat[:, 1, :], ACT.Sqrt).then_inc(root_done, 1)

                @block.vector
                def _(dve):
                    link = chain(dve, vec)
                    V = nc.vector
                    for o in range(2):
                        V.memset(slot_key[o][:, RUN + 1:COLS], 0)

                    def slots(o):
                        link(V.tensor_copy(slot_key[o][:, 0:1].bitcast(F32), slot_key[o][:, 1:2].bitcast(F32)))
                        link(V.tensor_scalar(gather_index[o][:, :], slot_key[o][:, :].bitcast(U32), ID_MASK, None, ALU.bitwise_and))
                        link(V.memset(gather_index[o][:, 0:1], 0))
                        V.drain().then_inc(edge_ready, 1)
                        if o:
                            dve.wait_ge(const_done, 6)
                        link(V.tensor_scalar(slot_int[:, :], slot_key[o][:, :], ID_BITS, None, ALU.logical_shift_right))
                        link(V.tensor_scalar(tmp[:, :], slot_int[:, :], -float(KEY_BIAS), float(NPAD - 1), ALU.add, ALU.min))
                        link(V.tensor_scalar(own_node[o][:, :], tmp[:, :], 0.0, None, ALU.max))
                        link(V.tensor_scalar(starts[o][:, :], gather_index[o][:, :], 0.0, None, ALU.is_equal))
                        link(V.memset(starts[o][:, RUN + 1:COLS], 0.0))
                        link(V.tensor_tensor(own_node[o][:, :], own_node[o][:, :], starts[o][:, :], ALU.mult))
                        link(V.tensor_scalar(tmp[:, :], starts[o][:, :], -4096.0, 4096.0, ALU.mult, ALU.add))
                        link(V.tensor_tensor(tmp[:, :], tmp[:, :], slot_ramp[:, :], ALU.add))
                        link(V.tensor_reduce(first[:, :], tmp[:, 1:RUN + 1], AX.X, ALU.min))
                        link(V.tensor_scalar(full[:, :], first[:, :], 4096.0, None, ALU.is_ge))
                        link(V.tensor_scalar(first[:, :], first[:, :], float(RUN + 1), -1.0, ALU.min, ALU.add))
                        link(V.tensor_scalar(f1[:, :], part_f[:, :], float(COLS), None, ALU.mult))
                        link(V.tensor_tensor(fix_row[o][:, :], f1[:, :], first[:, :], ALU.add))
                        link(V.tensor_copy(tmp[:, o * D:(o + 1) * D], full[:, 0:1].broadcast_to([P, D])))
                        V.drain().then_inc(full_ready, 1)
                        dve.wait_ge(full_turned, 2 - o)
                        link(V.tensor_copy(whole[o][:, :], full_t[0:D, o * P:(o + 1) * P]))

                    dve.wait_ge(keys_in1, 16)
                    slots(1)
                    link(V.tensor_scalar(minus_node[:, :], node_f[:, :], -1.0, None, ALU.mult))
                    sort_vector(dve, link, sort_in, turn_ready, copied)
                    dve.wait_ge(keys_in0, 16)
                    slots(0)
                    for o in range(2):
                        link(V.memset(inside[o][:, :, :, 0:1], 0))
                        link(V.tensor_scalar(tmp[:, :], starts[o][:, :], -1.0, 1.0, ALU.mult, ALU.add))
                        for k in range(CHUNKS):
                            link(V.tensor_copy(inside[o][:, k, :, 1:CT + 1], tmp[:, k * CT:(k + 1) * CT].unsqueeze(1).broadcast_to([P, D, CT])))
                    dve.wait_ge(ends_loaded, 48)
                    for i in range(3):
                        link(V.tensor_copy(w_parts[0:EP, i, :], w_in[0:EP, :]))
                        link(V.tensor_tensor(w_in[0:EP, :], w_in[0:EP, :], w_parts[0:EP, i, :], ALU.subtract))
                    link(V.tensor_copy(ramp16[:, :], ramp[:, :]))
                    for o in range(2):
                        link(V.tensor_scalar(low[0:EP, :], ends_in[o][0:EP, :], P - 1, None, ALU.bitwise_and))
                        link(V.tensor_scalar(high[0:EP, :], ends_in[o][0:EP, :], 7, None, ALU.logical_shift_right))
                        V.tensor_copy(low16[0:EP, :], low[0:EP, :])
                        link(V.tensor_copy(high16[0:EP, :], high[0:EP, :]))
                        for s in range(steps):
                            n = o * steps + s
                            if n >= 2:
                                dve.wait_ge(hot_used, n - 1)
                            part = slice(s * EB, (s + 1) * EB)
                            V.tensor_tensor(one_low[0:EP, n % 2, :, :], low16[0:EP, part].unsqueeze(2).broadcast_to([EP, EB, P]),
                                            ramp16[0:EP, :].unsqueeze(1).broadcast_to([EP, EB, P]), ALU.is_equal)
                            link(V.tensor_tensor(one_high[0:EP, n % 2, :, 0, :], high16[0:EP, part].unsqueeze(2).broadcast_to([EP, EB, HI]),
                                                 ramp16[0:EP, 0:HI].unsqueeze(1).broadcast_to([EP, EB, HI]), ALU.is_equal))
                            if o:
                                for i in range(3):
                                    link(V.tensor_tensor(one_high[0:EP, n % 2, :, 1 + i, :], one_high[0:EP, n % 2, :, 0, :],
                                                         w_parts[0:EP, i, part].unsqueeze(2).broadcast_to([EP, EB, HI]), ALU.mult))
                            V.drain().then_inc(hot_ready, 1)
                        dve.wait_ge(hot_used, (o + 1) * steps)
                        link(V.tensor_copy(count[:, :], hist[:, 0:HI]))
                        V.drain().then_inc(count_ready, 1)
                        if o:
                            link(V.tensor_copy(degree[:, :], count[:, :]))
                            link(V.tensor_reduce(stat[:, 0, :], hist[:, HI:4 * HI].rearrange("p (a h) -> p h a", a=3), AX.X, ALU.add))
                            link(V.tensor_scalar(stat[:, 0, :], stat[:, 0, :], 1.0, None, ALU.add))
                            link(V.tensor_scalar(stat[:, 1, :], stat[:, 0, :], 1e-30, None, ALU.max))
                            V.drain().then_inc(root_ready, 1)
                            dve.wait_ge(root_done, 1)
                            link(V.reciprocal(stat[:, 3, :], stat[:, 2, :]))
                            link(V.tensor_scalar(stat[:, 0, :], stat[:, 0, :], 0.0, None, ALU.is_gt))
                            link(V.tensor_tensor(inv_root[:, :], stat[:, 3, :], stat[:, 0, :], ALU.mult))
                        dve.wait_ge(sums_done, o + 1)
                        link(V.tensor_copy(total[:, :], sums[:, HI:2 * HI]))
                        link(V.memset(cum[:, 0:1], 0.0))
                        link(V.memset(t0[:, :], 1.0))
                        link(V.tensor_tensor_scan(cum[:, 1:HI + 1], t0[:, :], total[:, :], 0.0, ALU.mult, ALU.add))
                        link(V.tensor_tensor(last_at[:, :], sums[:, 0:HI], cum[:, 0:HI], ALU.add))
                        link(V.tensor_tensor(last_at[:, :], last_at[:, :], node_f[:, :], ALU.add))
                        link(V.tensor_scalar(last_at[:, :], last_at[:, :], float(P * RUN - 1), None, ALU.min))
                        link(V.tensor_scalar(run[:, :], last_at[:, :], 1.0 / RUN, None, ALU.mult))
                        link(V.tensor_scalar(t0[:, :], run[:, :], -float(RUN), None, ALU.mult))
                        link(V.tensor_tensor(t0[:, :], t0[:, :], last_at[:, :], ALU.add))
                        link(V.tensor_scalar(t1[:, :], t0[:, :], 0.0, None, ALU.is_lt))
                        link(V.tensor_scalar(t0[:, :], t0[:, :], float(RUN), None, ALU.is_ge))
                        link(V.tensor_tensor(t0[:, :], t0[:, :], t1[:, :], ALU.subtract))
                        link(V.tensor_tensor(t0[:, :], t0[:, :], run[:, :], ALU.add))
                        link(V.tensor_scalar(t0[:, :], t0[:, :], float(COLS - RUN), 1.0, ALU.mult, ALU.add))
                        link(V.tensor_tensor(end_row[o][:, :], t0[:, :], last_at[:, :], ALU.add))
                    dve.wait_ge(got_done, 16 * (RUN + 1))
                    read_records(dve, link, 1, (1, 2), got, tmp, tmp2, hot_cols, hot_rows, hot_t, cols_ready, cols_turned, index_ready)
                    link(V.tensor_tensor(tmp[:, :], got[:, :, 1].bitcast(F32), tmp2[:, :], ALU.mult))
                    link(V.tensor_tensor(weight[:, :], tmp[:, :], starts[1][:, :], ALU.add))
                    link(V.memset(real[:, :], 1.0))
                    for part in (weight, real):
                        V.memset(part[:, 0:1], 0.0)
                        link(V.memset(part[:, RUN + 1:COLS], 0.0))

        gathered = [sb(f"gathered{i}", [P, CT, D]) for i in range(2)]
        staged = [sb(f"staged{i}", [P, CT, D]) for i in range(2)]
        own_row_space = sb("own_row_space", [P, 2 * D * (CT + 1)])
        own_row = [own_row_space[:, i * D * (CT + 1):(i + 1) * D * (CT + 1)].rearrange("p (c t) -> p c t", c=D) for i in range(2)]
        value = sb("value", [P, D, CT + 1])
        result = [sb(f"result{i}", [P, D, CT + 1]) for i in range(2)]
        last_row = sb("last_row", [P, D])
        last_t = sb("last_t", [D, 1 + P])
        fix = sb("fix", [P, D])
        BY_SRC, BY_DST = 0, 1
        LAST = RUN - (CHUNKS - 1) * CT

        def of_chunk(tile, k):
            return tile[:, k * CT:(k + 1) * CT]

        def over_channels(columns):
            return columns.unsqueeze(1).broadcast_to([P, D, CT])

        def layer_norm(dve, link, norm_ready, norm_root, count, to, of):
            V = nc.vector
            mean, var = stat[:, 0, :], stat[:, 1, :]
            link(V.tensor_reduce(mean, of, AX.X, ALU.add))
            link(V.tensor_scalar(mean, mean, 1.0 / D, None, ALU.mult))
            link(V.tensor_tensor(to, of, mean.unsqueeze(2).broadcast_to([P, HI, D]), ALU.subtract))
            link(V.tensor_tensor(spare[:, :, :], to, to, ALU.mult))
            link(V.tensor_reduce(var, spare[:, :, :], AX.X, ALU.add))
            link(V.tensor_scalar(var, var, 1.0 / D, EPS, ALU.mult, ALU.add))
            V.drain().then_inc(norm_ready, 1)
            dve.wait_ge(norm_root, count)
            link(V.reciprocal(stat[:, 3, :], stat[:, 2, :]))
            link(V.tensor_tensor(to, to, stat[:, 3, :].unsqueeze(2).broadcast_to([P, HI, D]), ALU.mult))

        def root(act, norm_ready, norm_root, count):
            act.wait_ge(norm_ready, count)
            act.activation(stat[:, 2, :], stat[:, 1, :], ACT.Sqrt).then_inc(norm_root, 1)

        def gather_chunk(pool, o, k, chunk_in, used, share):
            if k >= 2:
                pool.wait_ge(used, k - 1)
            for t in dma_columns(k, share):
                at = k * CT + t
                pool.indirect_dma_start(gathered[k % 2][:, t, :], None, table_dram,
                                        bass.IndirectOffsetOnAxis(ap=gather_index[o][:, at:at + 1], axis=0)).then_inc(chunk_in[k % 2], 16)

        def dmas_until(k, share):
            return 16 * sum(len(dma_columns(c, share)) for c in range(k % 2, k + 1, 2))

        def gather_chunks(pool, o, chunk_in, used, share):
            for k in range(CHUNKS):
                gather_chunk(pool, o, k, chunk_in, used, share)
            for i in range(2):
                pool.wait_ge(chunk_in[i], dmas_until(CHUNKS - 2 + i, share))

        def hot_blocks(dve, sets, k, part, index_rows, hot, hot_index_in, hot_ready, hot_used):
            if index_count(sets, k):
                dve.wait_ge(hot_index_in[k % 2], index_count(sets, k))
            w = banks_of(sets, k) * BANK
            for i in part:
                n = k * len(DVE_BLOCKS) + i
                if n >= RING:
                    dve.wait_ge(hot_used, n - RING + 1)
                nc.vector.tensor_scalar(hot[n % RING][:, 0:w], index_rows[k % 2][:, 0:w], node_f[:, DVE_BLOCKS[i]:DVE_BLOCKS[i] + 1],
                                        None, ALU.is_equal).then_inc(hot_ready, 1)

        def act_hot_block(act, sets, n, index_rows, far, act_hot, hot_index_in, far_ready, act_hot_ready, act_hot_used, acc_done):
            k, i = divmod(n, len(ACT_BLOCKS))
            if k >= len(sets) * CHUNKS:
                return
            w = banks_of(sets, k) * BANK
            b = ACT_BLOCKS[i]
            if index_count(sets, k):
                act.wait_ge(hot_index_in[k % 2], index_count(sets, k))
            if n >= 2:
                act.wait_ge(act_hot_ready, n - 1)
            act.activation(far[n % 2][:, 0:w], index_rows[k % 2][:, 0:w], ACT.Abs, bias=minus_node[:, b:b + 1]).then_inc(far_ready, 1)
            if n >= ACT_RING:
                k_was, i_was = divmod(n - ACT_RING, len(ACT_BLOCKS))
                if i_was == len(ACT_BLOCKS) - 1:
                    act.wait_ge(acc_done, (k_was + 1) * HOT_BANKS)
                else:
                    act.wait_ge(act_hot_used, k_was * (len(ACT_BLOCKS) - 1) + i_was + 1)
            act.wait_ge(far_ready, n + 1)
            act.activation(act_hot[n % ACT_RING][:, 0:w], far[n % 2][:, 0:w], ACT.Relu, bias=1.0, scale=-1.0).then_inc(act_hot_ready, 1)

        def index_count(sets, k):
            return 16 * (k // 2 + (1 if k % 2 or len(sets) > 1 else 0))

        def hot_index_of(s, c):
            return hot_index_dram[s, c * HOT_TILES:(c + 1) * HOT_TILES, :].rearrange("i p -> (i p)").partition_broadcast(P)

        def load_hot_index(sp, sets, k, index_rows, hot_index_in, hot_ready, act_hot_ready):
            if k >= 2:
                sp.wait_ge(hot_ready, (k - 1) * len(DVE_BLOCKS))
                sp.wait_ge(act_hot_ready, (k - 1) * len(ACT_BLOCKS))
            c, u = divmod(k, len(sets))
            if index_count(sets, k):
                sp.dma_start(index_rows[k % 2][:, :], hot_index_of(sets[u], c)).then_inc(hot_index_in[k % 2], 16)

        def load_first_index(sp, s, index_rows, hot_index_in, hot_ready, act_hot_ready):
            sp.wait_ge(hot_ready, CHUNKS * len(DVE_BLOCKS))
            sp.wait_ge(act_hot_ready, CHUNKS * len(ACT_BLOCKS))
            sp.dma_start(index_rows[0][:, :], hot_index_of(s, 0)).then_inc(hot_index_in[0], 16)

        def multiply_hot(pe, sets, hot, act_hot, acc, moved, summed, hot_ready, hot_used, act_hot_ready, act_hot_used, acc_done, acc_moved, sum_done, row_ready):
            def sum_up(k):
                for j in range(banks_of(sets, k)):
                    pe.wait_ge(acc_moved, k * HOT_BANKS + j + 1)
                    if k and not j:
                        pe.wait_ge(row_ready, k)
                    for i in range(BANK // P):
                        t = j * (BANK // P) + i
                        last = nc.tensor.matmul(summed[:, t * D:(t + 1) * D], moved[k % 2][:, t * P:(t + 1) * P], sum_parts[:, :], start=True, stop=True)
                last.then_inc(sum_done, 1)

            for k in range(len(sets) * CHUNKS):
                for b in range(HI):
                    if b == 6 and k:
                        sum_up(k - 1)
                    if b in ACT_BLOCKS:
                        n = k * len(ACT_BLOCKS) + ACT_BLOCKS.index(b)
                        pe.wait_ge(act_hot_ready, n + 1)
                        columns, columns_used = act_hot[n % ACT_RING], act_hot_used
                    else:
                        n = k * len(DVE_BLOCKS) + DVE_BLOCKS.index(b)
                        pe.wait_ge(hot_ready, n + 1)
                        columns, columns_used = hot[n % RING], hot_used
                    for j in range(banks_of(sets, k)):
                        m = k * HOT_BANKS + j
                        if not b and m >= len(acc):
                            pe.wait_ge(acc_moved, m - len(acc) + 1)
                        last = nc.tensor.matmul(acc[m % len(acc)][0:SPLIT, :], parts[:, b, :, :].rearrange("p s c -> p (s c)"),
                                                columns[:, j * BANK:(j + 1) * BANK], start=(b == 0), stop=(b == HI - 1))
                        if b == HI - 1:
                            last.then_inc(acc_done, 1)
                    if b < HI - 1:
                        last.then_inc(columns_used, 1)
            sum_up(len(sets) * CHUNKS - 1)

        def move_parts(act, sets, k, acc, moved, acc_done, acc_moved, sum_done):
            for j in range(banks_of(sets, k)):
                m = k * HOT_BANKS + j
                act.wait_ge(acc_done, m + 1)
                if k >= 2 and not j:
                    act.wait_ge(sum_done, k - 1)
                act.activation(moved[k % 2][:, j * BANK:(j + 1) * BANK], acc[m % len(acc)][0:SPLIT, :], ACT.Copy).then_inc(acc_moved, 1)

        def move_rows(act, sets, k, summed, sum_done, used, row_ready):
            act.wait_ge(sum_done, k + 1)
            c, u = divmod(k, len(sets))
            if c >= 2:
                act.wait_ge(used, c - 1)
            tiles = banks_of(sets, k) * BANK // P
            act.activation(gathered[c % 2][:, SETS[sets[u]]:SETS[sets[u]] + tiles, :].rearrange("p t c -> p (t c)"), summed[:, 0:tiles * D],
                           ACT.Copy).then_inc(row_ready, 1)

        def scalar_chunks(act, sets, index_rows, far, act_hot, hot_index_in, far_ready, act_hot_ready, act_hot_used, acc, moved, summed,
                          acc_done, acc_moved, sum_done, used, row_ready, result_ready, stored, staged_ready):
            def hot_block(n):
                act_hot_block(act, sets, n, index_rows, far, act_hot, hot_index_in, far_ready, act_hot_ready, act_hot_used, acc_done)
            count = len(ACT_BLOCKS)
            for n in range(ACT_RING):
                hot_block(n)
            for k in range(len(sets) * CHUNKS + 1):
                if k:
                    move_rows(act, sets, k - 1, summed, sum_done, used, row_ready)
                for n in range(k * count + ACT_RING, (k + 1) * count):
                    hot_block(n)
                c = (k - 1) // len(sets) - 1
                if c >= 0 and (k - 1) % len(sets) == 0:
                    stage_result(act, c, result_ready, stored, staged_ready)
                hot_block((k + 1) * count)
                hot_block((k + 1) * count + 1)
                if k < len(sets) * CHUNKS:
                    move_parts(act, sets, k, acc, moved, acc_done, acc_moved, sum_done)
                hot_block((k + 1) * count + 2)
            stage_result(act, CHUNKS - 1, result_ready, stored, staged_ready)

        def stage_result(act, k, result_ready, stored, staged_ready):
            act.wait_ge(result_ready, k + 1)
            if k >= 2:
                act.wait_ge(stored[k % 2], 16 * (k // 2))
            act.activation(staged[k % 2][:, :, :], result[k % 2][:, :, 1:CT + 1].rearrange("p c t -> p t c"), ACT.Copy).then_inc(staged_ready, 1)

        def store_chunk(sp, k, staged_ready, stored):
            sp.wait_ge(staged_ready, k + 1)
            sp.dma_start(scan_rows[:, k * CT:(k + 1) * CT, :], staged[k % 2][:, :, :]).then_inc(stored[k % 2], 16)

        def turn_last(pe, turned, last_ready, last_turned, joined_ready):
            pe.wait_ge(last_ready, 1)
            nc.tensor.transpose(turned[0:D, 0:P], last_row[:, :], identity[:, :]).then_inc(last_turned, 1)
            pe.wait_ge(joined_ready, 1)
            nc.tensor.transpose(turned[:, P:P + D], last_t[:, 0:P], identity[0:D, 0:D]).then_inc(last_turned, 1)

        def join_runs(dve, link, o, op, turned, last_turned, joined_ready):
            V = nc.vector
            link(V.memset(last_t[:, 0:1], 0.0))
            dve.wait_ge(last_turned, 1)
            link(V.tensor_tensor_scan(last_t[:, 1:P + 1], whole[o][:, :], turned[0:D, 0:P], 0.0, ALU.mult, op))
            V.drain().then_inc(joined_ready, 1)

        def fix_ends(dve, link, op, turned, last_turned, fix_in, fix_ready):
            dve.wait_ge(last_turned, 2)
            dve.wait_ge(fix_in, 16)
            link(nc.vector.tensor_tensor(fix[:, :], fix[:, :], turned[:, P:P + D], op))
            nc.vector.drain().then_inc(fix_ready, 1)

        def gather_ends(pool, o, table, stored, count, fix_in, fix_ready, ends_in_):
            for s in stored:
                pool.wait_ge(s, count)
            row = bass.IndirectOffsetOnAxis(ap=fix_row[o][:, :], axis=0)
            pool.indirect_dma_start(fix[:, :], None, table, row).then_inc(fix_in, 16)
            pool.wait_ge(fix_ready, 1)
            pool.indirect_dma_start(table, row, fix[:, :], None).then_inc(fix_in, 16)
            pool.wait_ge(fix_in, 32)
            per = HI // len(ends_in_)
            for h in range(HI):
                pool.indirect_dma_start(ends[:, h, :], None, table,
                                        bass.IndirectOffsetOnAxis(ap=end_row[o][:, h:h + 1], axis=0)).then_inc(ends_in_[h // per], 16)
            for sem in ends_in_:
                pool.wait_ge(sem, 16 * per)

        def carry(link, k, tile, before):
            if k:
                link(nc.vector.tensor_copy(tile[:, :, 0:1], before[:, :, CT:CT + 1]))
            else:
                link(nc.vector.memset(tile[:, :, 0:1], 0.0))

        def spread_own_rows(link, k, o, value):
            V = nc.vector
            carry(link, k, value, own_row[(k - 1) % 2])
            link(V.tensor_tensor(value[:, :, 1:CT + 1], gathered[k % 2][:, :, :].rearrange("p t c -> p c t"),
                                 over_channels(of_chunk(starts[o], k)), ALU.mult))
            link(V.tensor_tensor_scan(flat(own_row[k % 2]), inside_of(o, k), flat(value), 0.0, ALU.mult, ALU.add))

        def flat(tile):
            return tile[:, :, :].rearrange("p c t -> p (c t)")

        def inside_of(o, k):
            return inside[o][:, k, :, :].rearrange("p c t -> p (c t)")

        def scan_value(dve, link, k, o, op, staged_ready, result_ready):
            carry(link, k, value, result[(k - 1) % 2])
            if k >= 2:
                dve.wait_ge(staged_ready, k - 1)
            link(nc.vector.tensor_tensor_scan(flat(result[k % 2]), inside_of(o, k), flat(value), 0.0, ALU.mult, op))
            nc.vector.drain().then_inc(result_ready, 1)

        def keep_last(link, last_ready):
            link(nc.vector.tensor_copy(last_row[:, :], result[(CHUNKS - 1) % 2][:, :, 1 + LAST]))
            nc.vector.drain().then_inc(last_ready, 1)

        def wait_rows(dve, k, chunk_in, share, row_ready, shares=1):
            dve.wait_ge(chunk_in[k % 2], dmas_until(k, share))
            dve.wait_ge(row_ready, (k + 1) * shares)

        COMMON = ("chunk_in0", "chunk_in1", "used", "vec", "result_ready", "staged_ready", "stored0", "stored1",
                  "last_ready", "last_turned", "joined_ready", "fix_in", "fix_ready", "ends_in",
                  "rows_ready", "table_in", "norm_ready", "norm_root")
        HOTS_ = ("hot_index_in0", "hot_index_in1", "hot_ready", "hot_used", "far_ready", "act_hot_ready", "act_hot_used",
                 "acc_done", "acc_moved", "sum_done", "row_ready")

        FIRST_PART, SECOND_PART = range(0, 16), range(16, len(DVE_BLOCKS))

        def sum_chunk(dve, link, k, factor, chunk_in, row_ready, used, share=ONE_SHARE, shares=1):
            V = nc.vector
            wait_rows(dve, k, chunk_in, share, row_ready, shares)
            link(V.tensor_tensor(value[:, :, 1:CT + 1], gathered[k % 2][:, :, :].rearrange("p t c -> p c t"),
                                 over_channels(of_chunk(factor, k)), ALU.mult))
            V.drain().then_inc(used, 1)

        with ExitStack() as hots:
            index_rows = [sb(f"index_rows{i}", [P, HOT], I16, hots) for i in range(2)]
            hot_space = sb("hot_space", [P, RING * HOT], BF16, hots)
            hot = [hot_space[:, i * HOT:(i + 1) * HOT] for i in range(RING)]
            act_hot = [sb(f"act_hot{i}", [P, HOT], BF16, hots) for i in range(ACT_RING)]
            got_src = own_row_space[:, 0:2 * COLS].bitcast(I32).rearrange("p (t w) -> p t w", w=2)
            far = [sb(f"far{i}", [P, HOT], BF16, hots) for i in range(2)]
            moved = [sb(f"moved{i}", [SPLIT, HOT], BF16, hots) for i in range(2)]

            with ExitStack() as own:
                acc = [own.enter_context(nc.psum_tensor(f"acc0_{i}", [P, BANK], F32)) for i in range(7)]
                summed = own.enter_context(nc.psum_tensor("summed0", [P, BANK], F32))
                with phase(*COMMON, *HOTS_, "got_done") as (
                        block, chunk_in0, chunk_in1, used, vec, result_ready, staged_ready, stored0, stored1,
                        last_ready, last_turned, joined_ready, fix_in, fix_ready, ends_in_, rows_ready, table_in, norm_ready, norm_root,
                        hot_index_in0, hot_index_in1, hot_ready, hot_used, far_ready, act_hot_ready, act_hot_used, acc_done, acc_moved, sum_done, row_ready, got_done):
                    chunk_in, stored, hot_index_in = (chunk_in0, chunk_in1), (stored0, stored1), (hot_index_in0, hot_index_in1)

                    SHARES = (2, 1)

                    @block.sync
                    def _(sp):
                        for m in range(len(SHARES) * (CHUNKS + 2)):
                            if m < len(SHARES) * CHUNKS:
                                load_hot_index(sp, SHARES, m, index_rows, hot_index_in, hot_ready, act_hot_ready)
                            if m % len(SHARES) == 0 and m >= 2 * len(SHARES):
                                store_chunk(sp, m // len(SHARES) - 2, staged_ready, stored)
                        sp.wait_ge(rows_ready, 1)
                        sp.dma_start(table_nodes, state[:, :, :]).then_inc(table_in, 16)
                        sp.wait_ge(table_in, 16)

                    @block.gpsimd
                    def _(pool):
                        for k in range(CHUNKS):
                            gather_chunk(pool, BY_DST, k, chunk_in, used, TWO_SHARES)
                            gather_records(pool, BY_SRC, k * CT, min((k + 1) * CT, RUN + 1), got_src, got_done)
                        for i in range(2):
                            pool.wait_ge(chunk_in[i], dmas_until(CHUNKS - 2 + i, TWO_SHARES))
                        pool.wait_ge(got_done, 16 * (RUN + 1))
                        gather_ends(pool, BY_DST, scan_dram, stored, 16 * CHUNKS // 2, fix_in, fix_ready, (ends_in_,))

                    @block.tensor
                    def _(pe):
                        multiply_hot(pe, SHARES, hot, act_hot, acc, moved, summed, hot_ready, hot_used, act_hot_ready, act_hot_used, acc_done, acc_moved, sum_done, row_ready)
                        turn_last(pe, acc[0], last_ready, last_turned, joined_ready)

                    @block.scalar
                    def _(act):
                        scalar_chunks(act, SHARES, index_rows, far, act_hot, hot_index_in, far_ready, act_hot_ready, act_hot_used, acc, moved, summed,
                                      acc_done, acc_moved, sum_done, used, row_ready, result_ready, stored, staged_ready)
                        root(act, norm_ready, norm_root, 1)

                    @block.vector
                    def _(dve):
                        link = chain(dve, vec)
                        for m in range(len(SHARES) * CHUNKS + 1):
                            whole_chunk = m and m % len(SHARES) == 0
                            c = m // len(SHARES) - 1
                            if m < len(SHARES) * CHUNKS:
                                hot_blocks(dve, SHARES, m, FIRST_PART, index_rows, hot, hot_index_in, hot_ready, hot_used)
                            if whole_chunk:
                                sum_chunk(dve, link, c, real, chunk_in, row_ready, used, TWO_SHARES, len(SHARES))
                            if m < len(SHARES) * CHUNKS:
                                hot_blocks(dve, SHARES, m, SECOND_PART, index_rows, hot, hot_index_in, hot_ready, hot_used)
                            if whole_chunk:
                                scan_value(dve, link, c, BY_DST, ALU.add, staged_ready, result_ready)
                        keep_last(link, last_ready)
                        join_runs(dve, link, BY_DST, ALU.add, acc[0], last_turned, joined_ready)
                        fix_ends(dve, link, ALU.add, acc[0], last_turned, fix_in, fix_ready)
                        dve.wait_ge(ends_in_, 16 * HI)
                        layer_norm(dve, link, norm_ready, norm_root, 1, state[:, :, :], ends[:, :, :])
                        link(nc.vector.tensor_copy(rows[:, :, :], state[:, :, :]))
                        nc.vector.drain().then_inc(rows_ready, 1)
                        split_rows(link, rows[:, :, :])

            with ExitStack() as own:
                hot_t = own.enter_context(nc.psum_tensor("hot_t_src", [P, BANK], F32))
                with phase("vec", "cols_ready", "cols_turned", "index_ready", "index_out", "root_ready", "root_done", "index_in") as (
                        block, vec, cols_ready, cols_turned, index_ready, index_out, root_ready, root_done, index_in):
                    tmp, tmp2, hot_cols = [hot_space[:, i * 2 * COLS:(i + 1) * 2 * COLS].bitcast(F32) for i in range(3)]
                    hot_cols = hot_cols[:, 0:HOTS].rearrange("p (i n) -> p i n", i=1)
                    hot_rows = act_hot[0][:, 0:len(HOT_PARTS) * P].bitcast(I16).rearrange("p (i b n) -> p i b n", i=1, n=P)

                    @block.sync
                    def _(sp):
                        store_hot_index(sp, (0,), hot_rows, index_ready, index_out)
                        sp.dma_start(index_rows[0][:, :], hot_index_of(0, 0)).then_inc(index_in, 16)
                        sp.wait_ge(index_in, 16)

                    @block.tensor
                    def _(pe):
                        turn_hot_index(pe, 1, hot_cols, (hot_t,), cols_ready, cols_turned)

                    @block.scalar
                    def _(act):
                        act.wait_ge(root_ready, 1)
                        act.activation(tmp2, tmp2, ACT.Sqrt).then_inc(root_done, 1)

                    @block.vector
                    def _(dve):
                        link = chain(dve, vec)
                        V = nc.vector
                        read_records(dve, link, BY_SRC, (0,), got_src, tmp, tmp2, hot_cols, hot_rows, (hot_t,), cols_ready, cols_turned, index_ready)
                        w_got = got_src[:, :, 1].bitcast(F32)
                        link(V.tensor_scalar(tmp, w_got, 0.0, None, ALU.is_gt))
                        link(V.tensor_tensor(tmp, tmp, tmp2, ALU.mult))
                        link(V.tensor_scalar(tmp2, w_got, 1e-30, None, ALU.max))
                        V.drain().then_inc(root_ready, 1)
                        dve.wait_ge(root_done, 1)
                        link(V.tensor_tensor(root_weight[:, :], tmp2, tmp, ALU.mult))

            GROUPS = 5
            GROUP = HI // GROUPS

            with ExitStack() as own:
                acc = [own.enter_context(nc.psum_tensor(f"acc1_{i}", [P, BANK], F32)) for i in range(7)]
                summed = own.enter_context(nc.psum_tensor("summed1", [P, BANK], F32))
                with nc.Fori(0, 10):
                    with phase(*COMMON, *HOTS_, "ends_in1", "ends_in2", "ends_in3", "ends_in4") as (
                            block, chunk_in0, chunk_in1, used, vec, result_ready, staged_ready, stored0, stored1,
                            last_ready, last_turned, joined_ready, fix_in, fix_ready, ends_in_, rows_ready, table_in, norm_ready, norm_root,
                            hot_index_in0, hot_index_in1, hot_ready, hot_used, far_ready, act_hot_ready, act_hot_used, acc_done, acc_moved, sum_done, row_ready,
                            ends_in1, ends_in2, ends_in3, ends_in4):
                        ends_in_ = (ends_in_, ends_in1, ends_in2, ends_in3, ends_in4)
                        chunk_in, stored, hot_index_in = (chunk_in0, chunk_in1), (stored0, stored1), (hot_index_in0, hot_index_in1)

                        @block.sync
                        def _(sp):
                            for k in range(CHUNKS + 2):
                                if k < CHUNKS:
                                    load_hot_index(sp, (0,), k, index_rows, hot_index_in, hot_ready, act_hot_ready)
                                if k >= 2:
                                    store_chunk(sp, k - 2, staged_ready, stored)
                            load_first_index(sp, 0, index_rows, hot_index_in, hot_ready, act_hot_ready)
                            for g in range(GROUPS):
                                cols = slice(g * GROUP, (g + 1) * GROUP)
                                sp.wait_ge(rows_ready, g + 1)
                                sp.dma_start(table_nodes[:, cols, :], rows[:, cols, :]).then_inc(table_in, 16)
                            sp.wait_ge(table_in, 16 * GROUPS)
                            sp.wait_ge(hot_index_in[0], 16 * (CHUNKS // 2))

                        @block.gpsimd
                        def _(pool):
                            gather_chunks(pool, BY_SRC, chunk_in, used, ONE_SHARE)
                            gather_ends(pool, BY_SRC, scan_dram, stored, 16 * CHUNKS // 2, fix_in, fix_ready, ends_in_)

                        @block.tensor
                        def _(pe):
                            multiply_hot(pe, (0,), hot, act_hot, acc, moved, summed, hot_ready, hot_used, act_hot_ready, act_hot_used, acc_done, acc_moved, sum_done, row_ready)
                            turn_last(pe, acc[0], last_ready, last_turned, joined_ready)

                        @block.scalar
                        def _(act):
                            scalar_chunks(act, (0,), index_rows, far, act_hot, hot_index_in, far_ready, act_hot_ready, act_hot_used, acc, moved, summed,
                                          acc_done, acc_moved, sum_done, used, row_ready, result_ready, stored, staged_ready)

                        @block.vector
                        def _(dve):
                            link = chain(dve, vec)
                            V = nc.vector
                            for k in range(CHUNKS + 1):
                                if k < CHUNKS:
                                    hot_blocks(dve, (0,), k, FIRST_PART, index_rows, hot, hot_index_in, hot_ready, hot_used)
                                if k:
                                    c = k - 1
                                    wait_rows(dve, c, chunk_in, ONE_SHARE, row_ready)
                                    spread_own_rows(link, c, BY_SRC, value)
                                    link(V.tensor_tensor(value[:, :, 1:CT + 1], gathered[c % 2][:, :, :].rearrange("p t c -> p c t"),
                                                         own_row[c % 2][:, :, 1:CT + 1], ALU.subtract))
                                    V.drain().then_inc(used, 1)
                                if k < CHUNKS:
                                    hot_blocks(dve, (0,), k, SECOND_PART, index_rows, hot, hot_index_in, hot_ready, hot_used)
                                if k:
                                    link(V.scalar_tensor_tensor(value[:, :, 1:CT + 1], value[:, :, 1:CT + 1], 0.0,
                                                                over_channels(of_chunk(root_weight, c)), ALU.max, ALU.mult))
                                    scan_value(dve, link, c, BY_SRC, ALU.max, staged_ready, result_ready)
                            keep_last(link, last_ready)
                            join_runs(dve, link, BY_SRC, ALU.max, acc[0], last_turned, joined_ready)
                            fix_ends(dve, link, ALU.max, acc[0], last_turned, fix_in, fix_ready)
                            for g in range(GROUPS):
                                cols = slice(g * GROUP, (g + 1) * GROUP)
                                dve.wait_ge(ends_in_[g], 16 * GROUP)
                                link(V.tensor_tensor(rows[:, cols, :], rows[:, cols, :], ends[:, cols, :], ALU.add))
                                V.drain().then_inc(rows_ready, 1)
                                split_rows(link, rows, cols)

            with phase("vec", "norm_ready", "norm_root", "rows_ready", "table_in", "index_in") as (
                    block, vec, norm_ready, norm_root, rows_ready, table_in, index_in):
                @block.scalar
                def _(act):
                    root(act, norm_ready, norm_root, 1)

                @block.sync
                def _(sp):
                    sp.dma_start(index_rows[0][:, :], hot_index_of(1, 0)).then_inc(index_in, 16)
                    sp.wait_ge(index_in, 16)
                    sp.wait_ge(rows_ready, 1)
                    sp.dma_start(table_nodes, rows[:, :, :]).then_inc(table_in, 16)
                    sp.wait_ge(table_in, 16)

                @block.vector
                def _(dve):
                    link = chain(dve, vec)
                    V = nc.vector
                    link(V.tensor_tensor(ends[:, :, :], state[:, :, :], rows[:, :, :], ALU.add))
                    layer_norm(dve, link, norm_ready, norm_root, 1, state[:, :, :], ends[:, :, :])
                    link(V.tensor_tensor(rows[:, :, :], state[:, :, :], inv_root[:, :].unsqueeze(2).broadcast_to([P, HI, D]), ALU.mult))
                    V.drain().then_inc(rows_ready, 1)
                    split_rows(link, rows[:, :, :])

            GATES = (0, 4, 6)
            GW = len(GATES) * D
            with ExitStack() as own:
                gate_w = sb("gate_w", [D + 1, 3, D], F32, own)
                bias_in = sb("bias_in", [D + 1, 3, GW], F32, own)
                peep = sb("peep", [P, D], F32, own)
                flat_t = hot_space[0:D + 1, 0:2 * NPAD].bitcast(F32)
                cell = spare
                gate = hot_space[:, 2 * NPAD:2 * (NPAD + HI * D)].bitcast(F32).rearrange("p (h c) -> p h c", c=D)
                psum = [own.enter_context(nc.psum_tensor(f"bank{i}", [P, BANK], F32)) for i in range(8)]
                acc, summed = psum[0:7], psum[7]
                with nc.Fori(0, 3) as layer:
                    with phase(*COMMON, *HOTS_, "weights_in", "bias_ready", "agg_ready", "agg_turned", "flat_ready", "gates_done", "act_done",
                               "out_ready", "out_done", "ends_in1", "ends_in2", "ends_in3", "ends_in4") as (
                            block, chunk_in0, chunk_in1, used, vec, result_ready, staged_ready, stored0, stored1,
                            last_ready, last_turned, joined_ready, fix_in, fix_ready, ends_in_, rows_ready, table_in, norm_ready, norm_root,
                            hot_index_in0, hot_index_in1, hot_ready, hot_used, far_ready, act_hot_ready, act_hot_used, acc_done, acc_moved, sum_done, row_ready,
                            weights_in, bias_ready, agg_ready, agg_turned, flat_ready, gates_done, act_done,
                            out_ready, out_done, ends_in1, ends_in2, ends_in3, ends_in4):
                        ends_in_ = (ends_in_, ends_in1, ends_in2, ends_in3, ends_in4)
                        chunk_in, stored, hot_index_in = (chunk_in0, chunk_in1), (stored0, stored1), (hot_index_in0, hot_index_in1)
                        turned_banks = ((psum[GROUPS], 0, BANK // P), (psum[GROUPS + 1], BANK // P, GROUP))

                        def columns(g):
                            return slice(g * GROUP, (g + 1) * GROUP)

                        def of_gate(i, g):
                            return psum[g][:, 0:GROUP * GW].rearrange("p (h n) -> p h n", n=GW)[:, :, i * D:(i + 1) * D]

                        @block.sync
                        def _(sp):
                            for i, g in enumerate(GATES):
                                sp.dma_start(gate_w[0:D, i, :], conv_w[bass.ds(layer, 1), g, :, :].rearrange("l k n -> (l k) n")).then_inc(weights_in, 16)
                                for r, gg in enumerate((g, g + 1)):
                                    sp.dma_start(bias_in[D:D + 1, r, i * D:(i + 1) * D], conv_b[bass.ds(layer, 1), gg, :]).then_inc(weights_in, 16)
                                sp.dma_start(bias_in[D:D + 1, 2, i * D:(i + 1) * D], bg[bass.ds(layer, 1), (0, 2, 3)[i], :]).then_inc(weights_in, 16)
                            sp.dma_start(peep[:, :], wc[bass.ds(layer, 1), 2, :].broadcast_to([P, D])).then_inc(weights_in, 16)
                            for k in range(CHUNKS + 2):
                                if k < CHUNKS:
                                    load_hot_index(sp, (1,), k, index_rows, hot_index_in, hot_ready, act_hot_ready)
                                if k >= 2:
                                    store_chunk(sp, k - 2, staged_ready, stored)
                            load_first_index(sp, 1, index_rows, hot_index_in, hot_ready, act_hot_ready)
                            sp.wait_ge(hot_index_in[0], 16 * (CHUNKS // 2))
                            for g in range(GROUPS):
                                sp.wait_ge(rows_ready, g + 1)
                                sp.dma_start(table_nodes[:, columns(g), :], gate[:, columns(g), :]).then_inc(table_in, 16)
                            sp.wait_ge(table_in, 16 * GROUPS)
                            sp.wait_ge(weights_in, 16 * 13)

                        @block.gpsimd
                        def _(pool):
                            gather_chunks(pool, BY_DST, chunk_in, used, ONE_SHARE)
                            gather_ends(pool, BY_DST, scan_dram, stored, 16 * CHUNKS // 2, fix_in, fix_ready, ends_in_)

                        @block.tensor
                        def _(pe):
                            multiply_hot(pe, (1,), hot, act_hot, acc, moved, summed, hot_ready, hot_used, act_hot_ready, act_hot_used, acc_done, acc_moved, sum_done, row_ready)
                            turn_last(pe, acc[0], last_ready, last_turned, joined_ready)
                            for g in range(GROUPS):
                                pe.wait_ge(agg_ready, g + 1)
                                if g:
                                    pe.wait_ge(flat_ready, 2 * g)
                                for bank, first, end in turned_banks:
                                    for h in range(first, end):
                                        last = nc.tensor.transpose(bank[0:D, (h - first) * P:(h - first + 1) * P], ends[:, g * GROUP + h, :], identity[:, :])
                                last.then_inc(agg_turned, 1)
                                if not g:
                                    pe.wait_ge(bias_ready, 1)
                                pe.wait_ge(flat_ready, 2 * (g + 1))
                                for h in range(GROUP):
                                    at = (g * GROUP + h) * P
                                    last = nc.tensor.matmul(psum[g][:, h * GW:(h + 1) * GW], flat_t[:, at:at + P],
                                                            gate_w[:, :, :].rearrange("k g n -> k (g n)"), start=True, stop=True)
                                last.then_inc(gates_done, 1)

                        @block.scalar
                        def _(act):
                            scalar_chunks(act, (1,), index_rows, far, act_hot, hot_index_in, far_ready, act_hot_ready, act_hot_used, acc, moved, summed,
                                          acc_done, acc_moved, sum_done, used, row_ready, result_ready, stored, staged_ready)
                            for g in range(GROUPS + 1):
                                if g < GROUPS:
                                    act.wait_ge(agg_turned, g + 1)
                                    for bank, first, end in turned_banks:
                                        at = (g * GROUP + first) * P
                                        n = (end - first) * P
                                        act.activation(flat_t[0:D, at:at + n], bank[0:D, 0:n], ACT.Copy).then_inc(flat_ready, 1)
                                    act.wait_ge(gates_done, g + 1)
                                    act.activation(ends[:, columns(g), :], of_gate(0, g), ACT.Sigmoid).then_inc(act_done, 1)
                                    act.activation(gate[:, columns(g), :], of_gate(1, g), ACT.Tanh).then_inc(act_done, 1)
                                if g:
                                    act.wait_ge(out_ready, g)
                                    was = columns(g - 1)
                                    act.activation(gate[:, was, :], gate[:, was, :], ACT.Sigmoid).then_inc(out_done, 1)
                                    act.activation(cell[:, was, :], cell[:, was, :], ACT.Tanh).then_inc(out_done, 1)

                        @block.vector
                        def _(dve):
                            link = chain(dve, vec)
                            V = nc.vector
                            dve.wait_ge(weights_in, 16 * 13)
                            bias = gate_w[D:D + 1, :, :].rearrange("k g n -> k (g n)")
                            link(V.tensor_tensor(bias, bias_in[D:D + 1, 0, :], bias_in[D:D + 1, 1, :], ALU.add))
                            link(V.tensor_tensor(bias, bias, bias_in[D:D + 1, 2, :], ALU.add))
                            V.drain().then_inc(bias_ready, 1)
                            for k in range(CHUNKS + 1):
                                if k < CHUNKS:
                                    hot_blocks(dve, (1,), k, FIRST_PART, index_rows, hot, hot_index_in, hot_ready, hot_used)
                                if k:
                                    sum_chunk(dve, link, k - 1, weight, chunk_in, row_ready, used)
                                if k < CHUNKS:
                                    hot_blocks(dve, (1,), k, SECOND_PART, index_rows, hot, hot_index_in, hot_ready, hot_used)
                                if k:
                                    scan_value(dve, link, k - 1, BY_DST, ALU.add, staged_ready, result_ready)
                            keep_last(link, last_ready)
                            join_runs(dve, link, BY_DST, ALU.add, acc[0], last_turned, joined_ready)
                            fix_ends(dve, link, ALU.add, acc[0], last_turned, fix_in, fix_ready)
                            link(V.memset(flat_t[D:D + 1, :], 1.0))

                            def by_root(to, of, g):
                                link(V.tensor_tensor(to[:, columns(g), :], of[:, columns(g), :],
                                                     inv_root[:, columns(g)].unsqueeze(2).broadcast_to([P, GROUP, D]), ALU.mult))

                            for g in range(GROUPS + 2):
                                if g < GROUPS:
                                    dve.wait_ge(ends_in_[g], 16 * GROUP)
                                    by_root(ends, ends, g)
                                    V.drain().then_inc(agg_ready, 1)
                                if 1 <= g <= GROUPS:
                                    was = columns(g - 1)
                                    dve.wait_ge(act_done, 2 * g)
                                    link(V.tensor_tensor(cell[:, was, :], ends[:, was, :], gate[:, was, :], ALU.mult))
                                    link(V.tensor_tensor(gate[:, was, :], cell[:, was, :], peep[:, :].unsqueeze(1).broadcast_to([P, GROUP, D]), ALU.mult))
                                    link(V.tensor_tensor(gate[:, was, :], gate[:, was, :], of_gate(2, g - 1), ALU.add))
                                    V.drain().then_inc(out_ready, 1)
                                if g >= 2:
                                    was = columns(g - 2)
                                    dve.wait_ge(out_done, 2 * (g - 1))
                                    link(V.tensor_tensor(rows[:, was, :], gate[:, was, :], cell[:, was, :], ALU.mult))
                                    by_root(gate, rows, g - 2)
                                    V.drain().then_inc(rows_ready, 1)
                                    split_rows(link, gate, was)

        with phase("vec", "norm_ready", "norm_root", "rows_ready", "table_in") as (block, vec, norm_ready, norm_root, rows_ready, table_in):
            @block.scalar
            def _(act):
                root(act, norm_ready, norm_root, 1)

            @block.sync
            def _(sp):
                sp.wait_ge(rows_ready, 1)
                sp.dma_start(table_nodes, state[:, :, :]).then_inc(table_in, 16)
                sp.wait_ge(table_in, 16)

            @block.vector
            def _(dve):
                link = chain(dve, vec)
                link(nc.vector.tensor_tensor(ends[:, :, :], state[:, :, :], rows[:, :, :], ALU.add))
                layer_norm(dve, link, norm_ready, norm_root, 1, state[:, :, :], ends[:, :, :])
                nc.vector.drain().then_inc(rows_ready, 1)
                split_rows(link, state)

        PAIRS = -(-CT // 2)
        STEP = BANK // P
        STEPS = [(i, min(STEP, PAIRS - i)) for i in range(0, PAIRS, STEP)]
        NS = len(STEPS)
        with ExitStack() as own:
            w1 = sb("w1", [P, 2 * HID], F32, own)
            w2 = sb("w2", [P, 2 * HID], F32, own)
            w3 = sb("w3", [P, HID], F32, own)
            w4 = sb("w4", [P, 2 * D], F32, own)
            bias1 = sb("bias1", [P, 1], F32, own)
            bias2 = sb("bias2", [P, 1], F32, own)
            bias3 = sb("bias3", [P, 1], F32, own)
            bias4 = sb("bias4", [P, D], F32, own)
            message = [sb(f"message{i}", [P, 2 * PAIRS, 2 * D], F32, own) for i in range(2)]
            turned_in = [sb(f"turned_in{i}", [P, BANK], F32, own) for i in range(2)]
            act1 = [sb(f"act1_{i}", [P, BANK], F32, own) for i in range(2)]
            act2 = [sb(f"act2_{i}", [P, 2, BANK], F32, own) for i in range(2)]
            act3 = [sb(f"act3_{i}", [P, BANK], F32, own) for i in range(2)]
            at_starts = inside_space[0][:, 0:4 * D * (CT + 1)].bitcast(F32).rearrange("p (c t) -> p c t", c=D)
            index_rows = [sb(f"index_rows3_{i}", [P, BANK], I16, own) for i in range(2)]
            hot = [sb(f"hot3_{b}", [P, BANK], BF16, own) for b in range(HI)]
            moved = [sb(f"moved3_{i}", [SPLIT, BANK], BF16, own) for i in range(2)]
            acc = own.enter_context(nc.psum_tensor("acc3", [P, BANK], F32))
            ps0 = own.enter_context(nc.psum_tensor("ps0", [P, BANK], F32))
            ps1 = own.enter_context(nc.psum_tensor("ps1", [P, BANK], F32))
            ps2 = [own.enter_context(nc.psum_tensor(f"ps2_{i}", [P, BANK], F32)) for i in range(2)]
            ps3 = own.enter_context(nc.psum_tensor("ps3", [P, BANK], F32))
            ps4 = [own.enter_context(nc.psum_tensor(f"ps4_{i}", [P, BANK // D, D], F32)) for i in range(2)]
            with phase(*COMMON, "hot_index_in0", "hot_index_in1", "hot_ready", "acc_done", "acc_moved",
                       "sum_done", "row_ready", "blank", "weights_in", "message_ready", "turns", "turned_moved", "mm1", "mm2", "mm3", "mm4",
                       "relu1", "relu2", "relu3", "masked") as (
                    block, chunk_in0, chunk_in1, used, vec, result_ready, staged_ready, stored0, stored1,
                    last_ready, last_turned, joined_ready, fix_in, fix_ready, ends_in_, rows_ready, table_in, norm_ready, norm_root,
                    hot_index_in0, hot_index_in1, hot_ready, acc_done, acc_moved, sum_done, row_ready,
                    blank, weights_in, message_ready, turns, turned_moved, mm1, mm2, mm3, mm4, relu1, relu2, relu3, masked):
                chunk_in, stored, hot_index_in = (chunk_in0, chunk_in1), (stored0, stored1), (hot_index_in0, hot_index_in1)
                LOADS = 2 * 5 + 2
                AHEAD_OF = 3
                TOTAL = CHUNKS * NS

                def width(n):
                    return STEPS[n % NS][1] * P


                @block.sync
                def _(sp):
                    col = lambda v: v.rearrange("(n o) -> n o", o=1)
                    sp.wait_ge(blank, 1)
                    for a, half in enumerate((slice(0, HID), slice(HID, 2 * HID))):
                        sp.dma_start(w1[half, half], W1).then_inc(weights_in, 16)
                        sp.dma_start(w2[half, :], W2).then_inc(weights_in, 16)
                        sp.dma_start(w4[half, a * D:(a + 1) * D], W4).then_inc(weights_in, 16)
                        sp.dma_start(bias1[half, :], col(b1)).then_inc(weights_in, 16)
                        sp.dma_start(bias3[half, :], col(b3)).then_inc(weights_in, 16)
                    sp.dma_start(w3[:, :], W3).then_inc(weights_in, 16)
                    sp.dma_start(bias2[:, :], col(b2)).then_inc(weights_in, 16)
                    sp.dma_start(bias4[:, :], b4.partition_broadcast(P)).then_inc(table_in, 16)
                    for k in range(CHUNKS + 3):
                        if k < CHUNKS:
                            if k >= 2:
                                sp.wait_ge(hot_ready, (k - 1) * HI)
                            first = k * HOT_TILES + MLP_SHARE[0] - SETS[1]
                            of = hot_index_dram[1, first:first + BANK // P, :].rearrange("i p -> (i p)")
                            sp.dma_start(index_rows[k % 2][:, :], of.partition_broadcast(P)).then_inc(hot_index_in[k % 2], 16)
                        if k >= 3:
                            store_chunk(sp, k - 3, staged_ready, stored)
                    sp.wait_ge(rows_ready, 1)
                    full = (N // P) * P
                    sp.dma_start(out[0:full, :].rearrange("(h p) c -> p h c", p=P), rows[:, 0:N // P, :]).then_inc(table_in, 16)
                    sp.dma_start(out[full:N, :], rows[0:N - full, HI - 1, :]).then_inc(table_in, 16)
                    sp.wait_ge(table_in, 48)

                @block.gpsimd
                def _(pool):
                    gather_chunks(pool, BY_DST, chunk_in, used, MLP_SHARE)
                    gather_ends(pool, BY_DST, scan_dram, stored, 16 * CHUNKS // 2, fix_in, fix_ready, (ends_in_,))

                @block.tensor
                def _(pe):
                    pe.wait_ge(weights_in, 16 * LOADS)

                    def turn(n):
                        k, (at, pairs) = n // NS, STEPS[n % NS]
                        pe.wait_ge(message_ready, k + 1)
                        if n:
                            pe.wait_ge(turned_moved, n)
                        for i in range(pairs):
                            last = nc.tensor.transpose(ps0[:, i * P:(i + 1) * P],
                                                       message[k % 2][:, 2 * (at + i):2 * (at + i) + 2, :].rearrange("p t c -> p (t c)"), identity[:, :])
                        last.then_inc(turns, 1)

                    def gather_blocks(k, blocks):
                        if k and not blocks[0]:
                            pe.wait_ge(row_ready, k)
                        for b in blocks:
                            n = k * HI + b
                            pe.wait_ge(hot_ready, n + 1)
                            last = nc.tensor.matmul(acc[0:SPLIT, :], parts[:, b, :, :].rearrange("p s c -> p (s c)"), hot[b][:, :],
                                                    start=(b == 0), stop=(b == HI - 1))
                        if blocks[-1] == HI - 1:
                            last.then_inc(acc_done, 1)

                    def sum_up(k):
                        pe.wait_ge(acc_moved, k + 1)
                        for t in range(BANK // P):
                            last = nc.tensor.matmul(acc[:, t * D:(t + 1) * D], moved[k % 2][:, t * P:(t + 1) * P], sum_parts[:, :], start=True, stop=True)
                        last.then_inc(sum_done, 1)

                    gather_blocks(0, range(HI))
                    sum_up(0)
                    halves = [slice(a * HID, (a + 1) * HID) for a in range(2)]
                    for i in range(TOTAL + 4):
                        if i < TOTAL:
                            turn(i)
                        ahead, at = i // NS + 1, i % NS
                        if ahead < CHUNKS and at < 2:
                            gather_blocks(ahead, range(at * HI // 2, (at + 1) * HI // 2))
                        if ahead < CHUNKS and at == 2:
                            sum_up(ahead)
                        n = i - 1
                        if 0 <= n < TOTAL:
                            w = width(n)
                            pe.wait_ge(turned_moved, n + 1)
                            if n:
                                pe.wait_ge(relu1, n)
                            nc.tensor.matmul(ps1[:, 0:w], w1[:, :], turned_in[n % 2][:, 0:w], start=True, stop=True).then_inc(mm1, 1)
                        n = i - 2
                        if 0 <= n < TOTAL:
                            w = width(n)
                            pe.wait_ge(relu1, n + 1)
                            for a, half in enumerate(halves):
                                if n:
                                    pe.wait_ge(relu2, 2 * (n - 1) + a + 1)
                                nc.tensor.matmul(ps2[a][:, 0:w], w2[half, :], act1[n % 2][half, 0:w], start=True, stop=True).then_inc(mm2, 1)
                        n = i - 3
                        if 0 <= n < TOTAL:
                            w = width(n)
                            if n:
                                pe.wait_ge(relu3, n)
                            for a, half in enumerate(halves):
                                pe.wait_ge(relu2, 2 * n + a + 1)
                                last = nc.tensor.matmul(ps3[half, 0:w], w3[:, :], act2[n % 2][:, a, 0:w], start=True, stop=True)
                            last.then_inc(mm3, 1)
                        n = i - 4
                        if n >= 0:
                            pe.wait_ge(relu3, n + 1)
                            if n >= 2:
                                pe.wait_ge(masked, n - 1)
                            for j in range(STEPS[n % NS][1]):
                                last = nc.tensor.matmul(ps4[n % 2][:, 2 * j:2 * j + 2, :].rearrange("p t c -> p (t c)"),
                                                        act3[n % 2][:, j * P:(j + 1) * P], w4[:, :], start=True, stop=True)
                            last.then_inc(mm4, 1)
                    turn_last(pe, ps0, last_ready, last_turned, joined_ready)

                @block.scalar
                def _(act):
                    def parts_out(k):
                        act.wait_ge(acc_done, k + 1)
                        if k >= 2:
                            act.wait_ge(sum_done, k - 1)
                        act.activation(moved[k % 2][:, :], acc[0:SPLIT, :], ACT.Copy).then_inc(acc_moved, 1)

                    def rows_out(k):
                        act.wait_ge(sum_done, k + 1)
                        if k >= 2:
                            act.wait_ge(used, k - 1)
                        act.activation(gathered[k % 2][:, MLP_SHARE[0]:MLP_SHARE[1], :].rearrange("p t c -> p (t c)"),
                                       acc[:, 0:BANK // P * D], ACT.Copy).then_inc(row_ready, 1)

                    parts_out(0)
                    rows_out(0)
                    act.wait_ge(weights_in, 16 * LOADS)
                    for i in range(TOTAL + 3):
                        n = i
                        if n < TOTAL:
                            act.wait_ge(turns, n + 1)
                            if n >= 2:
                                act.wait_ge(mm1, n - 1)
                            act.activation(turned_in[n % 2][:, 0:width(n)], ps0[:, 0:width(n)], ACT.Copy).then_inc(turned_moved, 1)
                        n = i - 1
                        if 0 <= n < TOTAL:
                            act.wait_ge(mm1, n + 1)
                            if n >= 2:
                                act.wait_ge(mm2, 2 * (n - 1))
                            act.activation(act1[n % 2][:, 0:width(n)], ps1[:, 0:width(n)], ACT.Relu, bias=bias1[:, :]).then_inc(relu1, 1)
                        n = i - 2
                        if 0 <= n < TOTAL:
                            for a in range(2):
                                act.wait_ge(mm2, 2 * n + a + 1)
                                if n >= 2:
                                    act.wait_ge(mm3, n - 1)
                                act.activation(act2[n % 2][:, a, 0:width(n)], ps2[a][:, 0:width(n)], ACT.Relu, bias=bias2[:, :]).then_inc(relu2, 1)
                        n = i - 3
                        if n >= 0:
                            act.wait_ge(mm3, n + 1)
                            if n >= 2:
                                act.wait_ge(mm4, n - 1)
                            act.activation(act3[n % 2][:, 0:width(n)], ps3[:, 0:width(n)], ACT.Relu, bias=bias3[:, :]).then_inc(relu3, 1)
                        if i // NS + 1 < CHUNKS and i % NS == 1:
                            parts_out(i // NS + 1)
                        if i // NS + 1 < CHUNKS and i % NS == 2:
                            rows_out(i // NS + 1)
                        if i % NS == NS - 1 and i >= NS:
                            stage_result(act, i // NS - 1, result_ready, stored, staged_ready)
                    stage_result(act, CHUNKS - 1, result_ready, stored, staged_ready)
                    root(act, norm_ready, norm_root, 1)

                @block.vector
                def _(dve):
                    link = chain(dve, vec)
                    V = nc.vector
                    V.memset(w1[:, :], 0.0)
                    link(V.memset(w4[:, :], 0.0))
                    V.drain().then_inc(blank, 1)
                    for i in range(2):
                        if CT % 2:
                            V.memset(message[i][:, CT:2 * PAIRS, :], 0.0)

                    def hot_columns(k):
                        dve.wait_ge(hot_index_in[k % 2], 16 * (k // 2 + 1))
                        if k:
                            dve.wait_ge(acc_done, k)
                        for b in range(HI):
                            V.tensor_scalar(hot[b][:, :], index_rows[k % 2][:, :], node_f[:, b:b + 1], None, ALU.is_equal).then_inc(hot_ready, 1)

                    def make_messages(k):
                        wait_rows(dve, k, chunk_in, MLP_SHARE, row_ready)
                        spread_own_rows(link, k, BY_DST, at_starts)
                        if k >= 2:
                            dve.wait_ge(turns, (k - 1) * NS)
                        own_part = own_row[k % 2][:, :, 1:CT + 1].rearrange("p c t -> p t c")
                        V.tensor_copy(message[k % 2][:, 0:CT, 0:D], own_part)
                        link(V.tensor_tensor(message[k % 2][:, 0:CT, D:2 * D], gathered[k % 2][:, :, :], own_part, ALU.subtract))
                        V.drain().then_inc(message_ready, 1)
                        V.drain().then_inc(used, 1)

                    def take_messages(c, s):
                        n, (at, pairs) = c * NS + s, STEPS[s]
                        cols = min(2 * pairs, CT - 2 * at)
                        lo = c * CT + 2 * at
                        dve.wait_ge(mm4, n + 1)
                        link(V.scalar_tensor_tensor(value[:, :, 1 + 2 * at:1 + 2 * at + cols],
                                                    starts[BY_DST][:, lo:lo + cols].unsqueeze(1).broadcast_to([P, D, cols]), 0.0,
                                                    ps4[n % 2][:, 0:cols, :].rearrange("p t c -> p c t"), ALU.is_equal, ALU.mult))
                        V.drain().then_inc(masked, 1)

                    hot_columns(0)
                    for k in range(2):
                        make_messages(k)
                        hot_columns(k + 1)
                    for c in range(CHUNKS):
                        for s in range(NS):
                            take_messages(c, s)
                            if s == AHEAD_OF:
                                if c + 2 < CHUNKS:
                                    make_messages(c + 2)
                                if c + 3 < CHUNKS:
                                    hot_columns(c + 3)
                        scan_value(dve, link, c, BY_DST, ALU.add, staged_ready, result_ready)
                    keep_last(link, last_ready)
                    join_runs(dve, link, BY_DST, ALU.add, ps0, last_turned, joined_ready)
                    fix_ends(dve, link, ALU.add, ps0, last_turned, fix_in, fix_ready)
                    dve.wait_ge(ends_in_, 16 * HI)
                    dve.wait_ge(table_in, 16)
                    link(V.tensor_tensor(spare[:, :, :], degree[:, :].unsqueeze(2).broadcast_to([P, HI, D]),
                                         bias4[:, :].unsqueeze(1).broadcast_to([P, HI, D]), ALU.mult))
                    link(V.tensor_tensor(ends[:, :, :], ends[:, :, :], spare[:, :, :], ALU.add))
                    link(V.tensor_scalar(stat[:, 0, :], degree[:, :], 1.0, None, ALU.max))
                    link(V.reciprocal(stat[:, 1, :], stat[:, 0, :]))
                    link(V.tensor_tensor(ends[:, :, :], ends[:, :, :], stat[:, 1, :].unsqueeze(2).broadcast_to([P, HI, D]), ALU.mult))
                    link(V.tensor_tensor(ends[:, :, :], ends[:, :, :], state[:, :, :], ALU.add))
                    layer_norm(dve, link, norm_ready, norm_root, 1, rows[:, :, :], ends[:, :, :])
                    V.drain().then_inc(rows_ready, 1)


_INS = ["x", "src", "dst", "edge_weight", "L2_gnn_conv_w", "L2_gnn_conv_b", "L2_gnn_wc", "L2_gnn_bg",
        "L3_gnn_W1", "L3_gnn_b1", "L3_gnn_W2", "L3_gnn_b2", "L3_gnn_W3", "L3_gnn_b3", "L3_gnn_W4", "L3_gnn_b4"]


def kernel(**inputs):
    import numpy as _np
    import concourse.bacc as _bacc
    from concourse.bass_utils import run_bass_kernel_spmd as _run

    nc = _bacc.Bacc("TRN2", target_bir_lowering=False, num_devices=1)
    arrays, args = {}, []
    for name in _INS:
        a = _np.ascontiguousarray(inputs[name])
        arrays[f"in_{name}"] = a
        args.append(nc.dram_tensor(f"in_{name}", a.shape, mybir.dt.from_np(a.dtype), kind="ExternalInput").ap())
    args.append(nc.dram_tensor("out_rows", (N, D), F32, kind="ExternalOutput").ap())
    program(nc, *args)
    r = _run(nc, [arrays], core_ids=[0])
    return r.results[0]["out_rows"]
```
